# Optimizing a Trainium2 kernel written in Bass

```python
import numpy as np
import jax
import jax.numpy as jnp

def _softmax(x, axis=-1):
    return jax.nn.softmax(x, axis=axis)

def _gelu(x):
    return jax.nn.gelu(x, approximate=True)

def _silu(x):
    return jax.nn.silu(x)

def _sigmoid(x):
    return jax.nn.sigmoid(x)

def _layernorm(x, axis=-1, eps=1e-05):
    m = jnp.mean(x, axis=axis, keepdims=True)
    v = jnp.var(x, axis=axis, keepdims=True)
    return (x - m) / jnp.sqrt(v + eps)

def _scatter_add(tgt, idx, src, axis=0):
    return tgt.at[idx].add(src)

def _segment_sum(src, seg, n):
    return jax.ops.segment_sum(src, seg, n)
kernel_name = 'mk_gnn_resnorm_d4_gnn_r32_164522'

def setup_inputs(seed: int=0):
    np.random.seed(seed)
    _w = jnp.asarray

    def _rec_inputs():
        import jax
        import jax.numpy as jnp
        _gk = jax.random.key(seed)
        x = -0.000125 + 0.9999 * jax.random.normal(jax.random.fold_in(_gk, 1), (4096, 256), jnp.float32)
        src = jax.random.randint(jax.random.fold_in(_gk, 2), (65536,), 0, 4096, jnp.int32)
        dst = jnp.minimum((4096 * jax.random.uniform(jax.random.fold_in(_gk, 3), (65536,)) ** 2.0).astype(jnp.int32), 131071)
        _o = jnp.argsort(dst, stable=True)
        src = src[_o]
        dst = dst[_o]
        edge_attr_16 = 0.000241658 + 0.999772 * jax.random.normal(jax.random.fold_in(_gk, 12), (65536, 16), jnp.float32)
        edge_weight = jax.random.uniform(jax.random.fold_in(_gk, 14), (65536,), jnp.float32, 0.0, 1)
        return (x, src, dst, edge_attr_16, edge_weight)
    x, src, dst, edge_attr_16, edge_weight = _rec_inputs()

    def _L0_gnn_setup():
        import jax, jax.numpy as jnp
        import numpy as np
        N = 4096
        E = 16384
        G = 128
        D = 256
        L = 5
        FE = 16
        EPS = 1e-05
        key = jax.random.key(seed)
        ks = jax.random.split(key, 24)
        s = 0.05
        x = jax.random.normal(ks[0], (N, D), jnp.float32)
        edge_index = jax.random.randint(ks[1], (2, E), 0, N, jnp.int32)
        edge_attr = jax.random.normal(ks[2], (E, FE), jnp.float32)
        batch = jnp.repeat(jnp.arange(G, dtype=jnp.int32), N // G)
        We = jax.random.normal(ks[3], (L, FE, D), jnp.float32) * s
        be = jnp.zeros((L, D), jnp.float32)
        W1 = jax.random.normal(ks[4], (L, D, 2 * D), jnp.float32) * s
        b1 = jnp.zeros((L, 2 * D), jnp.float32)
        W2 = jax.random.normal(ks[5], (L, 2 * D, D), jnp.float32) * s
        b2 = jnp.zeros((L, D), jnp.float32)
        bn_g = jnp.ones((L, D), jnp.float32)
        bn_b = jnp.zeros((L, D), jnp.float32)
        bn_m = jax.random.normal(ks[6], (L, D), jnp.float32) * 0.1
        bn_v = jax.random.uniform(ks[7], (L, D), jnp.float32, 0.5, 1.5)
        Wv1 = jax.random.normal(ks[8], (L - 1, D, D), jnp.float32) * s
        bv1 = jnp.zeros((L - 1, D), jnp.float32)
        vn_g = jnp.ones((L - 1, D), jnp.float32)
        vn_b = jnp.zeros((L - 1, D), jnp.float32)
        vn_m = jax.random.normal(ks[9], (L - 1, D), jnp.float32) * 0.1
        vn_v = jax.random.uniform(ks[10], (L - 1, D), jnp.float32, 0.5, 1.5)
        Wv2 = jax.random.normal(ks[11], (L - 1, D, D), jnp.float32) * s
        bv2 = jnp.zeros((L - 1, D), jnp.float32)
        vn_emb0 = jnp.zeros((D,), jnp.float32)
        return dict(x=x, edge_index=edge_index, edge_attr=edge_attr, batch=batch, vn_emb0=vn_emb0, We=We, be=be, W1=W1, b1=b1, W2=W2, b2=b2, bn_g=bn_g, bn_b=bn_b, bn_m=bn_m, bn_v=bn_v, Wv1=Wv1, bv1=bv1, vn_g=vn_g, vn_b=vn_b, vn_m=vn_m, vn_v=vn_v, Wv2=Wv2, bv2=bv2)
    _L0_gnn_all = _L0_gnn_setup()
    _L0_gnn_in = {k: v for k, v in _L0_gnn_all.items() if k in ('vn_emb0', 'We', 'be', 'W1', 'b1', 'W2', 'b2', 'bn_g', 'bn_b', 'bn_m', 'bn_v', 'Wv1', 'bv1', 'vn_g', 'vn_b', 'vn_m', 'vn_v', 'Wv2', 'bv2')}
    del _L0_gnn_all

    def _L1_gnn_setup():
        import jax, jax.numpy as jnp
        import numpy as np
        N, E, C = (50000, 25000, 256)
        EPS = 1e-05
        key = jax.random.key(seed)
        ks = jax.random.split(key, 6)
        s = 1.0 / np.sqrt(C)
        return {'x': jax.random.normal(ks[0], (N, C), jnp.float32), 'edge_weight': jax.random.uniform(ks[1], (E,), jnp.float32), 'W_rel': jax.random.normal(ks[2], (C, C), jnp.float32) * s, 'b_rel': jnp.zeros((C,), jnp.float32), 'W_root': jax.random.normal(ks[3], (C, C), jnp.float32) * s, 'gamma': jnp.ones((C,), jnp.float32), 'beta': jnp.zeros((C,), jnp.float32), 'edge_index': jax.random.randint(ks[4], (2, E), 0, N, jnp.int32), 'batch': jnp.zeros((N,), jnp.int32)}
    _L1_gnn_all = _L1_gnn_setup()
    _L1_gnn_in = {k: v for k, v in _L1_gnn_all.items() if k in ('W_rel', 'b_rel', 'W_root', 'gamma', 'beta')}
    del _L1_gnn_all

    def _L2_gnn_setup():
        import jax, jax.numpy as jnp
        import numpy as np
        N = 50000
        E = 25000
        IN = 256
        H = 8
        C = 32
        NEG_SLOPE = 0.2
        key = jax.random.key(seed)
        k0, k1, k2, k3, k4 = jax.random.split(key, 5)
        x = jax.random.normal(k0, (N, IN), jnp.float32)
        edge_index = jax.random.randint(k1, (2, E), 0, N, dtype=jnp.int64)
        W = jax.random.normal(k2, (IN, H * C), jnp.float32) / np.sqrt(IN).astype(np.float32)
        att_src = jax.random.normal(k3, (H, C), jnp.float32) * 0.1
        att_dst = jax.random.normal(k4, (H, C), jnp.float32) * 0.1
        bias = jnp.zeros((H * C,), jnp.float32)
        return {'x': x, 'edge_index': edge_index, 'W': W, 'att_src': att_src, 'att_dst': att_dst, 'bias': bias}
    _L2_gnn_all = _L2_gnn_setup()
    _L2_gnn_in = {k: v for k, v in _L2_gnn_all.items() if k in ('W', 'att_src', 'att_dst', 'bias')}
    del _L2_gnn_all

    def _L3_gnn_setup():
        import jax, jax.numpy as jnp
        import numpy as np
        N_NODES = 50000

        def _gcn_conv(h, src, dst, norm, W, b, n_nodes):
            h = h @ W
            msg = h[src] * norm[:, None]
            out = jax.ops.segment_sum(msg, dst, num_segments=n_nodes)
            return out + b
        key = jax.random.key(seed)
        ks = jax.random.split(key, 9)
        d = 256
        E = 25000
        inp = {'x': jax.random.normal(ks[0], (N_NODES, d), dtype=jnp.float32), 'edge_index': jax.random.randint(ks[1], (2, E), 0, N_NODES, dtype=jnp.int64)}
        scale = 1.0 / np.sqrt(d)
        for i in range(3):
            inp[f'W{i + 1}'] = jax.random.normal(ks[2 + 2 * i], (d, d), dtype=jnp.float32) * scale
            inp[f'b{i + 1}'] = jnp.zeros((d,), dtype=jnp.float32)
        return inp
    _L3_gnn_all = _L3_gnn_setup()
    _L3_gnn_in = {k: v for k, v in _L3_gnn_all.items() if k in ('W1', 'b1', 'W2', 'b2', 'W3', 'b3')}
    del _L3_gnn_all
    return {'x': x, 'src': src, 'dst': dst, 'edge_attr_16': edge_attr_16, 'edge_weight': edge_weight, 'L0_gnn_vn_emb0': _L0_gnn_in['vn_emb0'], 'L0_gnn_We': _L0_gnn_in['We'], 'L0_gnn_be': _L0_gnn_in['be'], 'L0_gnn_W1': _L0_gnn_in['W1'], 'L0_gnn_b1': _L0_gnn_in['b1'], 'L0_gnn_W2': _L0_gnn_in['W2'], 'L0_gnn_b2': _L0_gnn_in['b2'], 'L0_gnn_bn_g': _L0_gnn_in['bn_g'], 'L0_gnn_bn_b': _L0_gnn_in['bn_b'], 'L0_gnn_bn_m': _L0_gnn_in['bn_m'], 'L0_gnn_bn_v': _L0_gnn_in['bn_v'], 'L0_gnn_Wv1': _L0_gnn_in['Wv1'], 'L0_gnn_bv1': _L0_gnn_in['bv1'], 'L0_gnn_vn_g': _L0_gnn_in['vn_g'], 'L0_gnn_vn_b': _L0_gnn_in['vn_b'], 'L0_gnn_vn_m': _L0_gnn_in['vn_m'], 'L0_gnn_vn_v': _L0_gnn_in['vn_v'], 'L0_gnn_Wv2': _L0_gnn_in['Wv2'], 'L0_gnn_bv2': _L0_gnn_in['bv2'], 'L1_gnn_W_rel': _L1_gnn_in['W_rel'], 'L1_gnn_b_rel': _L1_gnn_in['b_rel'], 'L1_gnn_W_root': _L1_gnn_in['W_root'], 'L1_gnn_gamma': _L1_gnn_in['gamma'], 'L1_gnn_beta': _L1_gnn_in['beta'], 'L2_gnn_W': _L2_gnn_in['W'], 'L2_gnn_att_src': _L2_gnn_in['att_src'], 'L2_gnn_att_dst': _L2_gnn_in['att_dst'], 'L2_gnn_bias': _L2_gnn_in['bias'], 'L3_gnn_W1': _L3_gnn_in['W1'], 'L3_gnn_b1': _L3_gnn_in['b1'], 'L3_gnn_W2': _L3_gnn_in['W2'], 'L3_gnn_b2': _L3_gnn_in['b2'], 'L3_gnn_W3': _L3_gnn_in['W3'], 'L3_gnn_b3': _L3_gnn_in['b3']}

def reference(x, src, dst, edge_attr_16, edge_weight, L0_gnn_vn_emb0, L0_gnn_We, L0_gnn_be, L0_gnn_W1, L0_gnn_b1, L0_gnn_W2, L0_gnn_b2, L0_gnn_bn_g, L0_gnn_bn_b, L0_gnn_bn_m, L0_gnn_bn_v, L0_gnn_Wv1, L0_gnn_bv1, L0_gnn_vn_g, L0_gnn_vn_b, L0_gnn_vn_m, L0_gnn_vn_v, L0_gnn_Wv2, L0_gnn_bv2, L1_gnn_W_rel, L1_gnn_b_rel, L1_gnn_W_root, L1_gnn_gamma, L1_gnn_beta, L2_gnn_W, L2_gnn_att_src, L2_gnn_att_dst, L2_gnn_bias, L3_gnn_W1, L3_gnn_b1, L3_gnn_W2, L3_gnn_b2, L3_gnn_W3, L3_gnn_b3):
    import jax
    import jax.numpy as jnp

    def _L0_gnn_ref(x, edge_index, edge_attr, batch, vn_emb0, We, be, W1, b1, W2, b2, bn_g, bn_b, bn_m, bn_v, Wv1, bv1, vn_g, vn_b, vn_m, vn_v, Wv2, bv2):
        import jax, jax.numpy as jnp
        import numpy as np
        N = 4096
        E = 16384
        G = 128
        D = 256
        L = 5
        FE = 16
        EPS = 1e-05
        src, dst = (edge_index[0], edge_index[1])
        vn = jnp.tile(vn_emb0[None, :], (G, 1))
        h = x
        for l in range(L):
            h_in = h + vn[batch]
            emsg = jax.nn.relu(h_in[src] + edge_attr @ We[l] + be[l])
            agg = jax.ops.segment_sum(emsg, dst, num_segments=N)
            t = h_in + agg
            t = jax.nn.relu(t @ W1[l] + b1[l]) @ W2[l] + b2[l]
            t = (t - bn_m[l]) * (bn_g[l] * jax.lax.rsqrt(bn_v[l] + EPS)) + bn_b[l]
            if l < L - 1:
                t = jax.nn.relu(t)
            h = t + h_in
            if l < L - 1:
                vt = jax.ops.segment_sum(h_in, batch, num_segments=G) + vn
                z = vt @ Wv1[l] + bv1[l]
                z = (z - vn_m[l]) * (vn_g[l] * jax.lax.rsqrt(vn_v[l] + EPS)) + vn_b[l]
                z = jax.nn.relu(z) @ Wv2[l] + bv2[l]
                vn = vn + z
        return h

    def _L1_gnn_ref(x, edge_weight, W_rel, b_rel, W_root, gamma, beta, edge_index, batch):
        import jax, jax.numpy as jnp
        import numpy as np
        N, E, C = (50000, 25000, 256)
        EPS = 1e-05
        src, dst = (edge_index[0], edge_index[1])
        msg = x[src] * edge_weight[:, None]
        agg = jax.ops.segment_sum(msg, dst, num_segments=x.shape[0])
        out = agg @ W_rel.T + b_rel + x @ W_root.T
        mean = out.mean(axis=0)
        var = out.var(axis=0)
        out = (out - mean) * jax.lax.rsqrt(var + EPS) * gamma + beta
        out = jax.nn.relu(out)
        out = jax.nn.relu(out + x)
        return out

    def _L2_gnn_ref(x, edge_index, W, att_src, att_dst, bias):
        import jax, jax.numpy as jnp
        import numpy as np
        N = 50000
        E = 25000
        IN = 256
        H = 8
        C = 32
        NEG_SLOPE = 0.2
        n = x.shape[0]
        loops = jnp.arange(n, dtype=edge_index.dtype)
        ei = jnp.concatenate([edge_index, jnp.stack([loops, loops], axis=0)], axis=1)
        src, dst = (ei[0], ei[1])
        h = (x @ W).reshape(n, H, C)
        a_src = jnp.sum(h * att_src, axis=-1)
        a_dst = jnp.sum(h * att_dst, axis=-1)
        alpha = jax.nn.leaky_relu(a_src[src] + a_dst[dst], NEG_SLOPE)
        amax = jax.ops.segment_max(alpha, dst, num_segments=n)
        amax = jnp.where(jnp.isfinite(amax), amax, 0.0)
        ex = jnp.exp(alpha - amax[dst])
        denom = jax.ops.segment_sum(ex, dst, num_segments=n)
        coef = ex / (denom[dst] + 1e-16)
        msg = h[src] * coef[:, :, None]
        out = jax.ops.segment_sum(msg, dst, num_segments=n)
        return out.reshape(n, H * C) + bias

    def _L3_gnn_ref(x, edge_index, W1, b1, W2, b2, W3, b3):
        import jax, jax.numpy as jnp
        import numpy as np
        N_NODES = 50000

        def _gcn_conv(h, src, dst, norm, W, b, n_nodes):
            h = h @ W
            msg = h[src] * norm[:, None]
            out = jax.ops.segment_sum(msg, dst, num_segments=n_nodes)
            return out + b
        n = x.shape[0]
        loop = jnp.arange(n, dtype=edge_index.dtype)
        src = jnp.concatenate([edge_index[0], loop])
        dst = jnp.concatenate([edge_index[1], loop])
        deg = jax.ops.segment_sum(jnp.ones_like(dst, dtype=x.dtype), dst, num_segments=n)
        dinv = jnp.where(deg > 0, jax.lax.rsqrt(deg), 0.0)
        norm = dinv[src] * dinv[dst]
        h = _gcn_conv(x, src, dst, norm, W1, b1, n)
        h = jax.nn.relu(h)
        h = _gcn_conv(h, src, dst, norm, W2, b2, n)
        h = jax.nn.relu(h)
        h = _gcn_conv(h, src, dst, norm, W3, b3, n)
        return h
    edge_index = jnp.stack([src, dst])
    batch0 = jnp.zeros((4096,), jnp.int32)
    x = _layernorm(x + _L0_gnn_ref(x, edge_index, edge_attr_16, batch0, L0_gnn_vn_emb0, L0_gnn_We, L0_gnn_be, L0_gnn_W1, L0_gnn_b1, L0_gnn_W2, L0_gnn_b2, L0_gnn_bn_g, L0_gnn_bn_b, L0_gnn_bn_m, L0_gnn_bn_v, L0_gnn_Wv1, L0_gnn_bv1, L0_gnn_vn_g, L0_gnn_vn_b, L0_gnn_vn_m, L0_gnn_vn_v, L0_gnn_Wv2, L0_gnn_bv2), axis=-1)
    x = _layernorm(x + _L1_gnn_ref(x, edge_weight, L1_gnn_W_rel, L1_gnn_b_rel, L1_gnn_W_root, L1_gnn_gamma, L1_gnn_beta, edge_index, batch0), axis=-1)
    x = _layernorm(x + _L2_gnn_ref(x, edge_index, L2_gnn_W, L2_gnn_att_src, L2_gnn_att_dst, L2_gnn_bias), axis=-1)
    x = _layernorm(x + _L3_gnn_ref(x, edge_index, L3_gnn_W1, L3_gnn_b1, L3_gnn_W2, L3_gnn_b2, L3_gnn_W3, L3_gnn_b3), axis=-1)
    return x

_drawn_inputs = setup_inputs


def setup_inputs(seed=0):
    import zlib

    import numpy as np

    out = dict(_drawn_inputs(seed))
    spreads = {'L0_gnn_vn_emb0': (0.0, 0.1),
     'L0_gnn_be': (0.0, 0.8),
     'L0_gnn_b1': (0.0, 0.8),
     'L0_gnn_b2': (0.0, 0.8),
     'L0_gnn_bn_g': (1.0, 0.2),
     'L0_gnn_bn_b': (0.0, 0.8),
     'L0_gnn_bv1': (0.0, 0.8),
     'L0_gnn_vn_g': (1.0, 0.2),
     'L0_gnn_vn_b': (0.0, 0.8),
     'L0_gnn_bv2': (0.0, 0.8),
     'L1_gnn_b_rel': (0.0, 0.8),
     'L1_gnn_gamma': (1.0, 0.566),
     'L1_gnn_beta': (0.0, 0.1),
     'L2_gnn_bias': (0.0, 0.1),
     'L3_gnn_b1': (0.0, 0.1),
     'L3_gnn_b2': (0.0, 0.1),
     'L3_gnn_b3': (0.0, 0.1)}
    factors = {'edge_attr_16': 8.0,
     'edge_weight': 2.668,
     'L0_gnn_We': 8.0,
     'L0_gnn_bn_m': 8.0,
     'L0_gnn_vn_m': 8.0,
     'L1_gnn_W_root': 5.554,
     'L2_gnn_att_src': 4.32,
     'L2_gnn_att_dst': 8.0}
    for name, (base, spread) in spreads.items():
        noise = np.random.default_rng([zlib.crc32(name.encode()), seed]).standard_normal(out[name].shape)
        drawn = base * np.exp(spread * noise) if base else spread * noise
        out[name] = jnp.asarray(drawn.astype(out[name].dtype))
    for name, factor in factors.items():
        out[name] = (out[name] * factor).astype(out[name].dtype)
    return out
```

```python
import numpy as np
import concourse.bass as bass
from concourse import mybir
from contextlib import ExitStack

F32 = mybir.dt.float32
I32 = mybir.dt.int32
ALU = mybir.AluOpType
ACT = mybir.ActivationFunctionType
AX = mybir.AxisListType

P = 128
N = 4096
D = 256
E = 65536
FE = 16
L = 5
DH = 2 * D
HEADS = 8
C = D // HEADS
NB = N // P
NT = E // P
U = 8
NO = NT // U
NG = NO // 2
RING = 2 * U
GW = D + HEADS
AW = D + HEADS + 1
RW = AW + 3
EPS = 1e-5
BIG = 1e38

PLAIN, MESSAGE, WEIGHTED, ATTEND = range(4)
DVE, PE = mybir.EngineType.DVE, mybir.EngineType.PE


def build(nc, x, src, dst, edge_attr, edge_weight, vn_emb0, We, be, W1, b1, W2, b2, bn_g, bn_b, bn_m, bn_v,
          Wv1, bv1, vn_g, vn_b, vn_m, vn_v, Wv2, bv2, W_rel, b_rel, W_root, gamma, beta,
          gat_W, att_src, att_dst, gat_bias, gW1, gb1, gW2, gb2, gW3, gb3, out):
    ctx = ExitStack()
    with ctx:
        def sb(name, shape, dt=F32):
            return ctx.enter_context(nc.sbuf_tensor(name, shape, dt))

        def pb(name, shape):
            return ctx.enter_context(nc.psum_tensor(name, shape, F32))

        def sem(name):
            return ctx.enter_context(nc.semaphore(name))

        node_table = nc.dram_tensor("node_table", [N, D], F32, kind="Internal").ap()
        att_table = nc.dram_tensor("att_table", [N, GW], F32, kind="Internal").ap()
        score_table = nc.dram_tensor("score_table", [N, HEADS], F32, kind="Internal").ap()
        target_table = nc.dram_tensor("target_table", [N, 2 * HEADS], F32, kind="Internal").ap()
        range_scratch = nc.dram_tensor("range_scratch", [NO, 2], I32, kind="Internal").ap()

        H = sb("H", [P, NB * D])
        AGG = sb("AGG", [P, NB * AW])
        EAT = sb("EAT", [P, NO * P])
        Y = EAT
        iota = sb("iota", [P, N])
        iota_i = sb("iota_i", [P, P], I32)
        ring = sb("ring", [P, RING, RW])
        S = sb("S", [P, U, P])
        src_i = sb("src_i", [P, NT], I32)
        dst_i = sb("dst_i", [P, NT], I32)
        dst_f = sb("dst_f", [P, NT])
        weight = sb("weight", [P, NT])
        idx = sb("idx", [P, RING], I32)
        idx_d = sb("idx_d", [P, RING], I32)
        ident = sb("ident", [P, P])
        ones = sb("ones", [P, P])
        WeBig = sb("WeBig", [P, U * D])
        el = sb("el", [P, 2, P])
        w1_sb = sb("w1_sb", [P, 2, DH])
        w2_sb = sb("w2_sb", [P, 4, D])
        wa_sb = sb("wa_sb", [P, 2, D])
        wb_sb = sb("wb_sb", [P, 2, D])
        b1_col = sb("b1_col", [P, 4])
        rows = sb("rows", [P, 5, D])
        bias_row = sb("bias_row", [P, D])
        scale_row = sb("scale_row", [P, D])
        be_row = sb("be_row", [P, D])
        vn = sb("vn", [P, D])
        vnT = sb("vnT", [P, 2, P])
        tin = sb("tin", [P, 2, D])
        tT = sb("tT", [P, 2, 2 * P])
        tT2 = sb("tT2", [P, 2, 2 * P])
        hT = sb("hT", [P, 2, DH])
        tab = sb("tab", [P, 2, GW])
        small = sb("small", [P, 2 * NO])
        small2 = sb("small2", [P, 2 * NO])
        spans = sb("spans", [NO, 2])
        spans_i = sb("spans_i", [NO, 2], I32)
        span_row = sb("span_row", [1, 2 * NO], I32)
        unsorted_i = sb("unsorted_i", [1, 1], I32)
        stats = sb("stats", [P, NB, 6])
        mv = sb("mv", [P, NB, 2])
        rstd = sb("rstd", [P, NB])
        eps = sb("eps", [P, 1])
        a_src = sb("a_src", [P, NB, HEADS])
        a_dst = sb("a_dst", [P, NB, HEADS])
        a_max = sb("a_max", [P, NB, HEADS])
        ex_self = sb("ex_self", [P, NB, HEADS])
        dinv = sb("dinv", [P, NB])
        gs = sb("gs", [P, RING * HEADS])
        gt = sb("gt", [P, RING, 2 * HEADS])
        d16 = sb("d16", [P, RING * HEADS])
        GTp, DTp = WeBig[:, 0:2 * P], WeBig[:, 2 * P:5 * P]
        run, last, pen = (WeBig[:, n * P:n * P + P] for n in (5, 6, 7))
        picks = sb("picks", [P, RING, HEADS + 1])
        al = sb("al", [P, U, HEADS])
        cand = sb("cand", [P, U, HEADS])
        cmax = sb("cmax", [P, HEADS])

        psE = pb("psE", [P, 4 * 512])
        psA = pb("psA", [P, 512])
        psT = pb("psT", [P, 512])
        psO = pb("psO", [P, 512])
        psV = pb("psV", [P, 512])

        gathered = [sem(f"gathered{q}") for q in range(RING)]
        gathered_d = [sem(f"gathered_d{q}") for q in range(RING)]
        octet_free = sem("octet_free")
        onehot_ready = sem("onehot_ready")
        onehot_used = sem("onehot_used")
        unit_added = sem("unit_added")
        enc_staged = sem("enc_staged")
        encoded = sem("encoded")
        pre_added = sem("pre_added")
        message = sem("message")
        logits = sem("logits")
        exps = sem("exps")
        weighed = sem("weighed")
        d16_ready = sem("d16_ready")
        scoresT = sem("scoresT")
        runs_ready = sem("runs_ready")
        runsT = sem("runsT")
        picks_ready = sem("picks_ready")
        t_in = sem("t_in")
        t_done = sem("t_done")
        t_copied = sem("t_copied")
        hid_done = sem("hid_done")
        hid_relu = sem("hid_relu")
        o_done = sem("o_done")
        o_used = sem("o_used")
        tab_ready = sem("tab_ready")
        stored = [sem("stored0"), sem("stored1")]
        par = sem("par")
        sq = sem("sq")
        sqp = sem("sqp")

        loads_seen = sem("loads_seen")

        nd = nc.vector.alloc_register("units_dve")
        npe = nc.tensor.alloc_register("units_pe")

        def flat(ap):
            return ap.rearrange("p a b -> p (a b)")

        def copied(o, i):
            return nc.vector.tensor_scalar(o, i, 1.0, None, ALU.mult)

        def row_bcast(ap):
            return ap.partition_broadcast(P)

        def span_of(eng, h):
            lo = eng.value_load(span_row[0:1, bass.ds(2 * h, 1)], min_val=0, max_val=NB - 1)
            cnt = eng.value_load(span_row[0:1, bass.ds(2 * h + 1, 1)], min_val=1, max_val=NB)
            return lo, cnt

        def edge_pass(kind, k, l=0, loads=None):
            width = AW if kind == ATTEND else D
            gw = GW if kind == ATTEND else D
            table = att_table if kind == ATTEND else node_table
            with nc.Block() as block:
                @block.sync
                def _(sp):
                    if loads:
                        loads(sp)

                @block.gpsimd
                def _(pool):
                    with pool.Fori(0, NG) as i:
                        for half in range(2):
                            r = slice(U * half, U * half + U)
                            cols = bass.ds(RING * i + U * half, U)
                            pool.wait_ge(octet_free, NO * k + 2 * i + 1 + half)
                            nc.gpsimd.tensor_copy(idx[:, r], src_i[:, cols])
                            if kind == ATTEND:
                                nc.gpsimd.tensor_copy(idx_d[:, r], dst_i[:, cols])
                            pool.drain()
                            for q in range(U * half, U * half + U):
                                nc.gpsimd.indirect_dma_start(
                                    ring[:, q, 0:gw], None, table,
                                    bass.IndirectOffsetOnAxis(ap=idx[:, q:q + 1], axis=0)).then_inc(gathered[q], 16)
                                if kind == ATTEND:
                                    nc.gpsimd.indirect_dma_start(
                                        gt[:, q, :], None, target_table,
                                        bass.IndirectOffsetOnAxis(ap=idx_d[:, q:q + 1], axis=0)
                                    ).then_inc(gathered_d[q], 16)

                @block.tensor
                def _(pe):
                    with pe.Fori(0, NG) as i:
                        for half in range(2):
                            o = NO * l + 2 * i + half
                            if kind == MESSAGE:
                                pe.wait_ge(enc_staged, o + 1)
                                pe.wait_ge(pre_added, U * o + U)
                                for g in range(U // 2):
                                    nc.tensor.matmul(psE[:, 512 * g:512 * g + 512], el[:, half, :],
                                                     WeBig[:, 512 * g:512 * g + 512],
                                                     start=True, stop=True).then_inc(encoded, 1)
                            _, cnt = span_of(pe, 2 * i + half)
                            with pe.Fori(0, cnt) as _j:
                                c = pe.snap(npe)
                                pe.wait_ge(unit_added, c + U)
                                for u in range(U):
                                    q = U * half + u
                                    if kind == MESSAGE:
                                        pe.wait_ge(message, U * o + u + 1)
                                    elif kind == ATTEND:
                                        pe.wait_ge(weighed, U * (2 * i + half) + u + 1)
                                    else:
                                        pe.wait_ge(gathered[q], 16 * (NG * k + i + 1))
                                    pe.wait_ge(onehot_ready, c + u + 1)
                                    mm = nc.tensor.matmul(psA[:, 0:width], S[:, u, :], ring[:, q, 0:width],
                                                          start=(u == 0), stop=(u == U - 1))
                                    mm.then_inc(onehot_used, 1)
                                pe.reg_add(npe, npe, U)
                            pe.drain().then_inc(octet_free, 1)

                @block.scalar
                def _(act):
                    if kind == MESSAGE:
                        with act.Fori(0, NG) as i:
                            for half in range(2):
                                o = NO * l + 2 * i + half
                                act.wait_ge(encoded, U + 4 * (o - 1))
                                nc.scalar.copy(el[:, half, :], EAT[:, bass.ds((2 * i + half) * P, P)]
                                               ).then_inc(enc_staged, 1)
                                for u in range(U):
                                    q = U * half + u
                                    act.wait_ge(pre_added, U * o + U + u + 1)
                                    nc.scalar.activation(ring[:, q, 0:D], ring[:, q, 0:D], ACT.Relu
                                                         ).then_inc(message, 1)
                    if kind == ATTEND:
                        with act.Fori(0, NG) as i:
                            for half in range(2):
                                act.wait_ge(logits, 2 * i + half + 1)
                                nc.scalar.activation(ring[:, U * half:U * half + U, D:GW], al[:, :, :], ACT.Exp
                                                     ).then_inc(exps, 1)

                @block.vector
                def _(dve):
                    nc.vector.memset(AGG[:, :], 0.0)
                    dve.drain()
                    with dve.Fori(0, NG) as i:
                        for half in range(2):
                            h = 2 * i + half
                            o = NO * l + h
                            if kind == MESSAGE:
                                for u in range(U):
                                    q = U * half + u
                                    dve.wait_ge(gathered[q], 16 * (NG * k + i + 1))
                                    dve.wait_ge(encoded, 4 * o + u // 2 + 1 + U)
                                    nc.vector.tensor_tensor(ring[:, q, 0:D], ring[:, q, 0:D],
                                                            psE[:, D * u:D * u + D], ALU.add).then_inc(pre_added, 1)
                            if kind == ATTEND:
                                for u in range(U):
                                    q = U * half + u
                                    dve.wait_ge(gathered[q], 16 * (NG * k + i + 1))
                                    dve.wait_ge(gathered_d[q], 16 * (i + 1))
                                r = slice(U * half, U * half + U)
                                nc.vector.tensor_tensor(al[:, :, :], ring[:, r, D:GW], gt[:, r, 0:HEADS], ALU.add)
                                dve.drain()
                                nc.vector.scalar_tensor_tensor(al[:, :, :], al[:, :, :], 0.2, al[:, :, :],
                                                               ALU.mult, ALU.max)
                                dve.drain()
                                nc.vector.tensor_tensor(al[:, :, :], al[:, :, :], gt[:, r, HEADS:2 * HEADS],
                                                        ALU.subtract).then_inc(logits, 1)
                                dve.wait_ge(exps, h + 1)
                                for u in range(U):
                                    q = U * half + u
                                    hv = ring[:, q, 0:D].rearrange("p (h c) -> p h c", h=HEADS)
                                    nc.vector.tensor_tensor(
                                        hv, hv, ring[:, q, D:GW].unsqueeze(2).to_broadcast([P, HEADS, C]),
                                        ALU.mult).then_inc(weighed, 1)
                            lo, cnt = span_of(dve, h)
                            with dve.Fori(0, cnt) as j:
                                c = dve.snap(nd)
                                blk = nc.s_assert_within(lo + j, 0, NB - 1,
                                                         skip_runtime_bounds_check_because="lo + cnt <= NB")
                                for u in range(U):
                                    dve.wait_ge(onehot_used, c + u + 1)
                                    t = U * h + u
                                    nc.vector.tensor_scalar(
                                        S[:, u, :], iota[:, bass.ds(blk * P, P)], dst_f[:, bass.ds(t, 1)],
                                        weight[:, bass.ds(t, 1)] if kind == WEIGHTED else None,
                                        ALU.is_equal, ALU.mult if kind == WEIGHTED else ALU.bypass
                                    ).then_inc(onehot_ready, 1)
                                dve.wait_ge(onehot_used, c + 2 * U)
                                dve.wait_ge(unit_added, c + U)
                                a = AGG[:, bass.ds(blk * AW, width)]
                                nc.vector.tensor_tensor(a, a, psA[:, 0:width], ALU.add).then_inc(unit_added, U)
                                dve.reg_add(nd, nd, U)

        def max_pass(k):
            with nc.Block() as block:
                @block.gpsimd
                def _(pool):
                    with pool.Fori(0, NG) as i:
                        pool.wait_ge(scoresT, i + 1)
                        nc.gpsimd.tensor_copy(idx[:, :], src_i[:, bass.ds(RING * i, RING)])
                        pool.drain()
                        for q in range(RING):
                            nc.gpsimd.indirect_dma_start(
                                gs[:, HEADS * q:HEADS * q + HEADS], None, score_table,
                                bass.IndirectOffsetOnAxis(ap=idx[:, q:q + 1], axis=0)).then_inc(gathered[q], 16)

                @block.tensor
                def _(pe):
                    with pe.Fori(0, NG) as i:
                        for q in range(RING):
                            pe.wait_ge(gathered[q], 16 * (NG * k + i + 1))
                        pe.wait_ge(d16_ready, i + 1)
                        nc.tensor.transpose(psE[:, 0:P], gs[:, :], ident[:, :])
                        nc.tensor.transpose(psE[:, 512:512 + P], d16[:, :], ident[:, :]).then_inc(scoresT, 1)
                        pe.wait_ge(runs_ready, i + 1)
                        nc.tensor.transpose(psE[:, 1024:1024 + P], run[:, :], ident[:, :])
                        nc.tensor.transpose(psE[:, 1536:1536 + P], last[:, :], ident[:, :]).then_inc(runsT, 1)
                        pe.wait_ge(picks_ready, i + 1)
                        for half in range(2):
                            _, cnt = span_of(pe, 2 * i + half)
                            with pe.Fori(0, cnt) as _j:
                                c = pe.snap(npe)
                                pe.wait_ge(unit_added, c + U)
                                for u in range(U):
                                    pe.wait_ge(onehot_ready, c + u + 1)
                                    nc.tensor.matmul(psA[:, (HEADS + 1) * u:(HEADS + 1) * (u + 1)], S[:, u, :],
                                                     picks[:, U * half + u, :], start=True, stop=True
                                                     ).then_inc(onehot_used, 1)
                                pe.reg_add(npe, npe, U)
                            pe.drain().then_inc(octet_free, 1)

                @block.vector
                def _(dve):
                    nc.vector.memset(DTp[:, 0:P], -1.0)
                    nc.vector.memset(DTp[:, 2 * P:3 * P], -2.0)
                    nc.vector.memset(GTp[:, 0:P], 0.0)
                    nc.vector.tensor_copy(a_max[:, :, :], a_src[:, :, :])
                    dve.drain()
                    uns = dve.value_load(unsorted_i[0:1, 0:1], min_val=0, max_val=1)
                    am = flat(a_max[:, :, :])
                    GT, DT = GTp[:, P:2 * P], DTp[:, P:2 * P]
                    with dve.Fori(0, NG) as i:
                        dve.wait_ge(scoresT, i + 1)
                        copied(d16[:, :].rearrange("p (q h) -> p q h", h=HEADS),
                               dst_f[:, bass.ds(RING * i, RING)].unsqueeze(2).to_broadcast([P, RING, HEADS])
                               ).then_inc(d16_ready, 1)
                        dve.wait_ge(scoresT, i + 2)
                        nc.vector.tensor_copy(GT, psE[:, 0:P])
                        nc.vector.tensor_copy(DT, psE[:, 512:512 + P])
                        dve.drain()
                        with dve.If(uns > 0):
                            nc.vector.tensor_copy(run[:, :], GT)
                            nc.vector.memset(last[:, :], 1.0)
                            dve.drain()
                            with dve.Fori(1, P) as s:
                                nc.vector.tensor_tensor(pen[:, :], DT, DTp[:, bass.ds(P - s, P)], ALU.is_equal)
                                dve.drain()
                                nc.vector.tensor_scalar(pen[:, :], pen[:, :], 1.0, BIG, ALU.subtract, ALU.mult)
                                dve.drain()
                                nc.vector.tensor_tensor(pen[:, :], pen[:, :], GTp[:, bass.ds(P - s, P)], ALU.add)
                                dve.drain()
                                nc.vector.tensor_tensor(run[:, :], run[:, :], pen[:, :], ALU.max)
                                dve.drain()
                                nc.vector.tensor_tensor(pen[:, :], DT, DTp[:, bass.ds(s + P, P)], ALU.not_equal)
                                dve.drain()
                                nc.vector.tensor_tensor(last[:, :], last[:, :], pen[:, :], ALU.mult)
                                dve.drain()
                        with dve.Else():
                            nc.vector.tensor_tensor(pen[:, :], DT, DTp[:, P - 1:2 * P - 1], ALU.not_equal)
                            nc.vector.tensor_tensor(last[:, :], DT, DTp[:, P + 1:2 * P + 1], ALU.not_equal)
                            dve.drain()
                            nc.vector.tensor_scalar(pen[:, :], pen[:, :], -BIG, None, ALU.mult)
                            dve.drain()
                            nc.vector.tensor_tensor_scan(run[:, :], pen[:, :], GT, -BIG, ALU.add, ALU.max)
                            dve.drain()
                        nc.vector.tensor_tensor(run[:, :], run[:, :], last[:, :], ALU.mult).then_inc(runs_ready, 1)
                        dve.wait_ge(runsT, i + 1)
                        nc.vector.tensor_copy(picks[:, :, 0:HEADS],
                                              psE[:, 1024:1024 + P].rearrange("p (q h) -> p q h", h=HEADS))
                        nc.vector.tensor_copy(picks[:, :, HEADS:HEADS + 1],
                                              psE[:, 1536:1536 + P].rearrange("p (q h) -> p q h", h=HEADS)[:, :, 0:1]
                                              ).then_inc(picks_ready, 1)
                        for half in range(2):
                            h = 2 * i + half
                            lo, cnt = span_of(dve, h)
                            with dve.Fori(0, cnt) as j:
                                c = dve.snap(nd)
                                blk = nc.s_assert_within(lo + j, 0, NB - 1,
                                                         skip_runtime_bounds_check_because="lo + cnt <= NB")
                                for u in range(U):
                                    dve.wait_ge(onehot_used, c + u + 1)
                                    nc.vector.tensor_scalar(
                                        S[:, u, :], iota[:, bass.ds(blk * P, P)], dst_f[:, bass.ds(U * h + u, 1)],
                                        None, ALU.is_equal).then_inc(onehot_ready, 1)
                                dve.wait_ge(onehot_used, c + 2 * U)
                                pv = psA[:, 0:(HEADS + 1) * U].rearrange("p (u h) -> p u h", u=U)
                                nc.vector.tensor_scalar(cand[:, :, :], pv[:, :, HEADS:HEADS + 1].to_broadcast(
                                    [P, U, HEADS]), 1.0, BIG, ALU.subtract, ALU.mult)
                                dve.drain()
                                nc.vector.tensor_tensor(cand[:, :, :], cand[:, :, :], pv[:, :, 0:HEADS], ALU.add)
                                dve.drain()
                                nc.vector.tensor_reduce(cmax[:, :], cand[:, :, :].rearrange("p u h -> p h u"),
                                                        AX.X, ALU.max)
                                dve.drain()
                                a = am[:, bass.ds(blk * HEADS, HEADS)]
                                nc.vector.tensor_tensor(a, a, cmax[:, :], ALU.max)
                                dve.drain().then_inc(unit_added, U)
                                dve.reg_add(nd, nd, U)


        def staged(eng, *stages):
            for b in range(2):
                for s, stage in enumerate(stages):
                    if b >= s:
                        stage(b - s, (b - s) % 2, (b - s) // 2)
            with eng.Fori(1, NB // 2) as j:
                for q in range(2):
                    for s, stage in enumerate(stages):
                        stage(2 * j + (q - s), (q - s) % 2, j + (q - s) // 2)
            for b in range(NB, NB + 2):
                for s, stage in enumerate(stages):
                    if b - s < NB:
                        stage(b - s, (b - s) % 2, (b - s) // 2)

        turned = (psT, psV)

        def result_of(q):
            return psE[:, 512 * (2 + q):512 * (2 + q) + D]

        def node_phase(m, pre, post, hidden=False, second=False, bias=False, store=None, st=0, pool_post=None,
                       loads=None):
            def ready(b):
                return NB * m + b + 3

            def free(b):
                return NB * m + b + 1

            def rest(b, q, hb):
                pass

            with nc.Block() as block:
                @block.sync
                def _(sp):
                    if loads:
                        loads(sp)

                    def put(b, q, hb):
                        sp.wait_ge(tab_ready, NB * st + b + 1)
                        store(sp, b, q).then_inc(stored[q], 16)

                    if store:
                        staged(sp, put)
                        for q in range(2):
                            sp.wait_ge(stored[q], 16 * ((NB // 2) * (st + 1) + 1))
                        sp.sem_inc(loads_seen, 1)

                @block.gpsimd
                def _(pool):
                    def add(b, q, hb):
                        pool.wait_ge(o_used, ready(b))
                        pool.wait_ge(stored[q], 16 * ((NB // 2) * st + hb + 1))
                        pool_post(pool, b, q).then_inc(tab_ready, 1)

                    if pool_post:
                        staged(pool, add)

                @block.vector
                def _(dve):
                    def before(b, q, hb):
                        dve.wait_ge(t_done, free(b))
                        pre(dve, b, q).then_inc(t_in, 1)

                    def after(b, q, hb):
                        dve.wait_ge(o_done, ready(b))
                        if store and not pool_post:
                            dve.wait_ge(stored[q], 16 * ((NB // 2) * st + hb + 1))
                        post(dve, b, q).then_inc(o_used, 1)
                        if store and not pool_post:
                            dve.drain().then_inc(tab_ready, 1)

                    if hidden:
                        staged(dve, before, rest, after)
                    else:
                        staged(dve, before, after)

                @block.tensor
                def _(pe):
                    def turn(b, q, hb):
                        pe.wait_ge(t_in, ready(b))
                        pe.wait_ge(t_copied, free(b))
                        for f in range(2):
                            ins = nc.tensor.transpose(turned[q][:, P * f:P * f + P],
                                                      tin[:, q, P * f:P * f + P], ident[:, :])
                        if second:
                            for f in range(2):
                                ins = nc.tensor.transpose(turned[q][:, D + P * f:D + P * f + P],
                                                          tin2[:, q, P * f:P * f + P], ident[:, :])
                        ins.then_inc(t_done, 1)

                    def hid(b, q, hb):
                        pe.wait_ge(t_copied, ready(b))
                        pe.wait_ge(hid_relu, free(b))
                        for j in range(4):
                            for f in range(2):
                                ins = nc.tensor.matmul(psE[:, 512 * q + P * j:512 * q + P * j + P],
                                                       w1_sb[:, f, P * j:P * j + P], tT[:, q, P * f:P * f + P],
                                                       start=(f == 0), stop=(f == 1))
                        ins.then_inc(hid_done, 1)

                    def result(b, q, hb):
                        pe.wait_ge(hid_relu if hidden else t_copied, ready(b))
                        pe.wait_ge(o_used, free(b))
                        terms = ([(hT[:, q, P * j:P * j + P], w2_sb[:, j, :]) for j in range(4)] if hidden else
                                 [(tT[:, q, P * f:P * f + P], wa_sb[:, f, :]) for f in range(2)])
                        if second:
                            terms += [(tT2[:, q, P * f:P * f + P], wb_sb[:, f, :]) for f in range(2)]
                        if bias:
                            terms.append((ones[0:1, :], bias_row[0:1, :]))
                        for n, (a, w) in enumerate(terms):
                            ins = nc.tensor.matmul(result_of(q), a, w,
                                                   start=(n == 0), stop=(n == len(terms) - 1))
                        ins.then_inc(o_done, 1)

                    if hidden:
                        staged(pe, turn, hid, result)
                    else:
                        staged(pe, turn, result)
                        pe.sem_inc(hid_done, NB)

                @block.scalar
                def _(act):
                    def copy(b, q, hb):
                        act.wait_ge(t_done, ready(b))
                        act.wait_ge(hid_done if hidden else o_done, free(b))
                        ins = nc.scalar.copy(tT[:, q, :], turned[q][:, 0:D])
                        if second:
                            ins = nc.scalar.copy(tT2[:, q, :], turned[q][:, D:2 * D])
                        ins.then_inc(t_copied, 1)

                    def relu(b, q, hb):
                        act.wait_ge(hid_done, ready(b))
                        act.wait_ge(o_done, free(b))
                        for j in range(4):
                            ins = nc.scalar.activation(hT[:, q, P * j:P * j + P],
                                                       psE[:, 512 * q + P * j:512 * q + P * j + P],
                                                       ACT.Relu, bias=b1_col[:, j:j + 1])
                        ins.then_inc(hid_relu, 1)

                    if hidden:
                        staged(act, copy, relu)
                    else:
                        staged(act, copy)

        def on_vector(steps):
            with nc.Block() as block:
                @block.vector
                def _(dve):
                    for step in steps:
                        step()
                        dve.drain()

        def on_scalar(steps):
            with nc.Block() as block:
                @block.scalar
                def _(act):
                    for step in steps:
                        step()
                        act.drain()

        def on_tensor(steps):
            with nc.Block() as block:
                @block.tensor
                def _(pe):
                    for step in steps:
                        step()

        def blk(t, b, w=D, pitch=D):
            return t[:, bass.ds(b * pitch, w)] if not isinstance(b, int) else t[:, b * pitch:b * pitch + w]

        def whole(t, w=D, pitch=D):
            return t[:, 0:NB * pitch].rearrange("p (b f) -> p b f", f=pitch)[:, :, 0:w]

        def over(row, nb=NB):
            return row.unsqueeze(1).to_broadcast([P, nb, D])

        def dma_block(*copies):
            with nc.Block() as block:
                @block.sync
                def _(sp):
                    copy_in(sp, block_copied, block_count, *copies)

        block_copied = sem("block_copied")
        block_count = [0]

        def copy_in(sp, s, count, *copies):
            for o, i in copies:
                sp.dma_start(o, i).then_inc(s, 16)
            count[0] += 16 * len(copies)
            sp.wait_ge(s, count[0])

        node_view = node_table.rearrange("(b p) f -> p b f", p=P)

        dma_block((src_i[:, :].rearrange("p (h u) -> p h u", u=U), src.rearrange("(h p u) -> p h u", p=P, u=U)),
                  (dst_i[:, :].rearrange("p (h u) -> p h u", u=U), dst.rearrange("(h p u) -> p h u", p=P, u=U)),
                  (weight[:, :].rearrange("p (h u) -> p h u", u=U),
                   edge_weight.rearrange("(h p u) -> p h u", p=P, u=U)),
                  (whole(H), x.rearrange("(b p) f -> p b f", p=P)),
                  (vn[:, :], row_bcast(vn_emb0)))
        iota_t = AGG[:, 0:N].bitcast(I32)
        with nc.Block() as block:
            @block.gpsimd
            def _(pool):
                nc.gpsimd.iota(iota_t, pattern=[[1, N]], base=0, channel_multiplier=0)
                nc.gpsimd.iota(iota_i[:, :], pattern=[[1, P]], base=0, channel_multiplier=-1)

            @block.tensor
            def _(pe):
                pe.reg_mov(npe, 0)
                pe.sem_inc(octet_free, 2)
                pe.sem_inc(onehot_used, U)
                pe.sem_inc(encoded, U)
                pe.sem_inc(unit_added, U)
                pe.sem_inc(pre_added, U)
                pe.sem_inc(scoresT, 1)
                pe.sem_inc(stored[0], 16)
                pe.sem_inc(stored[1], 16)
                for s in (t_in, t_done, t_copied, hid_done, hid_relu, o_done, o_used):
                    pe.sem_inc(s, 2)

            @block.vector
            def _(dve):
                dve.reg_mov(nd, 0)
                nc.vector.memset(ones[:, :], 1.0)
                nc.vector.memset(eps[:, :], EPS)
                nc.vector.memset(WeBig[:, :], 0.0)
                nc.vector.memset(ring[:, :, AW - 1:AW], 1.0)
                nc.vector.tensor_copy(dst_f[:, :], dst_i[:, :])
        blk_t = AGG[:, N:N + NT].bitcast(I32)
        on_vector([
            lambda: nc.vector.tensor_copy(iota[:, :], iota_t),
            lambda: nc.vector.tensor_scalar(ident[:, :], iota_i[:, :], 0.0, None, ALU.is_equal),
            lambda: nc.vector.tensor_scalar(blk_t, dst_i[:, :], P.bit_length() - 1, None, ALU.arith_shift_right),
            lambda: nc.vector.tensor_reduce(small[:, 0:NO], blk_t.rearrange("p (h u) -> p h u", u=U), AX.X, ALU.min),
            lambda: nc.vector.tensor_reduce(small[:, NO:2 * NO], blk_t.rearrange("p (h u) -> p h u", u=U),
                                            AX.X, ALU.max),
        ])
        on_tensor([lambda: nc.tensor.transpose(psT[0:NO, 0:P], small[:, 0:NO], ident[:, :]),
                   lambda: nc.tensor.transpose(psT[0:NO, P:2 * P], small[:, NO:2 * NO], ident[:, :])] +
                  [(lambda c=c: nc.tensor.transpose(psE[:, P * c:P * c + P], dst_f[:, P * c:P * c + P], ident[:, :]))
                   for c in range(NT // P)])
        on_vector([
            lambda: nc.vector.tensor_reduce(spans[:, 0:1], psT[0:NO, 0:P], AX.X, ALU.min),
            lambda: nc.vector.tensor_reduce(spans[:, 1:2], psT[0:NO, P:2 * P], AX.X, ALU.max),
            lambda: nc.vector.tensor_tensor(spans[:, 1:2], spans[:, 1:2], spans[:, 0:1], ALU.subtract),
            lambda: nc.vector.tensor_scalar_add(spans[:, 1:2], spans[:, 1:2], 1.0),
            lambda: nc.vector.tensor_copy(spans_i[:, :], spans[:, :]),
            lambda: nc.vector.tensor_copy(AGG[:, 0:NT], psE[:, 0:NT]),
            lambda: nc.vector.tensor_tensor(
                AGG[:, NT:2 * NT].rearrange("p (c e) -> p c e", e=P)[:, :, 0:P - 1],
                AGG[:, 0:NT].rearrange("p (c e) -> p c e", e=P)[:, :, 0:P - 1],
                AGG[:, 0:NT].rearrange("p (c e) -> p c e", e=P)[:, :, 1:P], ALU.is_gt),
            lambda: nc.vector.tensor_reduce(
                small[:, 0:NT // P], AGG[:, NT:2 * NT].rearrange("p (c e) -> p c e", e=P)[:, :, 0:P - 1],
                AX.X, ALU.max),
            lambda: nc.vector.tensor_reduce(small2[:, 0:1], small[:, 0:NT // P], AX.X, ALU.max),
        ])
        on_tensor([lambda: nc.tensor.transpose(psT[0:1, 0:P], small2[:, 0:1], ident[:, :])])
        on_vector([
            lambda: nc.vector.tensor_reduce(small2[0:1, 0:1], psT[0:1, 0:P], AX.X, ALU.max),
            lambda: nc.vector.tensor_copy(unsorted_i[:, :], small2[0:1, 0:1]),
        ])
        dma_block((range_scratch, spans_i[:, :]),
                  (AGG[:, 0:NO * P].rearrange("p (h v) -> p h v", v=P),
                   edge_attr.rearrange("(h p u) f -> p h (u f)", p=P, u=U)))
        dma_block((span_row[:, :], range_scratch.rearrange("h c -> (h c)").unsqueeze(0)))

        eat_t, eat_c = sem("eat_t"), sem("eat_c")
        with nc.Block() as block:
            @block.tensor
            def _(pe):
                for g in range(NO // 4):
                    if g >= 4:
                        pe.wait_ge(eat_c, g - 3)
                    for c in range(4):
                        ins = nc.tensor.transpose(psE[:, 512 * (g % 4) + P * c:512 * (g % 4) + P * c + P],
                                                  AGG[:, (4 * g + c) * P:(4 * g + c + 1) * P], ident[:, :])
                    ins.then_inc(eat_t, 1)

            @block.vector
            def _(dve):
                for g in range(NO // 4):
                    dve.wait_ge(eat_t, g + 1)
                    nc.vector.tensor_copy(EAT[:, 512 * g:512 * g + 512], psE[:, 512 * (g % 4):512 * (g % 4) + 512]
                                          ).then_inc(eat_c, 1)

        def load_we(sp, s, value, l):
            for u in range(U):
                sp.dma_start(WeBig[FE * u:FE * u + FE, D * u:D * u + D], at(We, l)).then_inc(s, 16)
            sp.dma_start(be_row[:, :], row_bcast(at(be, l))).then_inc(s, 16)
            sp.wait_ge(s, value)
            sp.sem_inc(loads_seen, 1)

        def at(t, l):
            return t[bass.ds(l, 1)].squeeze(0) if not isinstance(l, int) else t[l]

        we_loaded = sem("we_loaded")
        with nc.Block() as block:
            @block.sync
            def _(sp):
                load_we(sp, we_loaded, 16 * (U + 1), 0)
        on_vector([
            lambda: nc.vector.tensor_tensor(whole(H), whole(H), over(vn[:, :]), ALU.add),
            lambda: nc.vector.tensor_tensor(whole(AGG), whole(H), over(be_row[:, :]), ALU.add),
        ])
        dma_block((node_view, whole(AGG)))

        layer_loaded = sem("layer_loaded")
        v_pe, v_dve, v_act = sem("v_pe"), sem("v_dve"), sem("v_act")
        ROWS = 8

        def layer(l, last_layer):
            def loads(sp):
                n = 0
                for o, i in ([(w1_sb[:, :, :], at(W1, l).rearrange("(f p) n -> p f n", p=P)),
                              (w2_sb[:, :, :], at(W2, l).rearrange("(f p) n -> p f n", p=P)),
                              (rows[:, 0, :], row_bcast(at(bn_v, l))), (rows[:, 1, :], row_bcast(at(bn_g, l))),
                              (rows[:, 2, :], row_bcast(at(bn_m, l))), (rows[:, 3, :], row_bcast(at(bn_b, l))),
                              (rows[:, 4, :], row_bcast(at(b2, l)))] +
                             [(b1_col[:, j:j + 1], at(b1, l)[P * j:P * j + P].unsqueeze(1)) for j in range(4)]):
                    sp.dma_start(o, i).then_inc(layer_loaded, 16)
                    n += 1
                sp.wait_ge(layer_loaded, 16 * n * (l + 1))
                sp.sem_inc(loads_seen, 1)

            edge_pass(MESSAGE, l, l, loads)
            if not last_layer:
                with nc.Block() as block:
                    @block.sync
                    def _(sp):
                        virtual_loads(sp, l)
                    @block.tensor
                    def _(pe):
                        for b in range(NB):
                            ins = nc.tensor.matmul(psV[:, 0:D], ones[:, :], H[:, D * b:D * b + D],
                                                   start=(b == 0), stop=(b == NB - 1))
            on_scalar([lambda: nc.scalar.activation(rows[:, 0, :], rows[:, 0, :], ACT.Sqrt, bias=eps[:, 0:1])] +
                      ([] if last_layer else
                       [lambda: nc.scalar.activation(vrows[:, 0, :], vrows[:, 0, :], ACT.Sqrt, bias=eps[:, 0:1])]))
            on_vector([
                lambda: nc.vector.reciprocal(rows[:, 0, :], rows[:, 0, :]),
                lambda: nc.vector.tensor_tensor(scale_row[:, :], rows[:, 0, :], rows[:, 1, :], ALU.mult),
                lambda: nc.vector.tensor_tensor(bias_row[:, :], rows[:, 4, :], rows[:, 2, :], ALU.subtract),
                lambda: nc.vector.tensor_tensor(bias_row[:, :], bias_row[:, :], scale_row[:, :], ALU.mult),
                lambda: nc.vector.tensor_tensor(bias_row[:, :], bias_row[:, :], rows[:, 3, :], ALU.add),
                lambda: nc.vector.tensor_tensor(w2_sb[:, :, :], w2_sb[:, :, :], over(scale_row[:, :], 4), ALU.mult),
            ])
            if not last_layer:
                on_vector([
                    lambda: nc.vector.reciprocal(vrows[:, 0, :], vrows[:, 0, :]),
                    lambda: nc.vector.tensor_tensor(scale_row[:, :], vrows[:, 0, :], vrows[:, 1, :], ALU.mult),
                    lambda: nc.vector.tensor_tensor(vrows[:, 2, :], vrows[:, 4, :], vrows[:, 2, :], ALU.subtract),
                    lambda: nc.vector.tensor_tensor(vrows[:, 2, :], vrows[:, 2, :], scale_row[:, :], ALU.mult),
                    lambda: nc.vector.tensor_tensor(vrows[:, 2, :], vrows[:, 2, :], vrows[:, 3, :], ALU.add),
                    lambda: nc.vector.tensor_tensor(tin[:, 0, :], psV[:, 0:D], vn[:, :], ALU.add),
                ])
                on_tensor([(lambda f=f: nc.tensor.transpose(psT[:, P * f:P * f + P], tin[:, 0, P * f:P * f + P],
                                                            ident[:, :])) for f in range(2)])
                on_vector([lambda: nc.vector.tensor_copy(tT[:, 0, :], psT[:, 0:D])])
                on_tensor([(lambda f=f: nc.tensor.matmul(psO[:, 0:D], tT[:, 0, P * f:P * f + P], wa_sb[:, f, :],
                                                         start=(f == 0), stop=(f == 1))) for f in range(2)])
                on_vector([
                    lambda: nc.vector.tensor_tensor(tin[:, 0, :], psO[:, 0:D], scale_row[:, :], ALU.mult),
                    lambda: nc.vector.tensor_tensor(tin[:, 0, :], tin[:, 0, :], vrows[:, 2, :], ALU.add),
                    lambda: nc.vector.tensor_scalar(tin[:, 0, :], tin[:, 0, :], 0.0, None, ALU.max),
                ])
                on_tensor([(lambda f=f: nc.tensor.transpose(psT[:, P * f:P * f + P], tin[:, 0, P * f:P * f + P],
                                                            ident[:, :])) for f in range(2)])
                on_vector([lambda: nc.vector.tensor_copy(tT[:, 0, :], psT[:, 0:D])])
                on_tensor([(lambda f=f: nc.tensor.matmul(psO[:, 0:D], tT[:, 0, P * f:P * f + P], wb_sb[:, f, :],
                                                         start=(f == 0), stop=(f == 1))) for f in range(2)])
                on_vector([
                    lambda: nc.vector.tensor_tensor(vn[:, :], psO[:, 0:D], vn[:, :], ALU.add),
                    lambda: nc.vector.tensor_tensor(vn[:, :], vn[:, :], vrows[:, 5, :], ALU.add),
                ])

            def pre(dve, b, q):
                return nc.vector.tensor_tensor(tin[:, q, :], blk(H, b), blk(AGG, b, D, agg_pitch), ALU.add)

            def post(dve, b, q):
                h = blk(H, b)
                if last_layer:
                    return nc.vector.tensor_tensor(blk(AGG, b, D, agg_pitch), result_of(q), h, ALU.add)
                nc.vector.scalar_tensor_tensor(h, result_of(q), 0.0, h, ALU.max, ALU.add)
                dve.drain()
                return nc.vector.tensor_tensor(h, h, vn[:, :], ALU.add)

            def table_rows(pool, b, q):
                return nc.gpsimd.tensor_tensor(tab[:, q, 0:D], blk(H, b), be_row[:, :], ALU.add)

            def store(sp, b, q):
                return sp.dma_start(node_rows(b), tab[:, q, 0:D])

            if last_layer:
                node_phase(l, pre, post, hidden=True, bias=True)
            else:
                with nc.Block() as block:
                    @block.sync
                    def _(sp):
                        load_we(sp, we_loaded, 16 * (U + 1) * (l + 2), l + 1)
                node_phase(l, pre, post, hidden=True, bias=True, store=store, st=l, pool_post=table_rows)

        agg_pitch = AW

        def node_rows(b):
            return node_table[bass.ds(b * P, P), :] if not isinstance(b, int) else node_table[b * P:b * P + P, :]

        vrows = sb("vrows", [P, 6, D])
        tin2 = sb("tin2", [P, 2, D])
        virtual_loaded = sem("virtual_loaded")

        def virtual_loads(sp, l):
            n = 0
            for o, i in [(wa_sb[:, :, :], at(Wv1, l).rearrange("(f p) n -> p f n", p=P)),
                         (wb_sb[:, :, :], at(Wv2, l).rearrange("(f p) n -> p f n", p=P)),
                         (vrows[:, 0, :], row_bcast(at(vn_v, l))), (vrows[:, 1, :], row_bcast(at(vn_g, l))),
                         (vrows[:, 2, :], row_bcast(at(vn_m, l))), (vrows[:, 3, :], row_bcast(at(vn_b, l))),
                         (vrows[:, 4, :], row_bcast(at(bv1, l))), (vrows[:, 5, :], row_bcast(at(bv2, l)))]:
                sp.dma_start(o, i).then_inc(virtual_loaded, 16)
                n += 1
            sp.wait_ge(virtual_loaded, 16 * n * (l + 1))
            sp.sem_inc(loads_seen, 1)

        with nc.Fori(0, L - 1) as l:
            layer(l, False)
        layer(L - 1, True)

        def layer_norm():
            with nc.Block() as block:
                @block.vector
                def _(dve):
                    with dve.Fori(0, NB // 2) as j:
                        for q in range(2):
                            b = 2 * j + q
                            nc.vector.bn_stats(flat(stats[:, :, :])[:, bass.ds(b * 6, 6)],
                                               AGG[:, bass.ds(b * AW, D)])
                    dve.drain()
                    for b in range(NB):
                        nc.vector.bn_aggr(mv[:, b, :], stats[:, b, :])
            on_scalar([lambda: nc.scalar.activation(rstd[:, :], mv[:, :, 1:2].rearrange("p b o -> p (b o)"),
                                                    ACT.Sqrt, bias=eps[:, 0:1])])
            with nc.Block() as block:
                @block.vector
                def _(dve):
                    nc.vector.reciprocal(rstd[:, :], rstd[:, :])
                    dve.drain()
                    with dve.Fori(0, NB // 2) as j:
                        for q in range(2):
                            b = 2 * j + q
                            nc.vector.tensor_scalar(H[:, bass.ds(b * D, D)], AGG[:, bass.ds(b * AW, D)],
                                                    flat(mv[:, :, :])[:, bass.ds(b * 2, 1)],
                                                    rstd[:, bass.ds(b, 1)], ALU.subtract, ALU.mult)

        agg = whole(AGG, D, AW)
        dma_block((whole(H), x.rearrange("(b p) f -> p b f", p=P)))
        on_vector([lambda: nc.vector.tensor_tensor(agg, agg, whole(H), ALU.add)])
        layer_norm()
        dma_block((node_view, whole(H)))

        def col_w(w):
            return w.rearrange("(f p) n -> p f n", p=P)

        def second_loads(sp):
            copy_in(sp, block_copied, block_count, (w1_sb[:, :, 0:D], col_w(W_rel)), (w1_sb[:, :, D:2 * D], col_w(W_root)),
                    (bias_row[:, :], row_bcast(b_rel)), (rows[:, 0, :], row_bcast(gamma)),
                    (rows[:, 1, :], row_bcast(beta)))

        edge_pass(WEIGHTED, L, 0, second_loads)
        on_tensor([(lambda s=s, f=f, g=g: nc.tensor.transpose(
            psE[:, 1024 * s + 512 * f + P * g:1024 * s + 512 * f + P * g + P],
            w1_sb[:, g, D * s + P * f:D * s + P * f + P], ident[:, :]))
            for s in range(2) for f in range(2) for g in range(2)])
        on_vector([(lambda s=s, f=f: nc.vector.tensor_copy((wa_sb, wb_sb)[s][:, f, :],
                                                           psE[:, 1024 * s + 512 * f:1024 * s + 512 * f + D]))
                   for s in range(2) for f in range(2)])

        def pre_second(dve, b, q):
            copied(tin2[:, q, :], blk(H, b))
            dve.drain()
            return copied(tin[:, q, :], blk(AGG, b, D, AW))

        def to_agg(dve, b, q):
            return copied(blk(AGG, b, D, AW), result_of(q))

        node_phase(L, pre_second, to_agg, second=True, bias=True)
        on_tensor([(lambda b=b: nc.tensor.matmul(psV[:, 0:D], ones[:, :], AGG[:, AW * b:AW * b + D],
                                                 start=(b == 0), stop=(b == NB - 1))) for b in range(NB)])
        sqr = whole(Y)
        on_vector([
            lambda: nc.vector.tensor_scalar(scale_row[:, :], psV[:, 0:D], 1.0 / N, None, ALU.mult),
            lambda: nc.vector.tensor_tensor(agg, agg, over(scale_row[:, :]), ALU.subtract),
            lambda: nc.vector.tensor_tensor(sqr, agg, agg, ALU.mult),
        ])
        on_tensor([(lambda b=b: nc.tensor.matmul(psV[:, 0:D], ones[:, :], Y[:, D * b:D * b + D],
                                                 start=(b == 0), stop=(b == NB - 1))) for b in range(NB)])
        on_scalar([lambda: nc.scalar.activation(scale_row[:, :], psV[:, 0:D], ACT.Sqrt, bias=eps[:, 0:1],
                                                scale=1.0 / N)])
        on_vector([
            lambda: nc.vector.reciprocal(scale_row[:, :], scale_row[:, :]),
            lambda: nc.vector.tensor_tensor(scale_row[:, :], scale_row[:, :], rows[:, 0, :], ALU.mult),
            lambda: nc.vector.tensor_tensor(agg, agg, over(scale_row[:, :]), ALU.mult),
            lambda: nc.vector.tensor_tensor(agg, agg, over(rows[:, 1, :]), ALU.add),
            lambda: nc.vector.scalar_tensor_tensor(agg, agg, 0.0, whole(H), ALU.max, ALU.add),
            lambda: nc.vector.scalar_tensor_tensor(agg, agg, 0.0, whole(H), ALU.max, ALU.add),
        ])
        layer_norm()

        dma_block((wa_sb[:, :, :], col_w(gat_W)), (rows[:, 0, :], row_bcast(att_src.rearrange("h c -> (h c)"))),
                  (rows[:, 1, :], row_bcast(att_dst.rearrange("h c -> (h c)"))), (rows[:, 2, :], row_bcast(gat_bias)))

        def pre_h(dve, b, q):
            return copied(tin[:, q, :], blk(H, b))

        def post_att(dve, b, q):
            y = blk(Y, b)
            copied(y, result_of(q))
            for r, scores in ((0, a_src), (1, a_dst)):
                s = flat(scores[:, :, :])
                dve.drain()
                nc.vector.tensor_tensor(tin2[:, r, :], y, rows[:, r, :], ALU.mult)
                dve.drain()
                nc.vector.tensor_reduce(s[:, bass.ds(b * HEADS, HEADS)] if not isinstance(b, int) else
                                        s[:, b * HEADS:b * HEADS + HEADS],
                                        tin2[:, r, :].rearrange("p (h c) -> p h c", h=HEADS), AX.X, ALU.add)
            dve.drain()
            copied(tab[:, q, D:GW], blk(flat(a_src[:, :, :]), b, HEADS, HEADS))
            return copied(tab[:, q, 0:D], y)

        def store_att(sp, b, q):
            t = att_table[bass.ds(b * P, P), :] if not isinstance(b, int) else att_table[b * P:b * P + P, :]
            return sp.dma_start(t, tab[:, q, :])

        node_phase(L + 1, pre_h, post_att, store=store_att, st=L - 1)
        dma_block((score_table.rearrange("(b p) h -> p b h", p=P), a_src[:, :, :]))
        max_pass(L + 1)
        lk = small[:, 0:P]
        aS, aD, aM, eS = (flat(t[:, :, :]) for t in (a_src, a_dst, a_max, ex_self))
        both = WeBig[:, 8 * P:8 * P + NB * 2 * HEADS].rearrange("p (b h) -> p b h", b=NB)
        on_vector([
            lambda: nc.vector.tensor_tensor(aM, aM, aD, ALU.add),
            lambda: nc.vector.scalar_tensor_tensor(aM, aM, 0.2, aM, ALU.mult, ALU.max),
            lambda: nc.vector.tensor_copy(both[:, :, 0:HEADS], a_dst[:, :, :]),
            lambda: nc.vector.tensor_copy(both[:, :, HEADS:2 * HEADS], a_max[:, :, :]),
            lambda: nc.vector.tensor_tensor(eS, aS, aD, ALU.add),
            lambda: nc.vector.scalar_tensor_tensor(eS, eS, 0.2, eS, ALU.mult, ALU.max),
            lambda: nc.vector.tensor_tensor(eS, eS, aM, ALU.subtract),
        ])
        on_scalar([lambda: nc.scalar.activation(eS, eS, ACT.Exp)])
        dma_block((target_table.rearrange("(b p) h -> p b h", p=P), both[:, :, :]))
        edge_pass(ATTEND, L + 2)
        den = AGG[:, 0:NB * AW].rearrange("p (b f) -> p b f", f=AW)[:, :, D:GW]
        count = AGG[:, 0:NB * AW].rearrange("p (b f) -> p b f", f=AW)[:, :, AW - 1:AW]
        y4 = Y[:, :].rearrange("p (k c) -> p k c", c=C)
        on_vector([
            lambda: nc.vector.tensor_tensor(y4, y4, eS.unsqueeze(2).to_broadcast([P, NB * HEADS, C]), ALU.mult),
            lambda: nc.vector.tensor_tensor(agg, agg, whole(Y), ALU.add),
            lambda: nc.vector.tensor_tensor(ex_self[:, :, :], ex_self[:, :, :], den, ALU.add),
            lambda: nc.vector.tensor_scalar_add(eS, eS, 1e-16),
            lambda: nc.vector.reciprocal(eS, eS),
            lambda: nc.vector.tensor_copy(whole(Y), agg),
            lambda: nc.vector.tensor_tensor(y4, y4, eS.unsqueeze(2).to_broadcast([P, NB * HEADS, C]), ALU.mult),
            lambda: nc.vector.tensor_tensor(agg, whole(Y), over(rows[:, 2, :]), ALU.add),
            lambda: nc.vector.tensor_tensor(agg, agg, whole(H), ALU.add),
            lambda: nc.vector.tensor_scalar_add(dinv[:, :], count.rearrange("p b o -> p (b o)"), 1.0),
        ])
        on_scalar([lambda: nc.scalar.activation(dinv[:, :], dinv[:, :], ACT.Sqrt)])
        on_vector([lambda: nc.vector.reciprocal(dinv[:, :], dinv[:, :])])
        layer_norm()

        def dv(b):
            return dinv[:, bass.ds(b, 1)] if not isinstance(b, int) else dinv[:, b:b + 1]

        def pre_conv(dve, b, q):
            nc.vector.tensor_tensor(tin2[:, q, :], blk(AGG, b, D, AW), blk(Y, b), ALU.add)
            dve.drain()
            nc.vector.scalar_tensor_tensor(tin2[:, q, :], tin2[:, q, :], dv(b), rows[:, 0, :], ALU.mult, ALU.add)
            dve.drain()
            return nc.vector.tensor_scalar(tin[:, q, :], tin2[:, q, :], 0.0, None, ALU.max)

        def post_conv(dve, b, q):
            nc.vector.tensor_scalar(tab[:, q, 0:D], result_of(q), dv(b), None, ALU.mult)
            return nc.vector.tensor_scalar(blk(Y, b), result_of(q), dv(b), None, ALU.mult)

        def store_conv(sp, b, q):
            return sp.dma_start(node_rows(b), tab[:, q, 0:D])

        for n, (w, bb) in enumerate(((gW1, gb1), (gW2, gb2), (gW3, gb3))):
            dma_block((wa_sb[:, :, :], col_w(w)))
            node_phase(L + 2 + n, pre_conv if n else pre_h, post_conv, store=store_conv, st=L + n)
            dma_block((rows[:, 0, :], row_bcast(bb)))
            edge_pass(PLAIN, L + 3 + n)
        on_vector([
            lambda: nc.vector.tensor_tensor(agg, agg, whole(Y), ALU.add),
            lambda: nc.vector.tensor_tensor(agg, agg, dinv[:, :].unsqueeze(2).to_broadcast([P, NB, D]), ALU.mult),
            lambda: nc.vector.tensor_tensor(agg, agg, over(rows[:, 0, :]), ALU.add),
            lambda: nc.vector.tensor_tensor(agg, agg, whole(H), ALU.add),
        ])
        layer_norm()
        dma_block((out.rearrange("(b p) f -> p b f", p=P), whole(H)))


_INS = ["x", "src", "dst", "edge_attr_16", "edge_weight", "L0_gnn_vn_emb0", "L0_gnn_We", "L0_gnn_be", "L0_gnn_W1",
        "L0_gnn_b1", "L0_gnn_W2", "L0_gnn_b2", "L0_gnn_bn_g", "L0_gnn_bn_b", "L0_gnn_bn_m", "L0_gnn_bn_v",
        "L0_gnn_Wv1", "L0_gnn_bv1", "L0_gnn_vn_g", "L0_gnn_vn_b", "L0_gnn_vn_m", "L0_gnn_vn_v", "L0_gnn_Wv2",
        "L0_gnn_bv2", "L1_gnn_W_rel", "L1_gnn_b_rel", "L1_gnn_W_root", "L1_gnn_gamma", "L1_gnn_beta", "L2_gnn_W",
        "L2_gnn_att_src", "L2_gnn_att_dst", "L2_gnn_bias", "L3_gnn_W1", "L3_gnn_b1", "L3_gnn_W2", "L3_gnn_b2",
        "L3_gnn_W3", "L3_gnn_b3"]


def kernel(**inputs):
    import concourse.bacc as bacc
    from concourse.bass_utils import run_bass_kernel_spmd

    nc = bacc.Bacc("TRN2", target_bir_lowering=False, num_devices=1)
    arrays, args = {}, []
    for name in _INS:
        a = np.ascontiguousarray(inputs[name])
        arrays[f"in_{name}"] = a
        args.append(nc.dram_tensor(f"in_{name}", a.shape, mybir.dt.from_np(a.dtype), kind="ExternalInput").ap())
    args.append(nc.dram_tensor("out_dram", [N, D], F32, kind="ExternalOutput").ap())
    build(nc, *args)
    r = run_bass_kernel_spmd(nc, [arrays], core_ids=[0])
    return r.results[0]["out_dram"]
```

```python
import numpy as np
import concourse.bass as bass
from concourse import mybir
from contextlib import ExitStack

F32 = mybir.dt.float32
I32 = mybir.dt.int32
ALU = mybir.AluOpType
ACT = mybir.ActivationFunctionType
AX = mybir.AxisListType

P = 128
N = 4096
D = 256
E = 65536
FE = 16
L = 5
DH = 2 * D
HEADS = 8
C = D // HEADS
NB = N // P
NT = E // P
U = 8
NO = NT // U
OB = 4
NG = NO // OB
RING = OB * U
MT = P // 8
GR = RING // MT
PARTS = P // FE
GW = D + HEADS
AW = D + HEADS + 1
RW = AW + 3
EPS = 1e-5
BIG = 1e38

BF16 = mybir.dt.bfloat16
PLAIN, MESSAGE, WEIGHTED, ATTEND = range(4)
DVE, PE = mybir.EngineType.DVE, mybir.EngineType.PE


def build(nc, x, src, dst, edge_attr, edge_weight, vn_emb0, We, be, W1, b1, W2, b2, bn_g, bn_b, bn_m, bn_v,
          Wv1, bv1, vn_g, vn_b, vn_m, vn_v, Wv2, bv2, W_rel, b_rel, W_root, gamma, beta,
          gat_W, att_src, att_dst, gat_bias, gW1, gb1, gW2, gb2, gW3, gb3, out):
    ctx = ExitStack()
    with ctx:
        def sb(name, shape, dt=F32):
            return ctx.enter_context(nc.sbuf_tensor(name, shape, dt))

        def pb(name, shape):
            return ctx.enter_context(nc.psum_tensor(name, shape, F32))

        def sem(name):
            return ctx.enter_context(nc.semaphore(name))

        node_table = nc.dram_tensor("node_table", [N, D], F32, kind="Internal").ap()
        att_table = nc.dram_tensor("att_table", [N, GW], F32, kind="Internal").ap()
        score_table = nc.dram_tensor("score_table", [N, HEADS], F32, kind="Internal").ap()
        target_table = nc.dram_tensor("target_table", [N, 2 * HEADS], F32, kind="Internal").ap()
        stack_table = nc.dram_tensor("stack_table", [NO * P, U * P], BF16, kind="Internal").ap()
        range_scratch = nc.dram_tensor("range_scratch", [NO, 2], I32, kind="Internal").ap()

        H = sb("H", [P, NB * D])
        AGG = sb("AGG", [P, NB * AW])
        Y = sb("Y", [P, NB * D])
        iota = sb("iota", [P, P])
        block_start = sb("block_start", [P, NB])
        iota_i = sb("iota_i", [P, P], I32)
        ring = sb("ring", [P, RING, RW])
        S = sb("S", [P, U, P])
        src_i = sb("src_i", [P, NT], I32)
        dst_i = sb("dst_i", [P, NT], I32)
        dst_f = sb("dst_f", [P, NT])
        weight = sb("weight", [P, NT])
        idx = sb("idx", [P, RING], I32)
        idx_d = sb("idx_d", [P, RING], I32)
        ident = sb("ident", [P, P])
        ones = sb("ones", [P, P])
        stk = sb("stk", [P, OB, U * P], BF16)
        we_rep = sb("we_rep", [P, D])
        we_stk = sb("we_stk", [P, D], BF16)
        wpart = sb("wpart", [P, 3])
        w1_sb = sb("w1_sb", [P, 2, DH])
        w2_sb = sb("w2_sb", [P, 4, D])
        wa_sb = sb("wa_sb", [P, 2, D])
        wb_sb = sb("wb_sb", [P, 2, D])
        b1_col = sb("b1_col", [P, 4])
        rows = sb("rows", [P, 5, D])
        bias_row = sb("bias_row", [P, D])
        scale_row = sb("scale_row", [P, D])
        be_row = sb("be_row", [P, D])
        vn = sb("vn", [P, D])
        vnT = sb("vnT", [P, 2, P])
        tin = sb("tin", [P, 2, D])
        tT = sb("tT", [P, 2, 2 * P])
        tT2 = sb("tT2", [P, 2, 2 * P])
        hT = sb("hT", [P, 2, DH])
        tab = sb("tab", [P, 2, GW])
        small = sb("small", [P, 2 * NO])
        small2 = sb("small2", [P, 2 * NO])
        spans = sb("spans", [NO, 2])
        spans_i = sb("spans_i", [NO, 2], I32)
        span_row = sb("span_row", [1, 2 * NO], I32)
        unsorted_i = sb("unsorted_i", [1, 1], I32)
        stats = sb("stats", [P, NB, 6])
        mv = sb("mv", [P, NB, 2])
        rstd = sb("rstd", [P, NB])
        eps = sb("eps", [P, 1])
        a_src = sb("a_src", [P, NB, HEADS])
        a_dst = sb("a_dst", [P, NB, HEADS])
        a_max = sb("a_max", [P, NB, HEADS])
        ex_self = sb("ex_self", [P, NB, HEADS])
        dinv = sb("dinv", [P, NB])
        gs = sb("gs", [P, RING * HEADS])
        gt = sb("gt", [P, RING, 2 * HEADS])
        d16 = sb("d16", [P, P])
        stk_f = stk[:, :, :].rearrange("p o n -> p (o n)").bitcast(F32)
        GTp, DTp = stk_f[:, 0:2 * P], stk_f[:, 2 * P:5 * P]
        run, last, pen = (stk_f[:, n * P:n * P + P] for n in (5, 6, 7))
        picks = sb("picks", [P, MT, HEADS + 1])
        al = sb("al", [P, U, HEADS])
        cand = sb("cand", [P, U, HEADS])
        cmax = sb("cmax", [P, HEADS])

        psE = pb("psE", [P, 4 * 512])
        psA = pb("psA", [P, 512])
        psT = pb("psT", [P, 512])
        psO = pb("psO", [P, 512])
        psV = pb("psV", [P, 512])

        gathered = [sem(f"gathered{q}") for q in range(RING)]
        gathered_d = [sem(f"gathered_d{q}") for q in range(RING)]
        idx_ready = sem("idx_ready")
        idx_seen = sem("idx_seen")
        octet_free = sem("octet_free")
        onehot_ready = sem("onehot_ready")
        onehot_used = sem("onehot_used")
        unit_added = sem("unit_added")
        stk_in = [sem(f"stk_in{n}") for n in range(OB)]
        encoded = sem("encoded")
        pre_added = sem("pre_added")
        message = sem("message")
        logits = sem("logits")
        exps = sem("exps")
        weighed = sem("weighed")
        d16_ready = sem("d16_ready")
        scoresT = sem("scoresT")
        runs_ready = sem("runs_ready")
        runsT = sem("runsT")
        picks_ready = sem("picks_ready")
        t_in = sem("t_in")
        t_done = sem("t_done")
        t_copied = sem("t_copied")
        hid_done = sem("hid_done")
        hid_relu = sem("hid_relu")
        o_done = sem("o_done")
        o_used = sem("o_used")
        tab_ready = sem("tab_ready")
        stored = [sem("stored0"), sem("stored1")]
        par = sem("par")
        sq = sem("sq")
        sqp = sem("sqp")

        loads_seen = sem("loads_seen")

        parts_seen = sem("parts_seen")

        nd = nc.vector.alloc_register("units_dve")
        npe = nc.tensor.alloc_register("units_pe")
        last_blk = nc.vector.alloc_register("last_block")

        def flat(ap):
            return ap.rearrange("p a b -> p (a b)")

        def copied(o, i):
            return nc.vector.tensor_scalar(o, i, 1.0, None, ALU.mult)

        def row_bcast(ap):
            return ap.partition_broadcast(P)

        def span_of(eng, h):
            lo = eng.value_load(span_row[0:1, bass.ds(2 * h, 1)], min_val=0, max_val=NB - 1)
            cnt = eng.value_load(span_row[0:1, bass.ds(2 * h + 1, 1)], min_val=1, max_val=NB)
            return lo, cnt

        def units(eng, lo, cnt, unit):
            unit(lo, True)
            with eng.If(cnt > 1):
                with eng.Fori(1, cnt) as j:
                    unit(nc.s_assert_within(lo + j, 0, NB - 1,
                                            skip_runtime_bounds_check_because="lo + cnt <= NB") if lo is not None
                         else None, False)

        def one_hots(dve, h, blk, c, g):
            dve.wait_ge(onehot_used, c + 4 * g + 4)
            nc.vector.scalar_tensor_tensor(
                S[:, 4 * g:4 * g + 4, :], iota[:, :].unsqueeze(1).to_broadcast([P, 4, P]),
                block_start[:, bass.ds(blk, 1)],
                dst_f[:, bass.ds(U * h + 4 * g, 4)].unsqueeze(2).to_broadcast([P, 4, P]), ALU.add, ALU.is_equal
            ).then_inc(onehot_ready, 4)

        def past_max(k):
            return isinstance(k, int) and k > L + 1

        def idx_barrier(pool, n):
            pool.wait_ge(idx_ready, n + 1)
            pool.sem_inc(idx_seen, 1)

        def edge_pass(kind, k, l=0, loads=None, first_work=None):
            width = AW if kind == ATTEND else D
            gw = GW if kind == ATTEND else D
            table = att_table if kind == ATTEND else node_table
            with nc.Block() as block:
                @block.sync
                def _(sp):
                    seen = loads(sp) if loads else None
                    if kind == MESSAGE:
                        with sp.Fori(0, NG) as i:
                            for ob in range(OB):
                                o = NO * l + OB * i + ob
                                sp.wait_ge(encoded, U * (o + 1))
                                sp.dma_start(stk[:, ob, :], stack_table[bass.ds((OB * i + ob) * P, P), :]
                                             ).then_inc(stk_in[ob], 16)
                    if seen:
                        seen(sp)

                @block.gpsimd
                def _(pool):
                    with pool.Fori(0, NG) as i:
                        for ob in range(OB):
                            r = slice(U * ob, U * ob + U)
                            cols = bass.ds(RING * i + U * ob, U)
                            pool.wait_ge(octet_free, NO * k + OB * i + 1 + ob)
                            ins = nc.gpsimd.tensor_copy(idx[:, r], src_i[:, cols])
                            if kind == ATTEND:
                                ins = nc.gpsimd.tensor_copy(idx_d[:, r], dst_i[:, cols])
                            ins.then_inc(idx_ready, 1)
                            idx_barrier(pool, NO * k + OB * i + ob - (NO - NO // 2 if past_max(k) else 0))
                            for q in range(U * ob, U * ob + U):
                                nc.gpsimd.indirect_dma_start(
                                    ring[:, q, 0:gw], None, table,
                                    bass.IndirectOffsetOnAxis(ap=idx[:, q:q + 1], axis=0)).then_inc(gathered[q], 16)
                                if kind == ATTEND:
                                    nc.gpsimd.indirect_dma_start(
                                        gt[:, q, :], None, target_table,
                                        bass.IndirectOffsetOnAxis(ap=idx_d[:, q:q + 1], axis=0)
                                    ).then_inc(gathered_d[q], 16)

                @block.tensor
                def _(pe):
                    if first_work:
                        first_work[0](pe)
                    def encode(i, ob):
                        o = NO * l + OB * i + ob
                        pe.wait_ge(stk_in[ob], 16 * (NG * l + i + 1))
                        for u in range(U):
                            if u % 2 == 0:
                                pe.wait_ge(pre_added, U * o + u + 2)
                            nc.tensor.matmul(psE[:, D * u:D * u + D], stk[:, ob, P * u:P * u + P],
                                             we_stk[:, :], start=True, stop=True).then_inc(encoded, 1)

                    if kind == MESSAGE:
                        encode(0, 0)
                    with pe.Fori(0, NG) as i:
                        for ob in range(OB):
                            h = OB * i + ob
                            if kind == MESSAGE:
                                if ob < OB - 1:
                                    encode(i, ob + 1)
                                else:
                                    with pe.If(i < NG - 1):
                                        encode(i + 1, 0)
                            cnt = pe.value_load(span_row[0:1, bass.ds(2 * h + 1, 1)], min_val=1, max_val=NB)

                            def unit(_, first):
                                c = pe.snap(npe)
                                pe.wait_ge(unit_added, c + 2 * U)
                                for u in range(U):
                                    q = U * ob + u
                                    if first:
                                        if kind in (MESSAGE, WEIGHTED):
                                            pe.wait_ge(message, NT * k + U * h + u + 1)
                                        elif kind == ATTEND:
                                            pe.wait_ge(weighed, U * h + u + 1)
                                        else:
                                            pe.wait_ge(gathered[q], 16 * (NG * k + i + 1))
                                    if u % 4 == 0:
                                        pe.wait_ge(onehot_ready, c + u + 4)
                                    nc.tensor.matmul(psA[:, 0:width], S[:, u, :], ring[:, q, 0:width],
                                                     start=(u == 0), stop=(u == U - 1)).then_inc(onehot_used, 1)
                                pe.reg_add(npe, npe, U)

                            units(pe, None, cnt, unit)
                            pe.drain().then_inc(octet_free, 1)

                @block.scalar
                def _(act):
                    if first_work:
                        first_work[1](act)
                    if kind == MESSAGE:
                        with act.Fori(0, NG) as i:
                            for q in range(RING):
                                t = NT * l + RING * i + q
                                act.wait_ge(pre_added, U + t + 1)
                                nc.scalar.activation(ring[:, q, 0:D], ring[:, q, 0:D], ACT.Relu
                                                     ).then_inc(message, 1)
                    if kind == WEIGHTED:
                        with act.Fori(0, NG) as i:
                            for q in range(RING):
                                act.wait_ge(gathered[q], 16 * (NG * k + i + 1))
                                nc.scalar.activation(ring[:, q, 0:D], ring[:, q, 0:D], ACT.Copy,
                                                     scale=weight[:, bass.ds(RING * i + q, 1)]).then_inc(message, 1)
                    if kind == ATTEND:
                        with act.Fori(0, NG) as i:
                            for ob in range(OB):
                                act.wait_ge(logits, OB * i + ob + 1)
                                nc.scalar.activation(ring[:, U * ob:U * ob + U, D:GW], al[:, :, :], ACT.Exp
                                                     ).then_inc(exps, 1)

                @block.vector
                def _(dve):
                    nc.vector.memset(AGG[:, :], 0.0)
                    nc.vector.memset(psA[:, 0:width], 0.0)
                    dve.reg_mov(last_blk, 0)
                    dve.drain()
                    if first_work:
                        first_work[2](dve)

                    def add_sums():
                        b = nc.s_assert_within(dve.snap(last_blk), 0, NB - 1,
                                               skip_runtime_bounds_check_because="a unit's block")
                        a = AGG[:, bass.ds(b * AW, width)]
                        return nc.vector.tensor_tensor(a, a, psA[:, 0:width], ALU.add)

                    with dve.Fori(0, NG) as i:
                        for ob in range(OB):
                            h = OB * i + ob
                            o = NO * l + h
                            lo, cnt = span_of(dve, h)

                            def messages():
                                for u in range(U):
                                    q = U * ob + u
                                    dve.wait_ge(gathered[q], 16 * (NG * k + i + 1))
                                    if u % 2 == 0:
                                        dve.wait_ge(encoded, U * o + u + 2 + OB * U)
                                    nc.vector.tensor_tensor(ring[:, q, 0:D], ring[:, q, 0:D],
                                                            psE[:, D * u:D * u + D], ALU.add).then_inc(pre_added, 1)

                            def attention():
                                for u in range(U):
                                    q = U * ob + u
                                    dve.wait_ge(gathered[q], 16 * (NG * k + i + 1))
                                    dve.wait_ge(gathered_d[q], 16 * (i + 1))
                                r = slice(U * ob, U * ob + U)
                                nc.vector.tensor_tensor(al[:, :, :], ring[:, r, D:GW], gt[:, r, 0:HEADS], ALU.add)
                                dve.drain()
                                nc.vector.scalar_tensor_tensor(al[:, :, :], al[:, :, :], 0.2, al[:, :, :],
                                                               ALU.mult, ALU.max)
                                dve.drain()
                                nc.vector.tensor_tensor(al[:, :, :], al[:, :, :], gt[:, r, HEADS:2 * HEADS],
                                                        ALU.subtract).then_inc(logits, 1)
                                dve.wait_ge(exps, h + 1)
                                for u in range(U):
                                    q = U * ob + u
                                    hv = ring[:, q, 0:D].rearrange("p (h c) -> p h c", h=HEADS)
                                    nc.vector.tensor_tensor(
                                        hv, hv, ring[:, q, D:GW].unsqueeze(2).to_broadcast([P, HEADS, C]),
                                        ALU.mult).then_inc(weighed, 1)

                            def unit(blk, first):
                                c = dve.snap(nd)
                                if first and kind == MESSAGE:
                                    messages()
                                if first and kind == ATTEND:
                                    attention()
                                one_hots(dve, h, blk, c, 0)
                                dve.wait_ge(onehot_used, c + U)
                                dve.wait_ge(unit_added, c + U)
                                add_sums().then_inc(unit_added, U)
                                one_hots(dve, h, blk, c, 1)
                                dve.reg_mov(last_blk, blk)
                                dve.reg_add(nd, nd, U)

                            units(dve, lo, cnt, unit)
                    c = dve.snap(nd)
                    dve.wait_ge(onehot_used, c + U)
                    dve.wait_ge(unit_added, c + U)
                    add_sums()

        def max_pass(k):
            with nc.Block() as block:
                @block.gpsimd
                def _(pool):
                    with pool.Fori(0, NG) as i:
                        for g in range(GR):
                            r = slice(MT * g, MT * g + MT)
                            pool.wait_ge(scoresT, GR * i + g + 1)
                            nc.gpsimd.tensor_copy(idx[:, r], src_i[:, bass.ds(RING * i + MT * g, MT)]
                                                  ).then_inc(idx_ready, 1)
                            idx_barrier(pool, NO * k + GR * i + g)
                            for q in range(MT * g, MT * g + MT):
                                nc.gpsimd.indirect_dma_start(
                                    gs[:, HEADS * q:HEADS * q + HEADS], None, score_table,
                                    bass.IndirectOffsetOnAxis(ap=idx[:, q:q + 1], axis=0)).then_inc(gathered[q], 16)

                @block.tensor
                def _(pe):
                    with pe.Fori(0, NG) as i:
                        for g in range(GR):
                            n = GR * i + g
                            for q in range(MT * g, MT * g + MT):
                                pe.wait_ge(gathered[q], 16 * (NG * k + i + 1))
                            pe.wait_ge(d16_ready, n + 1)
                            nc.tensor.transpose(psE[:, 0:P], gs[:, P * g:P * g + P], ident[:, :])
                            nc.tensor.transpose(psE[:, 512:512 + P], d16[:, :], ident[:, :]).then_inc(scoresT, 1)
                            pe.wait_ge(runs_ready, n + 1)
                            nc.tensor.transpose(psE[:, 1024:1024 + P], run[:, :], ident[:, :])
                            nc.tensor.transpose(psE[:, 1536:1536 + P], last[:, :], ident[:, :]).then_inc(runsT, 1)
                            pe.wait_ge(picks_ready, n + 1)
                            for half in range(2):
                                cnt = pe.value_load(span_row[0:1, bass.ds(2 * (2 * n + half) + 1, 1)],
                                                    min_val=1, max_val=NB)

                                def unit(_, first):
                                    c = pe.snap(npe)
                                    pe.wait_ge(unit_added, c + U)
                                    for u in range(U):
                                        if u % 4 == 0:
                                            pe.wait_ge(onehot_ready, c + u + 4)
                                        nc.tensor.matmul(psA[:, (HEADS + 1) * u:(HEADS + 1) * (u + 1)], S[:, u, :],
                                                         picks[:, U * half + u, :], start=True, stop=True
                                                         ).then_inc(onehot_used, 1)
                                    pe.reg_add(npe, npe, U)

                                units(pe, None, cnt, unit)
                                pe.drain().then_inc(octet_free, 1)

                @block.vector
                def _(dve):
                    nc.vector.memset(DTp[:, 0:P], -1.0)
                    nc.vector.memset(DTp[:, 2 * P:3 * P], -2.0)
                    nc.vector.memset(GTp[:, 0:P], 0.0)
                    nc.vector.tensor_copy(a_max[:, :, :], a_src[:, :, :])
                    dve.drain()
                    uns = dve.value_load(unsorted_i[0:1, 0:1], min_val=0, max_val=1)
                    am = flat(a_max[:, :, :])
                    GT, DT = GTp[:, P:2 * P], DTp[:, P:2 * P]
                    with dve.Fori(0, 2 * NG if GR == 2 else NG) as n:
                        dve.wait_ge(scoresT, n + 2)
                        copied(d16[:, :].rearrange("p (q h) -> p q h", h=HEADS),
                               dst_f[:, bass.ds(MT * n, MT)].unsqueeze(2).to_broadcast([P, MT, HEADS])
                               ).then_inc(d16_ready, 1)
                        dve.wait_ge(scoresT, n + 3)
                        nc.vector.tensor_copy(GT, psE[:, 0:P])
                        nc.vector.tensor_copy(DT, psE[:, 512:512 + P])
                        dve.drain()
                        with dve.If(uns > 0):
                            nc.vector.tensor_copy(run[:, :], GT)
                            nc.vector.memset(last[:, :], 1.0)
                            dve.drain()
                            with dve.Fori(1, P) as s:
                                nc.vector.tensor_tensor(pen[:, :], DT, DTp[:, bass.ds(P - s, P)], ALU.is_equal)
                                dve.drain()
                                nc.vector.tensor_scalar(pen[:, :], pen[:, :], 1.0, BIG, ALU.subtract, ALU.mult)
                                dve.drain()
                                nc.vector.tensor_tensor(pen[:, :], pen[:, :], GTp[:, bass.ds(P - s, P)], ALU.add)
                                dve.drain()
                                nc.vector.tensor_tensor(run[:, :], run[:, :], pen[:, :], ALU.max)
                                dve.drain()
                                nc.vector.tensor_tensor(pen[:, :], DT, DTp[:, bass.ds(s + P, P)], ALU.not_equal)
                                dve.drain()
                                nc.vector.tensor_tensor(last[:, :], last[:, :], pen[:, :], ALU.mult)
                                dve.drain()
                        with dve.Else():
                            nc.vector.tensor_tensor(pen[:, :], DT, DTp[:, P - 1:2 * P - 1], ALU.not_equal)
                            nc.vector.tensor_tensor(last[:, :], DT, DTp[:, P + 1:2 * P + 1], ALU.not_equal)
                            dve.drain()
                            nc.vector.tensor_scalar(pen[:, :], pen[:, :], -BIG, None, ALU.mult)
                            dve.drain()
                            nc.vector.tensor_tensor_scan(run[:, :], pen[:, :], GT, -BIG, ALU.add, ALU.max)
                            dve.drain()
                        nc.vector.tensor_tensor(run[:, :], run[:, :], last[:, :], ALU.mult).then_inc(runs_ready, 1)
                        dve.wait_ge(runsT, n + 1)
                        nc.vector.tensor_copy(picks[:, :, 0:HEADS],
                                              psE[:, 1024:1024 + P].rearrange("p (q h) -> p q h", h=HEADS))
                        nc.vector.tensor_copy(picks[:, :, HEADS:HEADS + 1],
                                              psE[:, 1536:1536 + P].rearrange("p (q h) -> p q h", h=HEADS)[:, :, 0:1]
                                              ).then_inc(picks_ready, 1)
                        for half in range(2):
                            h = 2 * n + half
                            lo, cnt = span_of(dve, h)

                            def unit(blk, first):
                                c = dve.snap(nd)
                                one_hots(dve, h, blk, c, 0)
                                one_hots(dve, h, blk, c, 1)
                                dve.wait_ge(onehot_used, c + 2 * U)
                                pv = psA[:, 0:(HEADS + 1) * U].rearrange("p (u h) -> p u h", u=U)
                                nc.vector.tensor_scalar(cand[:, :, :], pv[:, :, HEADS:HEADS + 1].to_broadcast(
                                    [P, U, HEADS]), 1.0, BIG, ALU.subtract, ALU.mult)
                                dve.drain()
                                nc.vector.tensor_tensor(cand[:, :, :], cand[:, :, :], pv[:, :, 0:HEADS], ALU.add)
                                dve.drain()
                                nc.vector.tensor_reduce(cmax[:, :], cand[:, :, :].rearrange("p u h -> p h u"),
                                                        AX.X, ALU.max)
                                dve.drain()
                                a = am[:, bass.ds(blk * HEADS, HEADS)]
                                nc.vector.tensor_tensor(a, a, cmax[:, :], ALU.max)
                                dve.drain().then_inc(unit_added, U)
                                dve.reg_add(nd, nd, U)

                            units(dve, lo, cnt, unit)

        def staged(eng, *stages):
            for b in range(2):
                for s, stage in enumerate(stages):
                    if b >= s:
                        stage(b - s, (b - s) % 2, (b - s) // 2)
            with eng.Fori(1, NB // 2) as j:
                for q in range(2):
                    for s, stage in enumerate(stages):
                        stage(2 * j + (q - s), (q - s) % 2, j + (q - s) // 2)
            for b in range(NB, NB + 2):
                for s, stage in enumerate(stages):
                    if b - s < NB:
                        stage(b - s, (b - s) % 2, (b - s) // 2)

        turned = (psT, psV)

        def result_of(q):
            return psE[:, 512 * (2 + q):512 * (2 + q) + D]

        def node_phase(m, pre, post, hidden=False, second=False, bias=False, store=None, st=0, pool_post=None,
                       loads=None):
            def ready(b):
                return NB * m + b + 3

            def free(b):
                return NB * m + b + 1

            def rest(b, q, hb):
                pass

            with nc.Block() as block:
                @block.sync
                def _(sp):
                    if loads:
                        loads(sp)

                    def put(b, q, hb):
                        sp.wait_ge(tab_ready, NB * st + b + 1)
                        store(sp, b, q).then_inc(stored[q], 16)

                    if store:
                        staged(sp, put)
                        for q in range(2):
                            sp.wait_ge(stored[q], 16 * ((NB // 2) * (st + 1) + 1))
                        sp.sem_inc(loads_seen, 1)

                @block.gpsimd
                def _(pool):
                    def add(b, q, hb):
                        pool.wait_ge(o_used, ready(b))
                        pool.wait_ge(stored[q], 16 * ((NB // 2) * st + hb + 1))
                        pool_post(pool, b, q).then_inc(tab_ready, 1)

                    if pool_post:
                        staged(pool, add)

                @block.vector
                def _(dve):
                    def before(b, q, hb):
                        dve.wait_ge(t_done, free(b))
                        pre(dve, b, q).then_inc(t_in, 1)

                    def after(b, q, hb):
                        dve.wait_ge(o_done, ready(b))
                        if store and not pool_post:
                            dve.wait_ge(stored[q], 16 * ((NB // 2) * st + hb + 1))
                        post(dve, b, q).then_inc(o_used, 1)
                        if store and not pool_post:
                            dve.drain().then_inc(tab_ready, 1)

                    if hidden:
                        staged(dve, before, rest, after)
                    else:
                        staged(dve, before, after)

                @block.tensor
                def _(pe):
                    def turn(b, q, hb):
                        pe.wait_ge(t_in, ready(b))
                        pe.wait_ge(t_copied, free(b))
                        for f in range(2):
                            ins = nc.tensor.transpose(turned[q][:, P * f:P * f + P],
                                                      tin[:, q, P * f:P * f + P], ident[:, :])
                        if second:
                            for f in range(2):
                                ins = nc.tensor.transpose(turned[q][:, D + P * f:D + P * f + P],
                                                          tin2[:, q, P * f:P * f + P], ident[:, :])
                        ins.then_inc(t_done, 1)

                    def hid(b, q, hb):
                        pe.wait_ge(t_copied, ready(b))
                        pe.wait_ge(hid_relu, free(b))
                        for j in range(4):
                            for f in range(2):
                                ins = nc.tensor.matmul(psE[:, 512 * q + P * j:512 * q + P * j + P],
                                                       w1_sb[:, f, P * j:P * j + P], tT[:, q, P * f:P * f + P],
                                                       start=(f == 0), stop=(f == 1))
                        ins.then_inc(hid_done, 1)

                    def result(b, q, hb):
                        pe.wait_ge(hid_relu if hidden else t_copied, ready(b))
                        pe.wait_ge(o_used, free(b))
                        terms = ([(hT[:, q, P * j:P * j + P], w2_sb[:, j, :]) for j in range(4)] if hidden else
                                 [(tT[:, q, P * f:P * f + P], wa_sb[:, f, :]) for f in range(2)])
                        if second:
                            terms += [(tT2[:, q, P * f:P * f + P], wb_sb[:, f, :]) for f in range(2)]
                        if bias:
                            terms.append((ones[0:1, :], bias_row[0:1, :]))
                        for n, (a, w) in enumerate(terms):
                            ins = nc.tensor.matmul(result_of(q), a, w,
                                                   start=(n == 0), stop=(n == len(terms) - 1))
                        ins.then_inc(o_done, 1)

                    if hidden:
                        staged(pe, turn, hid, result)
                    else:
                        staged(pe, turn, result)
                        pe.sem_inc(hid_done, NB)

                @block.scalar
                def _(act):
                    def copy(b, q, hb):
                        act.wait_ge(t_done, ready(b))
                        act.wait_ge(hid_done if hidden else o_done, free(b))
                        ins = nc.scalar.copy(tT[:, q, :], turned[q][:, 0:D])
                        if second:
                            ins = nc.scalar.copy(tT2[:, q, :], turned[q][:, D:2 * D])
                        ins.then_inc(t_copied, 1)

                    def relu(b, q, hb):
                        act.wait_ge(hid_done, ready(b))
                        act.wait_ge(o_done, free(b))
                        for j in range(4):
                            ins = nc.scalar.activation(hT[:, q, P * j:P * j + P],
                                                       psE[:, 512 * q + P * j:512 * q + P * j + P],
                                                       ACT.Relu, bias=b1_col[:, j:j + 1])
                        ins.then_inc(hid_relu, 1)

                    if hidden:
                        staged(act, copy, relu)
                    else:
                        staged(act, copy)

        def on_vector(steps):
            with nc.Block() as block:
                @block.vector
                def _(dve):
                    for step in steps:
                        step()
                        dve.drain()

        def on_scalar(steps):
            with nc.Block() as block:
                @block.scalar
                def _(act):
                    for step in steps:
                        step()
                        act.drain()

        def on_tensor(steps):
            with nc.Block() as block:
                @block.tensor
                def _(pe):
                    for step in steps:
                        step()

        def blk(t, b, w=D, pitch=D):
            return t[:, bass.ds(b * pitch, w)] if not isinstance(b, int) else t[:, b * pitch:b * pitch + w]

        def whole(t, w=D, pitch=D):
            return t[:, 0:NB * pitch].rearrange("p (b f) -> p b f", f=pitch)[:, :, 0:w]

        def over(row, nb=NB):
            return row.unsqueeze(1).to_broadcast([P, nb, D])

        def dma_block(*copies):
            with nc.Block() as block:
                @block.sync
                def _(sp):
                    copy_in(sp, block_copied, block_count, *copies)

        block_copied = sem("block_copied")
        block_count = [0]

        def copy_in(sp, s, count, *copies):
            for o, i in copies:
                sp.dma_start(o, i).then_inc(s, 16)
            count[0] += 16 * len(copies)
            sp.wait_ge(s, count[0])

        node_view = node_table.rearrange("(b p) f -> p b f", p=P)

        dma_block((src_i[:, :].rearrange("p (h u) -> p h u", u=U), src.rearrange("(h p u) -> p h u", p=P, u=U)),
                  (dst_i[:, :].rearrange("p (h u) -> p h u", u=U), dst.rearrange("(h p u) -> p h u", p=P, u=U)),
                  (weight[:, :].rearrange("p (h u) -> p h u", u=U),
                   edge_weight.rearrange("(h p u) -> p h u", p=P, u=U)),
                  (whole(H), x.rearrange("(b p) f -> p b f", p=P)),
                  (vn[:, :], row_bcast(vn_emb0)))
        iota_t = AGG[:, 0:P].bitcast(I32)
        start_t = AGG[:, P:P + NB].bitcast(I32)
        with nc.Block() as block:
            @block.gpsimd
            def _(pool):
                nc.gpsimd.iota(iota_t, pattern=[[1, P]], base=0, channel_multiplier=0)
                nc.gpsimd.iota(start_t, pattern=[[P, NB]], base=0, channel_multiplier=0)
                nc.gpsimd.iota(iota_i[:, :], pattern=[[1, P]], base=0, channel_multiplier=-1)

            @block.tensor
            def _(pe):
                pe.reg_mov(npe, 0)
                pe.sem_inc(octet_free, OB)
                pe.sem_inc(onehot_used, U)
                pe.sem_inc(encoded, OB * U)
                pe.sem_inc(unit_added, U)
                pe.sem_inc(pre_added, U)
                pe.sem_inc(scoresT, GR)
                pe.sem_inc(stored[0], 16)
                pe.sem_inc(stored[1], 16)
                for s in (t_in, t_done, t_copied, hid_done, hid_relu, o_done, o_used):
                    pe.sem_inc(s, 2)

            @block.vector
            def _(dve):
                dve.reg_mov(nd, 0)
                nc.vector.memset(ones[:, :], 1.0)
                nc.vector.memset(eps[:, :], EPS)
                nc.vector.memset(ring[:, :, AW - 1:AW], 1.0)
                nc.vector.tensor_copy(dst_f[:, :], dst_i[:, :])
        blk_t = AGG[:, N:N + NT].bitcast(I32)
        on_vector([
            lambda: nc.vector.tensor_copy(iota[:, :], iota_t),
            lambda: nc.vector.tensor_copy(block_start[:, :], start_t),
            lambda: nc.vector.tensor_scalar(ident[:, :], iota_i[:, :], 0.0, None, ALU.is_equal),
            lambda: nc.vector.tensor_scalar(blk_t, dst_i[:, :], P.bit_length() - 1, None, ALU.arith_shift_right),
            lambda: nc.vector.tensor_reduce(small[:, 0:NO], blk_t.rearrange("p (h u) -> p h u", u=U), AX.X, ALU.min),
            lambda: nc.vector.tensor_reduce(small[:, NO:2 * NO], blk_t.rearrange("p (h u) -> p h u", u=U),
                                            AX.X, ALU.max),
        ])
        on_tensor([lambda: nc.tensor.transpose(psT[0:NO, 0:P], small[:, 0:NO], ident[:, :]),
                   lambda: nc.tensor.transpose(psT[0:NO, P:2 * P], small[:, NO:2 * NO], ident[:, :])] +
                  [(lambda c=c: nc.tensor.transpose(psE[:, P * c:P * c + P], dst_f[:, P * c:P * c + P], ident[:, :]))
                   for c in range(NT // P)])
        on_vector([
            lambda: nc.vector.tensor_reduce(spans[:, 0:1], psT[0:NO, 0:P], AX.X, ALU.min),
            lambda: nc.vector.tensor_reduce(spans[:, 1:2], psT[0:NO, P:2 * P], AX.X, ALU.max),
            lambda: nc.vector.tensor_tensor(spans[:, 1:2], spans[:, 1:2], spans[:, 0:1], ALU.subtract),
            lambda: nc.vector.tensor_scalar_add(spans[:, 1:2], spans[:, 1:2], 1.0),
            lambda: nc.vector.tensor_copy(spans_i[:, :], spans[:, :]),
            lambda: nc.vector.tensor_copy(AGG[:, 0:NT], psE[:, 0:NT]),
            lambda: nc.vector.tensor_tensor(
                AGG[:, NT:2 * NT].rearrange("p (c e) -> p c e", e=P)[:, :, 0:P - 1],
                AGG[:, 0:NT].rearrange("p (c e) -> p c e", e=P)[:, :, 0:P - 1],
                AGG[:, 0:NT].rearrange("p (c e) -> p c e", e=P)[:, :, 1:P], ALU.is_gt),
            lambda: nc.vector.tensor_reduce(
                small[:, 0:NT // P], AGG[:, NT:2 * NT].rearrange("p (c e) -> p c e", e=P)[:, :, 0:P - 1],
                AX.X, ALU.max),
            lambda: nc.vector.tensor_reduce(small2[:, 0:1], small[:, 0:NT // P], AX.X, ALU.max),
        ])
        on_tensor([lambda: nc.tensor.transpose(psT[0:1, 0:P], small2[:, 0:1], ident[:, :])])
        on_vector([
            lambda: nc.vector.tensor_reduce(small2[0:1, 0:1], psT[0:1, 0:P], AX.X, ALU.max),
            lambda: nc.vector.tensor_copy(unsorted_i[:, :], small2[0:1, 0:1]),
        ])
        dma_block((range_scratch, spans_i[:, :]),
                  (AGG[:, 0:NO * P].rearrange("p (h v) -> p h v", v=P),
                   edge_attr.rearrange("(h p u) f -> p h (u f)", p=P, u=U)))
        dma_block((span_row[:, :], range_scratch.rearrange("h c -> (h c)").unsqueeze(0)))

        with nc.Block() as block:
            @block.gpsimd
            def _(pool):
                nc.gpsimd.iota(iota_i[:, 0:1], pattern=[[0, 1]], base=0, channel_multiplier=1)
        slot = small2[:, 0:1]
        on_vector([
            lambda: nc.vector.tensor_scalar(iota_i[:, 1:2], iota_i[:, 0:1], FE.bit_length() - 1, None,
                                            ALU.arith_shift_right),
            lambda: nc.vector.tensor_copy(slot, iota_i[:, 1:2]),
            lambda: nc.vector.tensor_scalar(wpart[:, 0:1], slot, 0.0, None, ALU.is_equal),
            lambda: nc.vector.tensor_scalar(wpart[:, 1:2], slot, 1.0, None, ALU.is_equal),
            lambda: nc.vector.tensor_scalar(wpart[:, 2:3], slot, 2.0, None, ALU.is_equal)] + [
            step for s_ in range(3, PARTS) for step in (
                lambda s_=s_: nc.vector.tensor_scalar(small2[:, 1:2], slot, float(s_), None, ALU.is_equal),
                lambda s_=s_: nc.vector.tensor_tensor(wpart[:, s_ % 3:s_ % 3 + 1], wpart[:, s_ % 3:s_ % 3 + 1],
                                                      small2[:, 1:2], ALU.add))])

        hi, mid, lo3 = (hT[:, 0, P * n:P * n + P] for n in range(3))
        parts_b = tab[:, :, :].rearrange("p a b -> p (a b)").bitcast(BF16)
        nat = tT[:, :, :].rearrange("p a b -> p (a b)").bitcast(BF16)
        turned_b = [psE[:, 1024 * q:1024 * q + 512].bitcast(BF16) for q in range(2)]
        stk_made, stk_turned, stk_copied = sem("stk_made"), sem("stk_turned"), sem("stk_copied")
        stk_out = [sem("stk_out0"), sem("stk_out1")]
        split_step = sem("split_step")
        ident_b = sb("ident_b", [P, P], BF16)
        on_vector([lambda: nc.vector.tensor_copy(ident_b[:, :], ident[:, :])])
        with nc.Block() as block:
            @block.vector
            def _(dve):
                for h in range(NO):
                    ea = AGG[:, P * h:P * h + P]
                    hb, mb, lb = (parts_b[:, P * (3 * (h % 2) + n):P * (3 * (h % 2) + n) + P] for n in range(3))
                    n = [0]

                    def then(ins):
                        n[0] += 1
                        ins.then_inc(split_step, 1)
                        dve.wait_ge(split_step, 5 * h + n[0])

                    then(nc.vector.tensor_copy(hb, ea))
                    then(nc.vector.tensor_tensor(mid, ea, hb, ALU.subtract))
                    then(nc.vector.tensor_copy(mb, mid))
                    then(nc.vector.tensor_tensor(lo3, mid, mb, ALU.subtract))
                    then(nc.vector.tensor_copy(lb, lo3))
                    if h:
                        dve.wait_ge(stk_turned, h)
                    for part, s0, s1 in ((hb, 0, 3), (mb, 3, 6), (lb, 6, PARTS)):
                        ins = nc.vector.tensor_copy(
                            nat.rearrange("p (u s f) -> p u s f", u=U, f=FE)[:, :, s0:s1, :],
                            part.rearrange("p (u f) -> p u f", u=U).unsqueeze(2).to_broadcast(
                                [P, U, s1 - s0, FE]))
                    ins.then_inc(stk_made, 1)

            @block.tensor
            def _(pe):
                for h in range(NO):
                    pe.wait_ge(stk_made, h + 1)
                    if h >= 2:
                        pe.wait_ge(stk_copied, h - 1)
                    for u in range(U):
                        ins = nc.tensor.transpose(turned_b[h % 2][:, P * u:P * u + P], nat[:, P * u:P * u + P],
                                                  ident_b[:, :])
                    ins.then_inc(stk_turned, 1)

            @block.scalar
            def _(act):
                for h in range(NO):
                    act.wait_ge(stk_turned, h + 1)
                    if h >= 2:
                        act.wait_ge(stk_out[h % 2], 16 * (h // 2))
                    nc.scalar.copy(stk[:, h % 2, :], turned_b[h % 2]).then_inc(stk_copied, 1)

            @block.sync
            def _(sp):
                for h in range(NO):
                    sp.wait_ge(stk_copied, h + 1)
                    sp.dma_start(stack_table[P * h:P * h + P, :], stk[:, h % 2, :]).then_inc(stk_out[h % 2], 16)
                for q in range(2):
                    sp.wait_ge(stk_out[q], 16 * (NO // 2))

        def load_we(sp, l):
            for g in range(PARTS):
                sp.dma_start(we_rep[FE * g:FE * g + FE, :], at(We, l)).then_inc(we_loaded, 16)
            sp.wait_ge(we_loaded, 16 * PARTS * (l + 1))
            sp.sem_inc(loads_seen, 1)

        def at(t, l):
            return t[bass.ds(l, 1)].squeeze(0) if not isinstance(l, int) else t[l]

        we_loaded = sem("we_loaded")
        with nc.Block() as block:
            @block.sync
            def _(sp):
                load_we(sp, 0)
                copy_in(sp, block_copied, block_count, (be_row[:, :], row_bcast(be[0])))
        on_vector([
            lambda: nc.vector.tensor_tensor(whole(H), whole(H), over(vn[:, :]), ALU.add),
            lambda: nc.vector.tensor_tensor(whole(AGG), whole(H), over(be_row[:, :]), ALU.add),
        ])
        dma_block((node_view, whole(AGG)))

        layer_loaded = sem("layer_loaded")
        virtual_loaded = sem("virtual_loaded")
        roots = sem("roots")
        we_split = sem("we_split")
        vn_pe, vn_dve = sem("vn_pe"), sem("vn_dve")
        vrows = Y[:, 0:6 * D].rearrange("p (r f) -> p r f", f=D)
        vtin = Y[:, 6 * D:7 * D]
        vtT = Y[:, 7 * D:8 * D]
        wsp = Y[:, 8 * D:12 * D]
        VPE, VDVE = 5, 4

        def layer(l, last_layer):
            copies = ([(w1_sb[:, :, :], at(W1, l).rearrange("(f p) n -> p f n", p=P)),
                       (w2_sb[:, :, :], at(W2, l).rearrange("(f p) n -> p f n", p=P)),
                       (rows[:, 0, :], row_bcast(at(bn_v, l))), (rows[:, 1, :], row_bcast(at(bn_g, l))),
                       (rows[:, 2, :], row_bcast(at(bn_m, l))), (rows[:, 3, :], row_bcast(at(bn_b, l))),
                       (rows[:, 4, :], row_bcast(at(b2, l)))] +
                      [(b1_col[:, j:j + 1], at(b1, l)[P * j:P * j + P].unsqueeze(1)) for j in range(4)])
            copies.append((be_row[:, :], row_bcast(at(be, l if last_layer else l + 1))))
            virtual = [] if last_layer else [
                (wa_sb[:, :, :], at(Wv1, l).rearrange("(f p) n -> p f n", p=P)),
                (wb_sb[:, :, :], at(Wv2, l).rearrange("(f p) n -> p f n", p=P)),
                (vrows[:, 0, :], row_bcast(at(vn_v, l))), (vrows[:, 1, :], row_bcast(at(vn_g, l))),
                (vrows[:, 2, :], row_bcast(at(vn_m, l))), (vrows[:, 3, :], row_bcast(at(vn_b, l))),
                (vrows[:, 4, :], row_bcast(at(bv1, l))), (vrows[:, 5, :], row_bcast(at(bv2, l)))]

            def loads(sp):
                for o, i in virtual:
                    sp.dma_start(o, i).then_inc(virtual_loaded, 16)
                for o, i in copies:
                    sp.dma_start(o, i).then_inc(layer_loaded, 16)

                def seen(sp):
                    sp.wait_ge(layer_loaded, 16 * len(copies) * (l + 1))
                    sp.sem_inc(loads_seen, 1)
                return seen

            def first_pe(pe):
                if not last_layer:
                    for b in range(NB):
                        ins = nc.tensor.matmul(psV[:, 0:D], ones[:, :], H[:, D * b:D * b + D],
                                               start=(b == 0), stop=(b == NB - 1))
                    ins.then_inc(vn_pe, 1)
                    for n, w in enumerate((wa_sb, wb_sb)):
                        pe.wait_ge(vn_dve, VDVE * l + 2 * n + 1)
                        for f in range(2):
                            ins = nc.tensor.transpose(psT[:, P * f:P * f + P], vtin[:, P * f:P * f + P], ident[:, :])
                        ins.then_inc(vn_pe, 1)
                        if n == 0:
                            pe.wait_ge(virtual_loaded, 16 * len(virtual) * (l + 1))
                        pe.wait_ge(vn_dve, VDVE * l + 2 * n + 2)
                        for f in range(2):
                            ins = nc.tensor.matmul(psO[:, 0:D], vtT[:, P * f:P * f + P], w[:, f, :],
                                                   start=(f == 0), stop=(f == 1))
                        ins.then_inc(vn_pe, 1)
                pe.wait_ge(we_split, l + 1)
                pe.sem_inc(parts_seen, 1)

            def first_act(act):
                act.wait_ge(layer_loaded, 16 * len(copies) * (l + 1))
                ins = nc.scalar.activation(rows[:, 0, :], rows[:, 0, :], ACT.Sqrt, bias=eps[:, 0:1])
                if not last_layer:
                    act.wait_ge(virtual_loaded, 16 * len(virtual) * (l + 1))
                    ins = nc.scalar.activation(vrows[:, 0, :], vrows[:, 0, :], ACT.Sqrt, bias=eps[:, 0:1])
                ins.then_inc(roots, 1)

            def first_dve(dve):
                def chain(*steps):
                    for step in steps:
                        ins = step()
                        dve.drain()

                a, b_, c = wsp[:, 0:D], wsp[:, D:2 * D], wsp[:, 2 * D:3 * D]
                ab, bb = wsp[:, 3 * D:3 * D + P].bitcast(BF16), wsp[:, 3 * D + P:4 * D].bitcast(BF16)
                chain(lambda: nc.vector.tensor_copy(ab, we_rep[:, :]),
                      lambda: nc.vector.tensor_tensor(b_, we_rep[:, :], ab, ALU.subtract),
                      lambda: nc.vector.tensor_copy(bb, b_),
                      lambda: nc.vector.tensor_tensor(c, b_, bb, ALU.subtract),
                      lambda: nc.vector.tensor_scalar(a, ab, wpart[:, 0:1], None, ALU.mult),
                      lambda: nc.vector.scalar_tensor_tensor(a, bb, wpart[:, 1:2], a, ALU.mult, ALU.add))
                nc.vector.scalar_tensor_tensor(we_stk[:, :], c, wpart[:, 2:3], a, ALU.mult, ALU.add
                                               ).then_inc(we_split, 1)
                dve.wait_ge(roots, l + 1)
                chain(lambda: nc.vector.reciprocal(rows[:, 0, :], rows[:, 0, :]),
                      lambda: nc.vector.tensor_tensor(scale_row[:, :], rows[:, 0, :], rows[:, 1, :], ALU.mult),
                      lambda: nc.vector.tensor_tensor(bias_row[:, :], rows[:, 4, :], rows[:, 2, :], ALU.subtract),
                      lambda: nc.vector.tensor_tensor(bias_row[:, :], bias_row[:, :], scale_row[:, :], ALU.mult),
                      lambda: nc.vector.tensor_tensor(bias_row[:, :], bias_row[:, :], rows[:, 3, :], ALU.add),
                      lambda: nc.vector.tensor_tensor(w2_sb[:, :, :], w2_sb[:, :, :], over(scale_row[:, :], 4),
                                                      ALU.mult))
                if last_layer:
                    return
                chain(lambda: nc.vector.reciprocal(vrows[:, 0, :], vrows[:, 0, :]),
                      lambda: nc.vector.tensor_tensor(scale_row[:, :], vrows[:, 0, :], vrows[:, 1, :], ALU.mult),
                      lambda: nc.vector.tensor_tensor(vrows[:, 2, :], vrows[:, 4, :], vrows[:, 2, :], ALU.subtract),
                      lambda: nc.vector.tensor_tensor(vrows[:, 2, :], vrows[:, 2, :], scale_row[:, :], ALU.mult),
                      lambda: nc.vector.tensor_tensor(vrows[:, 2, :], vrows[:, 2, :], vrows[:, 3, :], ALU.add))
                dve.wait_ge(vn_pe, VPE * l + 1)
                nc.vector.tensor_tensor(vtin, psV[:, 0:D], vn[:, :], ALU.add).then_inc(vn_dve, 1)
                dve.wait_ge(vn_pe, VPE * l + 2)
                nc.vector.tensor_scalar(vtT, psT[:, 0:D], 1.0, None, ALU.mult).then_inc(vn_dve, 1)
                dve.wait_ge(vn_pe, VPE * l + 3)
                chain(lambda: nc.vector.tensor_tensor(vtin, psO[:, 0:D], scale_row[:, :], ALU.mult),
                      lambda: nc.vector.tensor_tensor(vtin, vtin, vrows[:, 2, :], ALU.add))
                nc.vector.tensor_scalar(vtin, vtin, 0.0, None, ALU.max).then_inc(vn_dve, 1)
                dve.wait_ge(vn_pe, VPE * l + 4)
                nc.vector.tensor_scalar(vtT, psT[:, 0:D], 1.0, None, ALU.mult).then_inc(vn_dve, 1)
                dve.wait_ge(vn_pe, VPE * l + 5)
                chain(lambda: nc.vector.tensor_tensor(vn[:, :], psO[:, 0:D], vn[:, :], ALU.add),
                      lambda: nc.vector.tensor_tensor(vn[:, :], vn[:, :], vrows[:, 5, :], ALU.add))

            edge_pass(MESSAGE, l, l, loads, (first_pe, first_act, first_dve))

            def pre(dve, b, q):
                return nc.vector.tensor_tensor(tin[:, q, :], blk(H, b), blk(AGG, b, D, agg_pitch), ALU.add)

            def post(dve, b, q):
                h = blk(H, b)
                if last_layer:
                    return nc.vector.tensor_tensor(blk(AGG, b, D, agg_pitch), result_of(q), h, ALU.add)
                nc.vector.scalar_tensor_tensor(h, result_of(q), 0.0, h, ALU.max, ALU.add)
                dve.drain()
                return nc.vector.tensor_tensor(h, h, vn[:, :], ALU.add)

            def table_rows(pool, b, q):
                return nc.gpsimd.tensor_tensor(tab[:, q, 0:D], blk(H, b), be_row[:, :], ALU.add)

            def store(sp, b, q):
                return sp.dma_start(node_rows(b), tab[:, q, 0:D])

            if last_layer:
                node_phase(l, pre, post, hidden=True, bias=True)
            else:
                node_phase(l, pre, post, hidden=True, bias=True, store=store, st=l, pool_post=table_rows,
                           loads=lambda sp: load_we(sp, l + 1))

        agg_pitch = AW

        def node_rows(b):
            return node_table[bass.ds(b * P, P), :] if not isinstance(b, int) else node_table[b * P:b * P + P, :]

        tin2 = sb("tin2", [P, 2, D])

        with nc.Fori(0, L - 1) as l:
            layer(l, False)
        layer(L - 1, True)

        def layer_norm():
            with nc.Block() as block:
                @block.vector
                def _(dve):
                    with dve.Fori(0, NB // 2) as j:
                        for q in range(2):
                            b = 2 * j + q
                            nc.vector.bn_stats(flat(stats[:, :, :])[:, bass.ds(b * 6, 6)],
                                               AGG[:, bass.ds(b * AW, D)])
                    dve.drain()
                    for b in range(NB):
                        nc.vector.bn_aggr(mv[:, b, :], stats[:, b, :])
            on_scalar([lambda: nc.scalar.activation(rstd[:, :], mv[:, :, 1:2].rearrange("p b o -> p (b o)"),
                                                    ACT.Sqrt, bias=eps[:, 0:1])])
            with nc.Block() as block:
                @block.vector
                def _(dve):
                    nc.vector.reciprocal(rstd[:, :], rstd[:, :])
                    dve.drain()
                    with dve.Fori(0, NB // 2) as j:
                        for q in range(2):
                            b = 2 * j + q
                            nc.vector.tensor_scalar(H[:, bass.ds(b * D, D)], AGG[:, bass.ds(b * AW, D)],
                                                    flat(mv[:, :, :])[:, bass.ds(b * 2, 1)],
                                                    rstd[:, bass.ds(b, 1)], ALU.subtract, ALU.mult)

        agg = whole(AGG, D, AW)
        dma_block((whole(H), x.rearrange("(b p) f -> p b f", p=P)))
        on_vector([lambda: nc.vector.tensor_tensor(agg, agg, whole(H), ALU.add)])
        layer_norm()
        dma_block((node_view, whole(H)))

        def col_w(w):
            return w.rearrange("(f p) n -> p f n", p=P)

        def second_loads(sp):
            copy_in(sp, block_copied, block_count, (w1_sb[:, :, 0:D], col_w(W_rel)), (w1_sb[:, :, D:2 * D], col_w(W_root)),
                    (bias_row[:, :], row_bcast(b_rel)), (rows[:, 0, :], row_bcast(gamma)),
                    (rows[:, 1, :], row_bcast(beta)))

        edge_pass(WEIGHTED, L, 0, second_loads)
        on_tensor([(lambda s=s, f=f, g=g: nc.tensor.transpose(
            psE[:, 1024 * s + 512 * f + P * g:1024 * s + 512 * f + P * g + P],
            w1_sb[:, g, D * s + P * f:D * s + P * f + P], ident[:, :]))
            for s in range(2) for f in range(2) for g in range(2)])
        on_vector([(lambda s=s, f=f: nc.vector.tensor_copy((wa_sb, wb_sb)[s][:, f, :],
                                                           psE[:, 1024 * s + 512 * f:1024 * s + 512 * f + D]))
                   for s in range(2) for f in range(2)])

        def pre_second(dve, b, q):
            copied(tin2[:, q, :], blk(H, b))
            dve.drain()
            return copied(tin[:, q, :], blk(AGG, b, D, AW))

        def to_agg(dve, b, q):
            return copied(blk(AGG, b, D, AW), result_of(q))

        node_phase(L, pre_second, to_agg, second=True, bias=True)
        on_tensor([(lambda b=b: nc.tensor.matmul(psV[:, 0:D], ones[:, :], AGG[:, AW * b:AW * b + D],
                                                 start=(b == 0), stop=(b == NB - 1))) for b in range(NB)])
        sqr = whole(Y)
        on_vector([
            lambda: nc.vector.tensor_scalar(scale_row[:, :], psV[:, 0:D], 1.0 / N, None, ALU.mult),
            lambda: nc.vector.tensor_tensor(agg, agg, over(scale_row[:, :]), ALU.subtract),
            lambda: nc.vector.tensor_tensor(sqr, agg, agg, ALU.mult),
        ])
        on_tensor([(lambda b=b: nc.tensor.matmul(psV[:, 0:D], ones[:, :], Y[:, D * b:D * b + D],
                                                 start=(b == 0), stop=(b == NB - 1))) for b in range(NB)])
        on_scalar([lambda: nc.scalar.activation(scale_row[:, :], psV[:, 0:D], ACT.Sqrt, bias=eps[:, 0:1],
                                                scale=1.0 / N)])
        on_vector([
            lambda: nc.vector.reciprocal(scale_row[:, :], scale_row[:, :]),
            lambda: nc.vector.tensor_tensor(scale_row[:, :], scale_row[:, :], rows[:, 0, :], ALU.mult),
            lambda: nc.vector.tensor_tensor(agg, agg, over(scale_row[:, :]), ALU.mult),
            lambda: nc.vector.tensor_tensor(agg, agg, over(rows[:, 1, :]), ALU.add),
            lambda: nc.vector.scalar_tensor_tensor(agg, agg, 0.0, whole(H), ALU.max, ALU.add),
            lambda: nc.vector.scalar_tensor_tensor(agg, agg, 0.0, whole(H), ALU.max, ALU.add),
        ])
        layer_norm()

        dma_block((wa_sb[:, :, :], col_w(gat_W)), (rows[:, 0, :], row_bcast(att_src.rearrange("h c -> (h c)"))),
                  (rows[:, 1, :], row_bcast(att_dst.rearrange("h c -> (h c)"))), (rows[:, 2, :], row_bcast(gat_bias)))

        def pre_h(dve, b, q):
            return copied(tin[:, q, :], blk(H, b))

        def post_att(dve, b, q):
            y = blk(Y, b)
            copied(y, result_of(q))
            for r, scores in ((0, a_src), (1, a_dst)):
                s = flat(scores[:, :, :])
                dve.drain()
                nc.vector.tensor_tensor(tin2[:, r, :], y, rows[:, r, :], ALU.mult)
                dve.drain()
                nc.vector.tensor_reduce(s[:, bass.ds(b * HEADS, HEADS)] if not isinstance(b, int) else
                                        s[:, b * HEADS:b * HEADS + HEADS],
                                        tin2[:, r, :].rearrange("p (h c) -> p h c", h=HEADS), AX.X, ALU.add)
            dve.drain()
            copied(tab[:, q, D:GW], blk(flat(a_src[:, :, :]), b, HEADS, HEADS))
            return copied(tab[:, q, 0:D], y)

        def store_att(sp, b, q):
            t = att_table[bass.ds(b * P, P), :] if not isinstance(b, int) else att_table[b * P:b * P + P, :]
            return sp.dma_start(t, tab[:, q, :])

        node_phase(L + 1, pre_h, post_att, store=store_att, st=L - 1)
        dma_block((score_table.rearrange("(b p) h -> p b h", p=P), a_src[:, :, :]))
        max_pass(L + 1)
        lk = small[:, 0:P]
        aS, aD, aM, eS = (flat(t[:, :, :]) for t in (a_src, a_dst, a_max, ex_self))
        both = stk_f[:, 8 * P:8 * P + NB * 2 * HEADS].rearrange("p (b h) -> p b h", b=NB)
        on_vector([
            lambda: nc.vector.tensor_tensor(aM, aM, aD, ALU.add),
            lambda: nc.vector.scalar_tensor_tensor(aM, aM, 0.2, aM, ALU.mult, ALU.max),
            lambda: nc.vector.tensor_copy(both[:, :, 0:HEADS], a_dst[:, :, :]),
            lambda: nc.vector.tensor_copy(both[:, :, HEADS:2 * HEADS], a_max[:, :, :]),
            lambda: nc.vector.tensor_tensor(eS, aS, aD, ALU.add),
            lambda: nc.vector.scalar_tensor_tensor(eS, eS, 0.2, eS, ALU.mult, ALU.max),
            lambda: nc.vector.tensor_tensor(eS, eS, aM, ALU.subtract),
        ])
        on_scalar([lambda: nc.scalar.activation(eS, eS, ACT.Exp)])
        dma_block((target_table.rearrange("(b p) h -> p b h", p=P), both[:, :, :]))
        edge_pass(ATTEND, L + 2)
        den = AGG[:, 0:NB * AW].rearrange("p (b f) -> p b f", f=AW)[:, :, D:GW]
        count = AGG[:, 0:NB * AW].rearrange("p (b f) -> p b f", f=AW)[:, :, AW - 1:AW]
        y4 = Y[:, :].rearrange("p (k c) -> p k c", c=C)
        on_vector([
            lambda: nc.vector.tensor_tensor(y4, y4, eS.unsqueeze(2).to_broadcast([P, NB * HEADS, C]), ALU.mult),
            lambda: nc.vector.tensor_tensor(agg, agg, whole(Y), ALU.add),
            lambda: nc.vector.tensor_tensor(ex_self[:, :, :], ex_self[:, :, :], den, ALU.add),
            lambda: nc.vector.tensor_scalar_add(eS, eS, 1e-16),
            lambda: nc.vector.reciprocal(eS, eS),
            lambda: nc.vector.tensor_copy(whole(Y), agg),
            lambda: nc.vector.tensor_tensor(y4, y4, eS.unsqueeze(2).to_broadcast([P, NB * HEADS, C]), ALU.mult),
            lambda: nc.vector.tensor_tensor(agg, whole(Y), over(rows[:, 2, :]), ALU.add),
            lambda: nc.vector.tensor_tensor(agg, agg, whole(H), ALU.add),
            lambda: nc.vector.tensor_scalar_add(dinv[:, :], count.rearrange("p b o -> p (b o)"), 1.0),
        ])
        on_scalar([lambda: nc.scalar.activation(dinv[:, :], dinv[:, :], ACT.Sqrt)])
        on_vector([lambda: nc.vector.reciprocal(dinv[:, :], dinv[:, :])])
        layer_norm()

        def dv(b):
            return dinv[:, bass.ds(b, 1)] if not isinstance(b, int) else dinv[:, b:b + 1]

        def pre_conv(dve, b, q):
            nc.vector.tensor_tensor(tin2[:, q, :], blk(AGG, b, D, AW), blk(Y, b), ALU.add)
            dve.drain()
            nc.vector.scalar_tensor_tensor(tin2[:, q, :], tin2[:, q, :], dv(b), rows[:, 0, :], ALU.mult, ALU.add)
            dve.drain()
            return nc.vector.tensor_scalar(tin[:, q, :], tin2[:, q, :], 0.0, None, ALU.max)

        def post_conv(dve, b, q):
            nc.vector.tensor_scalar(tab[:, q, 0:D], result_of(q), dv(b), None, ALU.mult)
            return nc.vector.tensor_scalar(blk(Y, b), result_of(q), dv(b), None, ALU.mult)

        def store_conv(sp, b, q):
            return sp.dma_start(node_rows(b), tab[:, q, 0:D])

        for n, (w, bb) in enumerate(((gW1, gb1), (gW2, gb2), (gW3, gb3))):
            dma_block((wa_sb[:, :, :], col_w(w)))
            node_phase(L + 2 + n, pre_conv if n else pre_h, post_conv, store=store_conv, st=L + n)
            dma_block((rows[:, 0, :], row_bcast(bb)))
            edge_pass(PLAIN, L + 3 + n)
        on_vector([
            lambda: nc.vector.tensor_tensor(agg, agg, whole(Y), ALU.add),
            lambda: nc.vector.tensor_tensor(agg, agg, dinv[:, :].unsqueeze(2).to_broadcast([P, NB, D]), ALU.mult),
            lambda: nc.vector.tensor_tensor(agg, agg, over(rows[:, 0, :]), ALU.add),
            lambda: nc.vector.tensor_tensor(agg, agg, whole(H), ALU.add),
        ])
        layer_norm()
        dma_block((out.rearrange("(b p) f -> p b f", p=P), whole(H)))


_INS = ["x", "src", "dst", "edge_attr_16", "edge_weight", "L0_gnn_vn_emb0", "L0_gnn_We", "L0_gnn_be", "L0_gnn_W1",
        "L0_gnn_b1", "L0_gnn_W2", "L0_gnn_b2", "L0_gnn_bn_g", "L0_gnn_bn_b", "L0_gnn_bn_m", "L0_gnn_bn_v",
        "L0_gnn_Wv1", "L0_gnn_bv1", "L0_gnn_vn_g", "L0_gnn_vn_b", "L0_gnn_vn_m", "L0_gnn_vn_v", "L0_gnn_Wv2",
        "L0_gnn_bv2", "L1_gnn_W_rel", "L1_gnn_b_rel", "L1_gnn_W_root", "L1_gnn_gamma", "L1_gnn_beta", "L2_gnn_W",
        "L2_gnn_att_src", "L2_gnn_att_dst", "L2_gnn_bias", "L3_gnn_W1", "L3_gnn_b1", "L3_gnn_W2", "L3_gnn_b2",
        "L3_gnn_W3", "L3_gnn_b3"]


def kernel(**inputs):
    import concourse.bacc as bacc
    from concourse.bass_utils import run_bass_kernel_spmd

    nc = bacc.Bacc("TRN2", target_bir_lowering=False, num_devices=1)
    arrays, args = {}, []
    for name in _INS:
        a = np.ascontiguousarray(inputs[name])
        arrays[f"in_{name}"] = a
        args.append(nc.dram_tensor(f"in_{name}", a.shape, mybir.dt.from_np(a.dtype), kind="ExternalInput").ap())
    args.append(nc.dram_tensor("out_dram", [N, D], F32, kind="ExternalOutput").ap())
    build(nc, *args)
    r = run_bass_kernel_spmd(nc, [arrays], core_ids=[0])
    return r.results[0]["out_dram"]
```

```python
import numpy as np
import concourse.bass as bass
from concourse import mybir
from contextlib import ExitStack

F32 = mybir.dt.float32
I32 = mybir.dt.int32
ALU = mybir.AluOpType
ACT = mybir.ActivationFunctionType
AX = mybir.AxisListType

P = 128
N = 4096
D = 256
E = 65536
FE = 16
L = 5
DH = 2 * D
HEADS = 8
C = D // HEADS
NB = N // P
NT = E // P
U = 8
NO = NT // U
OB = 4
NG = NO // OB
RING = OB * U
MT = P // 8
GR = RING // MT
PARTS = P // FE
GW = D + HEADS
AW = D + HEADS + 1
RW = AW + 3
EPS = 1e-5
BIG = 1e38

BF16 = mybir.dt.bfloat16
PLAIN, MESSAGE, WEIGHTED = range(3)


def build(nc, x, src, dst, edge_attr, edge_weight, vn_emb0, We, be, W1, b1, W2, b2, bn_g, bn_b, bn_m, bn_v,
          Wv1, bv1, vn_g, vn_b, vn_m, vn_v, Wv2, bv2, W_rel, b_rel, W_root, gamma, beta,
          gat_W, att_src, att_dst, gat_bias, gW1, gb1, gW2, gb2, gW3, gb3, out):
    ctx = ExitStack()
    with ctx:
        def sb(name, shape, dt=F32):
            return ctx.enter_context(nc.sbuf_tensor(name, shape, dt))

        def pb(name, shape):
            return ctx.enter_context(nc.psum_tensor(name, shape, F32))

        def sem(name):
            return ctx.enter_context(nc.semaphore(name))

        node_table = nc.dram_tensor("node_table", [N, D], F32, kind="Internal").ap()
        att_table = nc.dram_tensor("att_table", [N, GW], F32, kind="Internal").ap()
        score_table = nc.dram_tensor("score_table", [N, HEADS], F32, kind="Internal").ap()
        stack_table = nc.dram_tensor("stack_table", [NO * P, U * P], BF16, kind="Internal").ap()
        range_scratch = nc.dram_tensor("range_scratch", [NO, 2], I32, kind="Internal").ap()

        H = sb("H", [P, NB * D])
        AGG = sb("AGG", [P, NB * AW])
        Y = sb("Y", [P, NB * D])
        iota = sb("iota", [P, P])
        block_start = sb("block_start", [P, NB])
        iota_i = sb("iota_i", [P, P], I32)
        ring = sb("ring", [P, RING, RW])
        S = sb("S", [P, U, P])
        src_i = sb("src_i", [P, NT], I32)
        dst_i = sb("dst_i", [P, NT], I32)
        dst_f = sb("dst_f", [P, NT])
        weight = sb("weight", [P, NT])
        idx = sb("idx", [P, RING], I32)
        ident = sb("ident", [P, P])
        ident_b = sb("ident_b", [P, P], BF16)
        ones = sb("ones", [P, P])
        stk = sb("stk", [P, OB, U * P], BF16)
        we_rep = sb("we_rep", [P, D])
        we_stk = sb("we_stk", [P, D], BF16)
        wpart = sb("wpart", [P, 3])
        w1_sb = sb("w1_sb", [P, 2, DH])
        w2_sb = sb("w2_sb", [P, 4, D])
        wa_sb = sb("wa_sb", [P, 2, D])
        wb_sb = sb("wb_sb", [P, 2, D])
        b1_col = sb("b1_col", [P, 4])
        rows = sb("rows", [P, 5, D])
        bias_row = sb("bias_row", [P, D])
        scale_row = sb("scale_row", [P, D])
        be_row = sb("be_row", [P, D])
        vn = sb("vn", [P, D])
        tin = sb("tin", [P, 2, D])
        tT = sb("tT", [P, 2, 2 * P])
        tT2 = sb("tT2", [P, 2, 2 * P])
        hT = sb("hT", [P, 2, DH])
        tab = sb("tab", [P, 2, GW])
        small = sb("small", [P, 2 * NO])
        small2 = sb("small2", [P, 2 * NO])
        spans = sb("spans", [NO, 2])
        spans_i = sb("spans_i", [NO, 2], I32)
        span_row = sb("span_row", [1, 2 * NO], I32)
        unsorted_i = sb("unsorted_i", [1, 1], I32)
        stats = sb("stats", [P, NB, 6])
        mv = sb("mv", [P, NB, 2])
        rstd = sb("rstd", [P, NB])
        eps = sb("eps", [P, 1])
        a_src = sb("a_src", [P, NB, HEADS])
        a_dst = sb("a_dst", [P, NB, HEADS])
        a_max = sb("a_max", [P, NB, HEADS])
        ex_self = sb("ex_self", [P, NB, HEADS])
        dinv = sb("dinv", [P, NB])
        gs = sb("gs", [P, RING * HEADS])
        tgt = sb("tgt", [P, NB, 3 * 2 * HEADS], BF16)
        d16 = sb("d16", [P, P])
        stk_f = stk[:, :, :].rearrange("p o n -> p (o n)").bitcast(F32)
        GTp, DTp = stk_f[:, 0:2 * P], stk_f[:, 2 * P:5 * P]
        S_of = (S, stk_f[:, 0:U * P].rearrange("p (u e) -> p u e", u=U),
                w1_sb[:, :, :].rearrange("p a (b e) -> p (a b) e", e=P),
                w2_sb[:, :, :].rearrange("p a (b e) -> p (a b) e", e=P),
                hT[:, :, :].rearrange("p a (b e) -> p (a b) e", e=P))
        ST = stk_f[:, U * P:3 * U * P // 2].bitcast(BF16)
        run, last, pen = (stk_f[:, n * P:n * P + P] for n in (5, 6, 7))
        picks = sb("picks", [P, MT, HEADS + 1])
        al = sb("al", [P, U, HEADS])
        cand = sb("cand", [P, U, HEADS])
        cmax = sb("cmax", [P, HEADS])

        psE = pb("psE", [P, 4 * 512])
        psAT = pb("psAT", [P, 2 * 512])
        psA = psAT[:, 0:512]
        psT = psAT[:, 512:1024]
        psO = pb("psO", [P, 512])
        psV = pb("psV", [P, 512])

        gathered = [sem(f"gathered{q}") for q in range(RING)]
        idx_ready = sem("idx_ready")
        idx_seen = sem("idx_seen")
        octet_free = sem("octet_free")
        onehot_ready = sem("onehot_ready")
        onehot_used = sem("onehot_used")
        unit_added = sem("unit_added")
        stk_in = [sem(f"stk_in{n}") for n in range(OB)]
        encoded = sem("encoded")
        pre_added = sem("pre_added")
        message = sem("message")
        logits = sem("logits")
        exps = sem("exps")
        weighed = sem("weighed")
        d16_ready = sem("d16_ready")
        scoresT = sem("scoresT")
        runs_ready = sem("runs_ready")
        runsT = sem("runsT")
        picks_ready = sem("picks_ready")
        t_in = sem("t_in")
        t_done = sem("t_done")
        t_copied = sem("t_copied")
        hid_done = sem("hid_done")
        hid_relu = sem("hid_relu")
        o_done = sem("o_done")
        o_used = sem("o_used")
        tab_ready = sem("tab_ready")
        stored = [sem("stored0"), sem("stored1")]

        loads_seen = sem("loads_seen")

        a_made = sem("a_made")
        a_turned = sem("a_turned")
        a_copied = sem("a_copied")
        a_found = sem("a_found")
        octet_found = sem("octet_found")
        zeros_ready = sem("zeros_ready")
        b_made = sem("b_made")
        b_used = sem("b_used")
        b_added = sem("b_added")
        parts_seen = sem("parts_seen")

        nd = nc.vector.alloc_register("units_dve")
        npe = nc.tensor.alloc_register("units_pe")
        na_dve, nb_dve = (nc.vector.alloc_register(f"n{c}_dve") for c in "ab")
        na_pe, nb_pe, nx_pe = (nc.tensor.alloc_register(f"n{c}_pe") for c in "abx")
        na_act = nc.scalar.alloc_register("na_act")
        lo_dve = [nc.vector.alloc_register(f"lo{q}_dve") for q in range(OB)]
        cnt_dve = [nc.vector.alloc_register(f"cnt{q}_dve") for q in range(OB)]
        cnt_pe = [nc.tensor.alloc_register(f"cnt{q}_pe") for q in range(OB)]
        last_blk = nc.vector.alloc_register("last_block")

        def flat(ap):
            return ap.rearrange("p a b -> p (a b)")

        def copied(o, i):
            return nc.vector.tensor_scalar(o, i, 1.0, None, ALU.mult)

        def row_bcast(ap):
            return ap.partition_broadcast(P)

        def span_of(eng, h):
            v = eng.value_load(span_row[0:1, bass.ds(2 * h, 1)], min_val=NB, max_val=NB * NB + NB - 1)
            lo = nc.s_assert_within(v & (NB - 1), 0, NB - 1,
                                    skip_runtime_bounds_check_because="the low bits")
            cnt = nc.s_assert_within(v >> (NB.bit_length() - 1), 1, NB,
                                     skip_runtime_bounds_check_because="1 to NB blocks")
            return eng.snap(lo), eng.snap(cnt)

        def units(eng, lo, cnt, unit):
            unit(lo, True)
            with eng.If(cnt > 1):
                with eng.Fori(1, cnt) as j:
                    unit(nc.s_assert_within(lo + j, 0, NB - 1,
                                            skip_runtime_bounds_check_because="lo + cnt <= NB") if lo is not None
                         else None, False)

        def one_hots(dve, h, blk, c, g):
            dve.wait_ge(onehot_used, c + 4 * g + 4)
            nc.vector.scalar_tensor_tensor(
                S[:, 4 * g:4 * g + 4, :], iota[:, :].unsqueeze(1).to_broadcast([P, 4, P]),
                block_start[:, bass.ds(blk, 1)],
                dst_f[:, bass.ds(U * h + 4 * g, 4)].unsqueeze(2).to_broadcast([P, 4, P]), ALU.add, ALU.is_equal
            ).then_inc(onehot_ready, 4)

        def next_indices(act, k, i, ob):
            for q in range(U * ob, U * ob + U):
                act.wait_ge(gathered[q], 16 * (NG * k + i + 1))
            nc.scalar.copy(idx[:, U * ob:U * ob + U],
                           src_i[:, bass.ds(nc.s_assert_within(
                               (i + 1) & (NG - 1), 0, NG - 1,
                               skip_runtime_bounds_check_because="the low bits") * RING + U * ob, U)]
                           ).then_inc(idx_ready, 1)

        def gather_rows(pool, k, table, gw):
            with pool.Fori(0, NG) as i:
                for ob in range(OB):
                    pool.wait_ge(octet_free, NO * k + OB * i + 1 + ob)
                    pool.wait_ge(idx_ready, NO * k + OB * i + ob + 1)
                    pool.sem_inc(idx_seen, 1)
                    for q in range(U * ob, U * ob + U):
                        nc.gpsimd.indirect_dma_start(
                            ring[:, q, 0:gw], None, table,
                            bass.IndirectOffsetOnAxis(ap=idx[:, q:q + 1], axis=0)).then_inc(gathered[q], 16)

        def edge_pass(kind, k, l=0, loads=None, first_work=None, first_dve=None):
            with nc.Block() as block:
                @block.sync
                def _(sp):
                    seen = loads(sp) if loads else None
                    if kind == MESSAGE:
                        with sp.Fori(0, NG) as i:
                            for ob in range(OB):
                                o = NO * l + OB * i + ob
                                sp.wait_ge(encoded, U * (o + 1))
                                sp.dma_start(stk[:, ob, :], stack_table[bass.ds((OB * i + ob) * P, P), :]
                                             ).then_inc(stk_in[ob], 16)
                    if seen:
                        seen(sp)

                @block.gpsimd
                def _(pool):
                    gather_rows(pool, k, node_table, D)

                @block.tensor
                def _(pe):
                    if first_work:
                        first_work[0](pe)
                    def encode(i, ob):
                        o = NO * l + OB * i + ob
                        pe.wait_ge(stk_in[ob], 16 * (NG * l + i + 1))
                        for u in range(U):
                            if u % 2 == 0:
                                pe.wait_ge(pre_added, U * o + u + 2)
                            nc.tensor.matmul(psE[:, D * u:D * u + D], stk[:, ob, P * u:P * u + P],
                                             we_stk[:, :], start=True, stop=True).then_inc(encoded, 1)

                    if kind == MESSAGE:
                        encode(0, 0)
                    with pe.Fori(0, NG) as i:
                        for ob in range(OB):
                            h = OB * i + ob
                            if kind == MESSAGE:
                                if ob < OB - 1:
                                    encode(i, ob + 1)
                                else:
                                    with pe.If(i < NG - 1):
                                        encode(i + 1, 0)
                            cnt = pe.value_load(span_row[0:1, bass.ds(2 * h + 1, 1)], min_val=1, max_val=NB)

                            def unit(_, first):
                                c = pe.snap(npe)
                                pe.wait_ge(unit_added, c + 2 * U)
                                for u in range(U):
                                    q = U * ob + u
                                    if first:
                                        if kind in (MESSAGE, WEIGHTED):
                                            pe.wait_ge(message, NT * k + U * h + u + 1)
                                        else:
                                            pe.wait_ge(gathered[q], 16 * (NG * k + i + 1))
                                    if u % 4 == 0:
                                        pe.wait_ge(onehot_ready, c + u + 4)
                                    nc.tensor.matmul(psA[:, 0:D], S[:, u, :], ring[:, q, 0:D],
                                                     start=(u == 0), stop=(u == U - 1)).then_inc(onehot_used, 1)
                                pe.reg_add(npe, npe, U)

                            units(pe, None, cnt, unit)
                            pe.drain().then_inc(octet_free, 1)

                @block.scalar
                def _(act):
                    if first_work:
                        first_work[1](act)
                    with act.Fori(0, NG) as i:
                        for ob in range(OB):
                            for q in range(U * ob, U * ob + U):
                                if kind == MESSAGE:
                                    act.wait_ge(pre_added, NT * l + RING * i + q + U + 1)
                                    nc.scalar.activation(ring[:, q, 0:D], ring[:, q, 0:D], ACT.Relu
                                                         ).then_inc(message, 1)
                                if kind == WEIGHTED:
                                    act.wait_ge(gathered[q], 16 * (NG * k + i + 1))
                                    nc.scalar.activation(ring[:, q, 0:D], ring[:, q, 0:D], ACT.Copy,
                                                         scale=weight[:, bass.ds(RING * i + q, 1)]
                                                         ).then_inc(message, 1)
                            next_indices(act, k, i, ob)

                @block.vector
                def _(dve):
                    nc.vector.memset(AGG[:, :], 0.0)
                    nc.vector.memset(psA[:, 0:D], 0.0)
                    dve.reg_mov(last_blk, 0)
                    dve.drain()
                    if first_work:
                        first_work[2](dve)
                    if first_dve:
                        first_dve(dve)

                    def add_sums():
                        b = nc.s_assert_within(dve.snap(last_blk), 0, NB - 1,
                                               skip_runtime_bounds_check_because="a unit's block")
                        a = AGG[:, bass.ds(b * AW, D)]
                        return nc.vector.tensor_tensor(a, a, psA[:, 0:D], ALU.add)

                    with dve.Fori(0, NG) as i:
                        for ob in range(OB):
                            h = OB * i + ob
                            o = NO * l + h
                            lo, cnt = span_of(dve, h)

                            def messages():
                                for u in range(U):
                                    q = U * ob + u
                                    dve.wait_ge(gathered[q], 16 * (NG * k + i + 1))
                                    if u % 2 == 0:
                                        dve.wait_ge(encoded, U * o + u + 2 + OB * U)
                                    nc.vector.tensor_tensor(ring[:, q, 0:D], ring[:, q, 0:D],
                                                            psE[:, D * u:D * u + D], ALU.add).then_inc(pre_added, 1)

                            def unit(blk, first):
                                c = dve.snap(nd)
                                if first and kind == MESSAGE:
                                    messages()
                                one_hots(dve, h, blk, c, 0)
                                dve.wait_ge(onehot_used, c + U)
                                dve.wait_ge(unit_added, c + U)
                                add_sums().then_inc(unit_added, U)
                                one_hots(dve, h, blk, c, 1)
                                dve.reg_mov(last_blk, blk)
                                dve.reg_add(nd, nd, U)

                            units(dve, lo, cnt, unit)
                    c = dve.snap(nd)
                    dve.wait_ge(onehot_used, c + U)
                    dve.wait_ge(unit_added, c + U)
                    add_sums()

        def max_pass(k):
            with nc.Block() as block:
                @block.gpsimd
                def _(pool):
                    with pool.Fori(0, NG) as i:
                        for g in range(GR):
                            pool.wait_ge(scoresT, GR * i + g + 1)
                            pool.wait_ge(idx_ready, NO * k + OB * i + OB // GR * (g + 1))
                            pool.sem_inc(idx_seen, 1)
                            for q in range(MT * g, MT * g + MT):
                                nc.gpsimd.indirect_dma_start(
                                    gs[:, HEADS * q:HEADS * q + HEADS], None, score_table,
                                    bass.IndirectOffsetOnAxis(ap=idx[:, q:q + 1], axis=0)).then_inc(gathered[q], 16)

                @block.tensor
                def _(pe):
                    with pe.Fori(0, NG) as i:
                        for g in range(GR):
                            n = GR * i + g
                            for q in range(MT * g, MT * g + MT):
                                pe.wait_ge(gathered[q], 16 * (NG * k + i + 1))
                            pe.wait_ge(d16_ready, n + 1)
                            nc.tensor.transpose(psE[:, 0:P], gs[:, P * g:P * g + P], ident[:, :])
                            nc.tensor.transpose(psE[:, 512:512 + P], d16[:, :], ident[:, :]).then_inc(scoresT, 1)
                            pe.wait_ge(runs_ready, n + 1)
                            nc.tensor.transpose(psE[:, 1024:1024 + P], run[:, :], ident[:, :])
                            nc.tensor.transpose(psE[:, 1536:1536 + P], last[:, :], ident[:, :]).then_inc(runsT, 1)
                            pe.wait_ge(picks_ready, n + 1)
                            for half in range(2):
                                cnt = pe.value_load(span_row[0:1, bass.ds(2 * (2 * n + half) + 1, 1)],
                                                    min_val=1, max_val=NB)

                                def unit(_, first):
                                    c = pe.snap(npe)
                                    pe.wait_ge(unit_added, c + 2 * U)
                                    for u in range(U):
                                        if u % 4 == 0:
                                            pe.wait_ge(onehot_ready, c + u + 4)
                                        nc.tensor.matmul(psA[:, (HEADS + 1) * u:(HEADS + 1) * (u + 1)], S[:, u, :],
                                                         picks[:, U * half + u, :], start=True, stop=True
                                                         ).then_inc(onehot_used, 1)
                                    pe.reg_add(npe, npe, U)

                                units(pe, None, cnt, unit)
                                pe.drain().then_inc(octet_free, 1)

                @block.scalar
                def _(act):
                    with act.Fori(0, NG) as i:
                        for ob in range(OB):
                            next_indices(act, k, i, ob)

                @block.vector
                def _(dve):
                    nc.vector.memset(DTp[:, 0:P], -1.0)
                    nc.vector.memset(DTp[:, 2 * P:3 * P], -2.0)
                    nc.vector.memset(GTp[:, 0:P], 0.0)
                    nc.vector.memset(psA[:, 0:(HEADS + 1) * U], 0.0)
                    dve.reg_mov(last_blk, 0)
                    nc.vector.tensor_copy(a_max[:, :, :], a_src[:, :, :])
                    dve.drain()
                    uns = dve.value_load(unsorted_i[0:1, 0:1], min_val=0, max_val=1)
                    am = flat(a_max[:, :, :])
                    GT, DT = GTp[:, P:2 * P], DTp[:, P:2 * P]

                    def merge_last(c, signal=True):
                        dve.wait_ge(onehot_used, c + U)
                        pv = psA[:, 0:(HEADS + 1) * U].rearrange("p (u h) -> p u h", u=U)
                        nc.vector.tensor_scalar(cand[:, :, :], pv[:, :, HEADS:HEADS + 1].to_broadcast(
                            [P, U, HEADS]), 1.0, BIG, ALU.subtract, ALU.mult)
                        dve.drain()
                        ins = nc.vector.tensor_tensor(cand[:, :, :], cand[:, :, :], pv[:, :, 0:HEADS], ALU.add)
                        if signal:
                            ins.then_inc(unit_added, U)
                        dve.drain()
                        nc.vector.tensor_reduce(cmax[:, :], cand[:, :, :].rearrange("p u h -> p h u"),
                                                AX.X, ALU.max)
                        dve.drain()
                        a = am[:, bass.ds(nc.s_assert_within(
                            dve.snap(last_blk), 0, NB - 1,
                            skip_runtime_bounds_check_because="a unit's block") * HEADS, HEADS)]
                        nc.vector.tensor_tensor(a, a, cmax[:, :], ALU.max)
                        dve.drain()

                    with dve.Fori(0, 2 * NG if GR == 2 else NG) as n:
                        dve.wait_ge(scoresT, n + 2)
                        copied(d16[:, :].rearrange("p (q h) -> p q h", h=HEADS),
                               dst_f[:, bass.ds(MT * n, MT)].unsqueeze(2).to_broadcast([P, MT, HEADS])
                               ).then_inc(d16_ready, 1)
                        dve.wait_ge(scoresT, n + 3)
                        nc.vector.tensor_copy(GT, psE[:, 0:P])
                        nc.vector.tensor_copy(DT, psE[:, 512:512 + P])
                        dve.drain()
                        with dve.If(uns > 0):
                            nc.vector.tensor_copy(run[:, :], GT)
                            nc.vector.memset(last[:, :], 1.0)
                            dve.drain()
                            with dve.Fori(1, P) as s:
                                nc.vector.tensor_tensor(pen[:, :], DT, DTp[:, bass.ds(P - s, P)], ALU.is_equal)
                                dve.drain()
                                nc.vector.tensor_scalar(pen[:, :], pen[:, :], 1.0, BIG, ALU.subtract, ALU.mult)
                                dve.drain()
                                nc.vector.tensor_tensor(pen[:, :], pen[:, :], GTp[:, bass.ds(P - s, P)], ALU.add)
                                dve.drain()
                                nc.vector.tensor_tensor(run[:, :], run[:, :], pen[:, :], ALU.max)
                                dve.drain()
                                nc.vector.tensor_tensor(pen[:, :], DT, DTp[:, bass.ds(s + P, P)], ALU.not_equal)
                                dve.drain()
                                nc.vector.tensor_tensor(last[:, :], last[:, :], pen[:, :], ALU.mult)
                                dve.drain()
                        with dve.Else():
                            nc.vector.tensor_tensor(pen[:, :], DT, DTp[:, P - 1:2 * P - 1], ALU.not_equal)
                            nc.vector.tensor_tensor(last[:, :], DT, DTp[:, P + 1:2 * P + 1], ALU.not_equal)
                            dve.drain()
                            nc.vector.tensor_scalar(pen[:, :], pen[:, :], -BIG, None, ALU.mult)
                            dve.drain()
                            nc.vector.tensor_tensor_scan(run[:, :], pen[:, :], GT, -BIG, ALU.add, ALU.max)
                            dve.drain()
                        nc.vector.tensor_tensor(run[:, :], run[:, :], last[:, :], ALU.mult).then_inc(runs_ready, 1)
                        dve.wait_ge(runsT, n + 1)
                        dve.wait_ge(onehot_used, dve.snap(nd) + U)
                        nc.vector.tensor_copy(picks[:, :, 0:HEADS],
                                              psE[:, 1024:1024 + P].rearrange("p (q h) -> p q h", h=HEADS))
                        nc.vector.tensor_copy(picks[:, :, HEADS:HEADS + 1],
                                              psE[:, 1536:1536 + P].rearrange("p (q h) -> p q h", h=HEADS)[:, :, 0:1]
                                              ).then_inc(picks_ready, 1)
                        for half in range(2):
                            h = 2 * n + half
                            lo, cnt = span_of(dve, h)

                            def unit(blk, first):
                                c = dve.snap(nd)
                                one_hots(dve, h, blk, c, 0)
                                merge_last(c)
                                one_hots(dve, h, blk, c, 1)
                                dve.reg_mov(last_blk, blk)
                                dve.reg_add(nd, nd, U)

                            units(dve, lo, cnt, unit)
                    merge_last(dve.snap(nd), signal=False)

        def attend_pass(k, loads):
            W = 3 * 2 * HEADS
            found = small[:, 0:U * 2 * HEADS].rearrange("p (u h) -> p u h", u=U)
            zeros = stk_f[:, 3 * U * P // 2:2 * U * P].bitcast(BF16)[:, 0:U * W]
            turnedS = [psE[:, 512 * g:512 * g + 256].bitcast(BF16) for g in range(2)]

            def high(ap):
                halves = ap.bitcast(BF16).rearrange("p (e two) -> p e two", two=2)
                return halves[:, :, 1:2].rearrange("p e o -> p (e o)")

            def sums_bank(eng, c):
                start = nc.s_assert_within((c & U) * (512 // U), 0, 512,
                                           skip_runtime_bounds_check_because="0 or 512")
                return psAT[:, bass.ds(eng.snap(start), AW)]

            def in_range(b):
                return nc.s_assert_within(b, 0, NB - 1, skip_runtime_bounds_check_because="a block of the octet")

            def ahead(eng, i, ob, by, work):
                if ob < OB - by:
                    work(i, ob + by)
                else:
                    with eng.If(i < NG - 1):
                        work(nc.s_assert_within(i + 1, 0, NG - 1, skip_runtime_bounds_check_because="i < NG - 1"),
                             ob + by - OB)

            def one_hot(dve, q, h, b, g):
                return nc.vector.scalar_tensor_tensor(
                    S_of[q][:, 4 * g:4 * g + 4, :], iota[:, :].unsqueeze(1).to_broadcast([P, 4, P]),
                    block_start[:, bass.ds(b, 1)],
                    dst_f[:, bass.ds(U * h + 4 * g, 4)].unsqueeze(2).to_broadcast([P, 4, P]), ALU.add, ALU.is_equal)

            with nc.Block() as block:
                @block.sync
                def _(sp):
                    loads(sp)

                @block.gpsimd
                def _(pool):
                    gather_rows(pool, k, att_table, GW)

                @block.tensor
                def _(pe):
                    pe.reg_mov(na_pe, 0)
                    pe.reg_mov(nb_pe, 0)
                    pe.reg_mov(nx_pe, 0)

                    def turn(ob, c):
                        for g in range(2):
                            pe.wait_ge(a_made, c + 4 * g + 4)
                            pe.wait_ge(a_copied, c + 4 * g + 4)
                            for u in range(4 * g, 4 * g + 4):
                                ins = nc.tensor.transpose(turnedS[g][:, P * (u % 4):P * (u % 4) + P],
                                                          high(S_of[ob][:, u, :]), ident_b[:, :])
                            ins.then_inc(a_turned, 4)

                    def turn_first(i, ob):
                        turn(ob, pe.snap(na_pe))

                    def find(b, c):
                        for g in range(2):
                            pe.wait_ge(a_copied, c + U + 4 * g + 4)
                            for u in range(4 * g, 4 * g + 4):
                                ins = nc.tensor.matmul(psO[:, W * u:W * (u + 1)], ST[:, P * u:P * u + P],
                                                       flat(tgt[:, :, :])[:, bass.ds(b * W, W)],
                                                       start=False, stop=False)
                            ins.then_inc(a_found, 4)
                        pe.reg_add(na_pe, na_pe, U)

                    def find_all(i, ob):
                        h = OB * i + ob
                        lo, cnt = span_of(pe, h)
                        pe.reg_mov(cnt_pe[ob], cnt)
                        if not (isinstance(h, int) and h == 0):
                            pe.wait_ge(logits, h)
                        nc.tensor.matmul(psO[:, 0:U * W], zeros[:, 0:P], zeros, start=True, stop=False)
                        find(lo, pe.snap(na_pe))
                        with pe.If(cnt > 1):
                            with pe.Fori(1, cnt) as j:
                                c = pe.snap(na_pe)
                                turn(ob, c)
                                find(in_range(lo + j), c)
                        nc.tensor.matmul(psO[:, 0:U * W], zeros[:, 0:P], zeros, start=False, stop=True
                                         ).then_inc(octet_found, 1)

                    pe.wait_ge(zeros_ready, 1)
                    for ob in range(2):
                        turn_first(0, ob)
                        find_all(0, ob)
                    with pe.Fori(0, NG) as i:
                        for ob in range(OB):
                            h = OB * i + ob

                            def sums(c, first, u0, u1):
                                bank = sums_bank(pe, c)
                                for u in range(u0, u1):
                                    if first:
                                        pe.wait_ge(weighed, U * h + u + 1)
                                    elif u % 4 == 0:
                                        pe.wait_ge(b_made, pe.snap(nx_pe) + u + 4)
                                    nc.tensor.matmul(bank, S_of[ob if first else OB][:, u, :],
                                                     ring[:, U * ob + u, 0:AW],
                                                     start=(u == 0), stop=(u == U - 1)).then_inc(b_used, 1)

                            c = pe.snap(nb_pe)
                            pe.wait_ge(b_added, c + U)
                            sums(c, True, 0, U - 2)
                            ahead(pe, i, ob, 2, turn_first)
                            sums(c, True, U - 2, U)
                            pe.reg_add(nb_pe, nb_pe, U)
                            cnt = pe.snap(cnt_pe[ob])
                            with pe.If(cnt > 1):
                                with pe.Fori(1, cnt):
                                    c = pe.snap(nb_pe)
                                    pe.wait_ge(b_added, c + U)
                                    sums(c, False, 0, U)
                                    pe.reg_add(nx_pe, nx_pe, U)
                                    pe.reg_add(nb_pe, nb_pe, U)
                            pe.drain().then_inc(octet_free, 1)
                            ahead(pe, i, ob, 2, find_all)

                @block.scalar
                def _(act):
                    act.reg_mov(na_act, 0)

                    def look_up(i, ob):
                        h = OB * i + ob
                        cnt = act.value_load(span_row[0:1, bass.ds(2 * h + 1, 1)], min_val=1, max_val=NB)

                        def unit(_, first):
                            c = act.snap(na_act)
                            for g in range(2):
                                act.wait_ge(a_turned, c + U + 4 * g + 4)
                                act.wait_ge(a_found, c + 4 * g + 4)
                                nc.scalar.copy(ST[:, 512 * g:512 * g + 512], turnedS[g]).then_inc(a_copied, 4)
                            act.reg_add(na_act, na_act, U)

                        units(act, None, cnt, unit)

                    def exp(i, ob):
                        act.wait_ge(logits, OB * i + ob + 1)
                        nc.scalar.activation(ring[:, U * ob:U * ob + U, D:GW], al[:, :, :], ACT.Exp).then_inc(exps, 1)

                    look_up(0, 0)
                    exp(0, 0)
                    look_up(0, 1)
                    with act.Fori(0, NG) as i:
                        for ob in range(OB):
                            ahead(act, i, ob, 1, exp)
                            ahead(act, i, ob, 2, look_up)
                            next_indices(act, k, i, ob)

                @block.vector
                def _(dve):
                    nc.vector.memset(zeros, 0.0).then_inc(zeros_ready, 1)
                    nc.vector.memset(AGG[:, :], 0.0)
                    nc.vector.memset(psT[:, 0:AW], 0.0)
                    dve.reg_mov(last_blk, 0)
                    dve.reg_mov(na_dve, 0)
                    dve.reg_mov(nb_dve, 0)
                    dve.drain()

                    def add_sums():
                        c = dve.snap(nb_dve)
                        dve.wait_ge(b_used, c + 2 * U)
                        dve.wait_ge(b_added, c + U)
                        a = AGG[:, bass.ds(in_range(dve.snap(last_blk)) * AW, AW)]
                        nc.vector.tensor_tensor(a, a, sums_bank(dve, c + U), ALU.add).then_inc(b_added, U)

                    def look_up(ob, h, b, first):
                        c = dve.snap(na_dve)
                        for g in range(2):
                            if first:
                                dve.wait_ge(b_used, dve.snap(nb_dve) + U)
                            dve.wait_ge(a_turned, c + 4 * g + 4)
                            one_hot(dve, ob, h, b, g).then_inc(a_made, 4)
                        dve.reg_add(na_dve, na_dve, U)

                    def look_up_first(i, ob):
                        lo, cnt = span_of(dve, OB * i + ob)
                        dve.reg_mov(lo_dve[ob], lo)
                        dve.reg_mov(cnt_dve[ob], cnt)
                        look_up(ob, OB * i + ob, lo, True)

                    def look_up_rest(i, ob):
                        lo, cnt = dve.snap(lo_dve[ob]), dve.snap(cnt_dve[ob])
                        with dve.If(cnt > 1):
                            with dve.Fori(1, cnt) as j:
                                look_up(ob, OB * i + ob, in_range(lo + j), False)

                    def exponents(i, ob):
                        h = OB * i + ob
                        r = slice(U * ob, U * ob + U)
                        for q in range(U * ob, U * ob + U):
                            dve.wait_ge(gathered[q], 16 * (NG * k + i + 1))
                        dve.wait_ge(octet_found, h + 1)
                        nc.vector.tensor_reduce(found, psO[:, 0:U * W].rearrange("p (u s h) -> p u h s", u=U, s=3),
                                                AX.X, ALU.add)
                        dve.drain()
                        nc.vector.tensor_tensor(al[:, :, :], ring[:, r, D:GW], found[:, :, 0:HEADS], ALU.add)
                        dve.drain()
                        nc.vector.scalar_tensor_tensor(al[:, :, :], al[:, :, :], 0.2, al[:, :, :],
                                                       ALU.mult, ALU.max)
                        dve.drain()
                        nc.vector.tensor_tensor(al[:, :, :], al[:, :, :], found[:, :, HEADS:2 * HEADS],
                                                ALU.subtract).then_inc(logits, 1)

                    look_up_first(0, 0)
                    look_up_rest(0, 0)
                    exponents(0, 0)
                    look_up_first(0, 1)
                    look_up_rest(0, 1)
                    with dve.Fori(0, NG) as i:
                        for ob in range(OB):
                            h = OB * i + ob
                            dve.wait_ge(exps, h + 1)
                            for u in range(U):
                                q = U * ob + u
                                hv = ring[:, q, 0:D].rearrange("p (h c) -> p h c", h=HEADS)
                                nc.vector.tensor_tensor(
                                    hv, hv, ring[:, q, D:GW].unsqueeze(2).to_broadcast([P, HEADS, C]),
                                    ALU.mult).then_inc(weighed, 1)
                            add_sums()
                            ahead(dve, i, ob, 2, look_up_first)
                            ahead(dve, i, ob, 1, exponents)
                            cnt = dve.snap(cnt_dve[ob])
                            hi = dve.snap(in_range(dve.snap(lo_dve[ob]) + cnt - 1))
                            dve.reg_mov(last_blk, hi)
                            dve.reg_add(nb_dve, nb_dve, U)

                            def again(j, second):
                                b = in_range(hi - j)
                                for g in range(2):
                                    dve.wait_ge(b_used, dve.snap(nb_dve) + U + (0 if second else 4 * g + 4))
                                    one_hot(dve, OB, h, b, g).then_inc(b_made, 4)
                                add_sums()
                                dve.reg_mov(last_blk, b)
                                dve.reg_add(nb_dve, nb_dve, U)

                            with dve.If(cnt > 1):
                                again(1, True)
                                with dve.If(cnt > 2):
                                    with dve.Fori(2, cnt) as j:
                                        again(j, False)
                            ahead(dve, i, ob, 2, look_up_rest)
                    add_sums()

        def staged(eng, *stages):
            ramp = max(2, (len(stages) + 1) // 2 * 2)
            for b in range(ramp):
                for s, stage in enumerate(stages):
                    if b >= s:
                        stage(b - s, (b - s) % 2, (b - s) // 2)
            with eng.Fori(ramp // 2, NB // 2) as j:
                for q in range(2):
                    for s, stage in enumerate(stages):
                        stage(2 * j + (q - s), (q - s) % 2, j + (q - s) // 2)
            for b in range(NB, NB + ramp):
                for s, stage in enumerate(stages):
                    if b - s < NB:
                        stage(b - s, (b - s) % 2, (b - s) // 2)

        turned = (psT, psV)

        def result_of(q):
            return psE[:, 512 * (2 + q):512 * (2 + q) + D]

        def node_phase(m, pre, post, hidden=False, second=False, store=None, st=0, pool_post=None,
                       loads=None, weights=wa_sb):
            def ready(b):
                return NB * m + b + 3

            def free(b):
                return NB * m + b + 1

            def rest(b, q, hb):
                pass

            with nc.Block() as block:
                @block.sync
                def _(sp):
                    if loads:
                        loads(sp)

                    def put(b, q, hb):
                        sp.wait_ge(tab_ready, NB * st + b + 1)
                        store(sp, b, q).then_inc(stored[q], 16)

                    if store:
                        staged(sp, put)
                        for q in range(2):
                            sp.wait_ge(stored[q], 16 * ((NB // 2) * (st + 1) + 1))
                        sp.sem_inc(loads_seen, 1)

                @block.gpsimd
                def _(pool):
                    def add(b, q, hb):
                        pool.wait_ge(o_used, ready(b))
                        pool.wait_ge(stored[q], 16 * ((NB // 2) * st + hb + 1))
                        pool_post(pool, b, q).then_inc(tab_ready, 1)

                    if pool_post:
                        staged(pool, add)

                @block.vector
                def _(dve):
                    def before(b, q, hb):
                        dve.wait_ge(t_done, free(b))
                        pre(dve, b, q).then_inc(t_in, 1)

                    def after(b, q, hb):
                        dve.wait_ge(o_done, ready(b))
                        if store and not pool_post:
                            dve.wait_ge(stored[q], 16 * ((NB // 2) * st + hb + 1))
                        post(dve, b, q).then_inc(o_used, 1)
                        if store and not pool_post:
                            dve.drain().then_inc(tab_ready, 1)

                    if hidden:
                        staged(dve, before, rest, rest, after)
                    else:
                        staged(dve, before, rest, after)

                @block.tensor
                def _(pe):
                    def turn(b, q, hb):
                        pe.wait_ge(t_in, ready(b))
                        pe.wait_ge(t_copied, free(b))
                        for f in range(2):
                            ins = nc.tensor.transpose(turned[q][:, P * f:P * f + P],
                                                      tin[:, q, P * f:P * f + P], ident[:, :])
                        if second:
                            for f in range(2):
                                ins = nc.tensor.transpose(turned[q][:, D + P * f:D + P * f + P],
                                                          tin2[:, q, P * f:P * f + P], ident[:, :])
                        ins.then_inc(t_done, 1)

                    def hid(b, q, hb):
                        pe.wait_ge(t_copied, ready(b))
                        pe.wait_ge(hid_relu, free(b))
                        for j in range(4):
                            for f in range(2):
                                ins = nc.tensor.matmul(psE[:, 512 * q + P * j:512 * q + P * j + P],
                                                       w1_sb[:, f, P * j:P * j + P], tT[:, q, P * f:P * f + P],
                                                       start=(f == 0), stop=(f == 1))
                        ins.then_inc(hid_done, 1)

                    def result(b, q, hb):
                        pe.wait_ge(hid_relu if hidden else t_copied, ready(b))
                        pe.wait_ge(o_used, free(b))
                        terms = ([(hT[:, q, P * j:P * j + P], w2_sb[:, j, :]) for j in range(4)] if hidden else
                                 [(tT[:, q, P * f:P * f + P], weights[:, f, :]) for f in range(2)])
                        if second:
                            terms += [(tT2[:, q, P * f:P * f + P], wb_sb[:, f, :]) for f in range(2)]
                        for n, (a, w) in enumerate(terms):
                            ins = nc.tensor.matmul(result_of(q), a, w,
                                                   start=(n == 0), stop=(n == len(terms) - 1))
                        ins.then_inc(o_done, 1)

                    if hidden:
                        staged(pe, turn, hid, result)
                    else:
                        staged(pe, turn, result)
                        pe.sem_inc(hid_done, NB)

                @block.scalar
                def _(act):
                    def copy(b, q, hb):
                        act.wait_ge(t_done, ready(b))
                        act.wait_ge(hid_done if hidden else o_done, free(b))
                        ins = nc.scalar.copy(tT[:, q, :], turned[q][:, 0:D])
                        if second:
                            ins = nc.scalar.copy(tT2[:, q, :], turned[q][:, D:2 * D])
                        ins.then_inc(t_copied, 1)

                    def relu(b, q, hb):
                        act.wait_ge(hid_done, ready(b))
                        act.wait_ge(o_done, free(b))
                        for j in range(4):
                            ins = nc.scalar.activation(hT[:, q, P * j:P * j + P],
                                                       psE[:, 512 * q + P * j:512 * q + P * j + P],
                                                       ACT.Relu, bias=b1_col[:, j:j + 1])
                        ins.then_inc(hid_relu, 1)

                    if hidden:
                        staged(act, copy, relu)
                    else:
                        staged(act, copy)

        def on_vector(steps):
            with nc.Block() as block:
                @block.vector
                def _(dve):
                    for step in steps:
                        step()
                        dve.drain()

        def on_scalar(steps):
            with nc.Block() as block:
                @block.scalar
                def _(act):
                    for step in steps:
                        step()
                        act.drain()

        def on_tensor(steps):
            with nc.Block() as block:
                @block.tensor
                def _(pe):
                    for step in steps:
                        step()

        def blk(t, b, w=D, pitch=D):
            return t[:, bass.ds(b * pitch, w)] if not isinstance(b, int) else t[:, b * pitch:b * pitch + w]

        def whole(t, w=D, pitch=D):
            return t[:, 0:NB * pitch].rearrange("p (b f) -> p b f", f=pitch)[:, :, 0:w]

        def over(row, nb=NB):
            return row.unsqueeze(1).to_broadcast([P, nb, D])

        def dma_block(*copies):
            with nc.Block() as block:
                @block.sync
                def _(sp):
                    copy_in(sp, block_copied, block_count, *copies)

        block_copied = sem("block_copied")
        block_count = [0]

        def copy_in(sp, s, count, *copies):
            for o, i in copies:
                sp.dma_start(o, i).then_inc(s, 16)
            count[0] += 16 * len(copies)
            sp.wait_ge(s, count[0])

        node_view = node_table.rearrange("(b p) f -> p b f", p=P)

        dma_block((src_i[:, :].rearrange("p (h u) -> p h u", u=U), src.rearrange("(h p u) -> p h u", p=P, u=U)),
                  (dst_i[:, :].rearrange("p (h u) -> p h u", u=U), dst.rearrange("(h p u) -> p h u", p=P, u=U)),
                  (weight[:, :].rearrange("p (h u) -> p h u", u=U),
                   edge_weight.rearrange("(h p u) -> p h u", p=P, u=U)),
                  (vn[:, :], row_bcast(vn_emb0)), (be_row[:, :], row_bcast(be[0])))
        x_in, features_in = sem("x_in"), sem("features_in")
        with nc.Block() as block:
            @block.sync
            def _(sp):
                sp.dma_start(AGG[:, 0:NO * P].rearrange("p (h v) -> p h v", v=P),
                             edge_attr.rearrange("(h p u) f -> p h (u f)", p=P, u=U)).then_inc(features_in, 16)
                sp.dma_start(whole(H), x.rearrange("(b p) f -> p b f", p=P)).then_inc(x_in, 16)
        iota_t = Y[:, 0:P].bitcast(I32)
        start_t = Y[:, P:P + NB].bitcast(I32)
        with nc.Block() as block:
            @block.gpsimd
            def _(pool):
                nc.gpsimd.iota(iota_t, pattern=[[1, P]], base=0, channel_multiplier=0)
                nc.gpsimd.iota(start_t, pattern=[[P, NB]], base=0, channel_multiplier=0)
                nc.gpsimd.iota(iota_i[:, :], pattern=[[1, P]], base=0, channel_multiplier=-1)

            @block.tensor
            def _(pe):
                pe.reg_mov(npe, 0)
                pe.sem_inc(octet_free, OB)
                pe.sem_inc(onehot_used, U)
                pe.sem_inc(encoded, OB * U)
                pe.sem_inc(unit_added, U)
                pe.sem_inc(pre_added, U)
                pe.sem_inc(scoresT, GR)
                for s in (a_turned, a_copied, a_found, b_used, b_used, b_added):
                    pe.sem_inc(s, U)
                pe.sem_inc(stored[0], 16)
                pe.sem_inc(stored[1], 16)
                for s in (t_in, t_done, t_copied, hid_done, hid_relu, o_done, o_used):
                    pe.sem_inc(s, 2)

            @block.vector
            def _(dve):
                dve.reg_mov(nd, 0)
                nc.vector.memset(ones[:, :], 1.0)
                nc.vector.memset(eps[:, :], EPS)
                nc.vector.memset(ring[:, :, AW - 1:AW], 1.0)
                nc.vector.tensor_copy(dst_f[:, :], dst_i[:, :])
                nc.vector.tensor_copy(idx[:, :], src_i[:, 0:RING]).then_inc(idx_ready, OB)
        blk_t = Y[:, N:N + NT].bitcast(I32)
        on_vector([
            lambda: nc.vector.tensor_copy(iota[:, :], iota_t),
            lambda: nc.vector.tensor_copy(block_start[:, :], start_t),
            lambda: nc.vector.tensor_scalar(ident[:, :], iota_i[:, :], 0.0, None, ALU.is_equal),
            lambda: nc.vector.tensor_scalar(blk_t, dst_i[:, :], P.bit_length() - 1, None, ALU.arith_shift_right),
            lambda: nc.vector.tensor_reduce(small[:, 0:NO], blk_t.rearrange("p (h u) -> p h u", u=U), AX.X, ALU.min),
            lambda: nc.vector.tensor_reduce(small[:, NO:2 * NO], blk_t.rearrange("p (h u) -> p h u", u=U),
                                            AX.X, ALU.max),
        ])
        on_tensor([lambda: nc.tensor.transpose(psT[0:NO, 0:P], small[:, 0:NO], ident[:, :]),
                   lambda: nc.tensor.transpose(psT[0:NO, P:2 * P], small[:, NO:2 * NO], ident[:, :])] +
                  [(lambda c=c: nc.tensor.transpose(psE[:, P * c:P * c + P], dst_f[:, P * c:P * c + P], ident[:, :]))
                   for c in range(NT // P)])
        on_vector([
            lambda: nc.vector.tensor_reduce(spans[:, 0:1], psT[0:NO, 0:P], AX.X, ALU.min),
            lambda: nc.vector.tensor_reduce(spans[:, 1:2], psT[0:NO, P:2 * P], AX.X, ALU.max),
            lambda: nc.vector.tensor_tensor(spans[:, 1:2], spans[:, 1:2], spans[:, 0:1], ALU.subtract),
            lambda: nc.vector.tensor_scalar_add(spans[:, 1:2], spans[:, 1:2], 1.0),
            lambda: nc.vector.scalar_tensor_tensor(spans[:, 0:1], spans[:, 1:2], float(NB), spans[:, 0:1],
                                                   ALU.mult, ALU.add),
            lambda: nc.vector.tensor_copy(spans_i[:, :], spans[:, :]),
            lambda: nc.vector.tensor_copy(Y[:, 0:NT], psE[:, 0:NT]),
            lambda: nc.vector.tensor_tensor(
                Y[:, NT:2 * NT].rearrange("p (c e) -> p c e", e=P)[:, :, 0:P - 1],
                Y[:, 0:NT].rearrange("p (c e) -> p c e", e=P)[:, :, 0:P - 1],
                Y[:, 0:NT].rearrange("p (c e) -> p c e", e=P)[:, :, 1:P], ALU.is_gt),
            lambda: nc.vector.tensor_reduce(
                small[:, 0:NT // P], Y[:, NT:2 * NT].rearrange("p (c e) -> p c e", e=P)[:, :, 0:P - 1],
                AX.X, ALU.max),
            lambda: nc.vector.tensor_reduce(small2[:, 0:1], small[:, 0:NT // P], AX.X, ALU.max),
        ])
        on_tensor([lambda: nc.tensor.transpose(psT[0:1, 0:P], small2[:, 0:1], ident[:, :])])
        on_vector([
            lambda: nc.vector.tensor_reduce(small2[0:1, 0:1], psT[0:1, 0:P], AX.X, ALU.max),
            lambda: nc.vector.tensor_copy(unsorted_i[:, :], small2[0:1, 0:1]),
        ])
        dma_block((range_scratch, spans_i[:, :]))
        dma_block((span_row[:, :], range_scratch.rearrange("h c -> (h c)").unsqueeze(0)))

        with nc.Block() as block:
            @block.gpsimd
            def _(pool):
                nc.gpsimd.iota(iota_i[:, 0:1], pattern=[[0, 1]], base=0, channel_multiplier=1)
        slot = small2[:, 0:1]
        on_vector([
            lambda: nc.vector.tensor_scalar(iota_i[:, 1:2], iota_i[:, 0:1], FE.bit_length() - 1, None,
                                            ALU.arith_shift_right),
            lambda: nc.vector.tensor_copy(slot, iota_i[:, 1:2]),
            lambda: nc.vector.tensor_scalar(wpart[:, 0:1], slot, 0.0, None, ALU.is_equal),
            lambda: nc.vector.tensor_scalar(wpart[:, 1:2], slot, 1.0, None, ALU.is_equal),
            lambda: nc.vector.tensor_scalar(wpart[:, 2:3], slot, 2.0, None, ALU.is_equal)] + [
            step for s_ in range(3, PARTS) for step in (
                lambda s_=s_: nc.vector.tensor_scalar(small2[:, 1:2], slot, float(s_), None, ALU.is_equal),
                lambda s_=s_: nc.vector.tensor_tensor(wpart[:, s_ % 3:s_ % 3 + 1], wpart[:, s_ % 3:s_ % 3 + 1],
                                                      small2[:, 1:2], ALU.add))])

        mid, lo3 = (hT[:, 0, 2 * P * n:2 * P * n + 2 * P] for n in range(2))
        parts_b = S[:, :, :].rearrange("p a b -> p (a b)").bitcast(BF16)

        def parts_of(hp):
            return [parts_b[:, 2 * P * (3 * (hp % 2) + n):2 * P * (3 * (hp % 2) + n + 1)] for n in range(3)]

        def of_octet(part, h, copies):
            return part[:, P * (h % 2):P * (h % 2) + P].rearrange("p (u f) -> p u f", u=U).unsqueeze(2).to_broadcast(
                [P, U, copies, FE])

        def stacked(h, s0, s1):
            return nats[h % 2].rearrange("p (u s f) -> p u s f", u=U, f=FE)[:, :, s0:s1, :]

        nats = [t[:, :, :].rearrange("p a b -> p (a b)").bitcast(BF16) for t in (tT, tT2)]
        turned_b = [psE[:, 1024 * q:1024 * q + 512].bitcast(BF16) for q in range(2)]
        stk_made, stk_turned, stk_copied = sem("stk_made"), sem("stk_turned"), sem("stk_copied")
        stk_out = [sem(f"stk_out{q}") for q in range(OB)]
        split_step, stk_high, first_table = sem("split_step"), sem("stk_high"), sem("first_table")
        on_vector([lambda: nc.vector.tensor_copy(ident_b[:, :], ident[:, :])])
        with nc.Block() as block:
            @block.gpsimd
            def _(pool):
                pool.wait_ge(x_in, 16)
                nc.gpsimd.tensor_tensor(whole(H), whole(H), over(vn[:, :]), ALU.add)
                pool.drain()
                nc.gpsimd.tensor_tensor(whole(Y), whole(H), over(be_row[:, :]), ALU.add)
                pool.drain()
                pool.dma_start(node_view, whole(Y)).then_inc(first_table, 16)
                pool.wait_ge(first_table, 16)

            @block.vector
            def _(dve):
                dve.wait_ge(features_in, 16)
                for hp in range(NO // 2):
                    ea = AGG[:, 2 * P * hp:2 * P * hp + 2 * P]
                    hb, mb, lb = parts_of(hp)
                    n = [0]

                    def then(ins):
                        n[0] += 1
                        ins.then_inc(split_step, 1)
                        dve.wait_ge(split_step, 5 * hp + n[0])

                    if hp >= 2:
                        dve.wait_ge(stk_high, 2 * (hp - 1))
                    then(nc.vector.tensor_copy(hb, ea))
                    then(nc.vector.tensor_tensor(mid, ea, hb, ALU.subtract))
                    then(nc.vector.tensor_copy(mb, mid))
                    then(nc.vector.tensor_tensor(lo3, mid, mb, ALU.subtract))
                    then(nc.vector.tensor_copy(lb, lo3))
                    for h in (2 * hp, 2 * hp + 1):
                        if h >= 2:
                            dve.wait_ge(stk_turned, h - 1)
                        for part, s0, s1 in ((mb, 3, 6), (lb, 6, PARTS)):
                            ins = nc.vector.tensor_copy(stacked(h, s0, s1), of_octet(part, h, s1 - s0))
                        ins.then_inc(stk_made, 1)

            @block.tensor
            def _(pe):
                for h in range(NO):
                    pe.wait_ge(stk_made, h + 1)
                    pe.wait_ge(stk_high, h + 1)
                    if h >= 2:
                        pe.wait_ge(stk_copied, h - 1)
                    for u in range(U):
                        ins = nc.tensor.transpose(turned_b[h % 2][:, P * u:P * u + P],
                                                  nats[h % 2][:, P * u:P * u + P], ident_b[:, :])
                    ins.then_inc(stk_turned, 1)

            @block.scalar
            def _(act):
                def high_part(h):
                    act.wait_ge(split_step, 5 * (h // 2) + 1)
                    if h >= 2:
                        act.wait_ge(stk_turned, h - 1)
                    nc.scalar.copy(stacked(h, 0, 3), of_octet(parts_of(h // 2)[0], h, 3)).then_inc(stk_high, 1)

                high_part(0)
                for h in range(NO):
                    if h < NO - 1:
                        high_part(h + 1)
                    act.wait_ge(stk_turned, h + 1)
                    if h >= OB:
                        act.wait_ge(stk_out[h % OB], 16 * (h // OB))
                    nc.scalar.copy(stk[:, h % OB, :], turned_b[h % 2]).then_inc(stk_copied, 1)

            @block.sync
            def _(sp):
                for h in range(NO):
                    sp.wait_ge(stk_copied, h + 1)
                    sp.dma_start(stack_table[P * h:P * h + P, :], stk[:, h % OB, :]).then_inc(stk_out[h % OB], 16)
                for q in range(OB):
                    sp.wait_ge(stk_out[q], 16 * (NO // OB))

        def load_we(sp, l):
            for g in range(PARTS):
                sp.dma_start(we_rep[FE * g:FE * g + FE, :], at(We, l)).then_inc(we_loaded, 16)
            sp.wait_ge(we_loaded, 16 * PARTS * (l + 1))
            sp.sem_inc(loads_seen, 1)

        def at(t, l):
            return t[bass.ds(l, 1)].squeeze(0) if not isinstance(l, int) else t[l]

        we_loaded = sem("we_loaded")
        with nc.Block() as block:
            @block.sync
            def _(sp):
                load_we(sp, 0)

        layer_loaded = sem("layer_loaded")
        virtual_loaded = sem("virtual_loaded")
        roots = sem("roots")
        we_split = sem("we_split")
        vn_pe, vn_dve = sem("vn_pe"), sem("vn_dve")
        vrows = Y[:, 0:6 * D].rearrange("p (r f) -> p r f", f=D)
        vtin = Y[:, 6 * D:7 * D]
        vtT = Y[:, 7 * D:8 * D]
        wsp = Y[:, 8 * D:12 * D]
        VPE, VDVE = 5, 4

        def layer(l, last_layer):
            copies = ([(w1_sb[:, :, :], at(W1, l).rearrange("(f p) n -> p f n", p=P)),
                       (w2_sb[:, :, :], at(W2, l).rearrange("(f p) n -> p f n", p=P)),
                       (rows[:, 0, :], row_bcast(at(bn_v, l))), (rows[:, 1, :], row_bcast(at(bn_g, l))),
                       (rows[:, 2, :], row_bcast(at(bn_m, l))), (rows[:, 3, :], row_bcast(at(bn_b, l))),
                       (rows[:, 4, :], row_bcast(at(b2, l)))] +
                      [(b1_col[:, j:j + 1], at(b1, l)[P * j:P * j + P].unsqueeze(1)) for j in range(4)])
            copies.append((be_row[:, :], row_bcast(at(be, l if last_layer else l + 1))))
            virtual = [] if last_layer else [
                (wa_sb[:, :, :], at(Wv1, l).rearrange("(f p) n -> p f n", p=P)),
                (wb_sb[:, :, :], at(Wv2, l).rearrange("(f p) n -> p f n", p=P)),
                (vrows[:, 0, :], row_bcast(at(vn_v, l))), (vrows[:, 1, :], row_bcast(at(vn_g, l))),
                (vrows[:, 2, :], row_bcast(at(vn_m, l))), (vrows[:, 3, :], row_bcast(at(vn_b, l))),
                (vrows[:, 4, :], row_bcast(at(bv1, l))), (vrows[:, 5, :], row_bcast(at(bv2, l)))]

            def loads(sp):
                for o, i in virtual:
                    sp.dma_start(o, i).then_inc(virtual_loaded, 16)
                for o, i in copies:
                    sp.dma_start(o, i).then_inc(layer_loaded, 16)

                def seen(sp):
                    sp.wait_ge(layer_loaded, 16 * len(copies) * (l + 1))
                    sp.sem_inc(loads_seen, 1)
                return seen

            def first_pe(pe):
                if not last_layer:
                    for b in range(NB):
                        ins = nc.tensor.matmul(psV[:, 0:D], ones[:, :], H[:, D * b:D * b + D],
                                               start=(b == 0), stop=(b == NB - 1))
                    ins.then_inc(vn_pe, 1)
                    for n, w in enumerate((wa_sb, wb_sb)):
                        pe.wait_ge(vn_dve, VDVE * l + 2 * n + 1)
                        for f in range(2):
                            ins = nc.tensor.transpose(psT[:, P * f:P * f + P], vtin[:, P * f:P * f + P], ident[:, :])
                        ins.then_inc(vn_pe, 1)
                        if n == 0:
                            pe.wait_ge(virtual_loaded, 16 * len(virtual) * (l + 1))
                        pe.wait_ge(vn_dve, VDVE * l + 2 * n + 2)
                        for f in range(2):
                            ins = nc.tensor.matmul(psO[:, 0:D], vtT[:, P * f:P * f + P], w[:, f, :],
                                                   start=(f == 0), stop=(f == 1))
                        ins.then_inc(vn_pe, 1)
                pe.wait_ge(we_split, l + 1)
                pe.sem_inc(parts_seen, 1)

            def first_act(act):
                act.wait_ge(layer_loaded, 16 * len(copies) * (l + 1))
                ins = nc.scalar.activation(rows[:, 0, :], rows[:, 0, :], ACT.Sqrt, bias=eps[:, 0:1])
                if not last_layer:
                    act.wait_ge(virtual_loaded, 16 * len(virtual) * (l + 1))
                    ins = nc.scalar.activation(vrows[:, 0, :], vrows[:, 0, :], ACT.Sqrt, bias=eps[:, 0:1])
                ins.then_inc(roots, 1)

            def first_dve(dve):
                def chain(*steps):
                    for step in steps:
                        ins = step()
                        dve.drain()

                a, b_, c = wsp[:, 0:D], wsp[:, D:2 * D], wsp[:, 2 * D:3 * D]
                ab, bb = wsp[:, 3 * D:3 * D + P].bitcast(BF16), wsp[:, 3 * D + P:4 * D].bitcast(BF16)
                chain(lambda: nc.vector.tensor_copy(ab, we_rep[:, :]),
                      lambda: nc.vector.tensor_tensor(b_, we_rep[:, :], ab, ALU.subtract),
                      lambda: nc.vector.tensor_copy(bb, b_),
                      lambda: nc.vector.tensor_tensor(c, b_, bb, ALU.subtract),
                      lambda: nc.vector.tensor_scalar(a, ab, wpart[:, 0:1], None, ALU.mult),
                      lambda: nc.vector.scalar_tensor_tensor(a, bb, wpart[:, 1:2], a, ALU.mult, ALU.add))
                nc.vector.scalar_tensor_tensor(we_stk[:, :], c, wpart[:, 2:3], a, ALU.mult, ALU.add
                                               ).then_inc(we_split, 1)
                dve.wait_ge(roots, l + 1)
                chain(lambda: nc.vector.reciprocal(rows[:, 0, :], rows[:, 0, :]),
                      lambda: nc.vector.tensor_tensor(scale_row[:, :], rows[:, 0, :], rows[:, 1, :], ALU.mult),
                      lambda: nc.vector.tensor_tensor(bias_row[:, :], rows[:, 4, :], rows[:, 2, :], ALU.subtract),
                      lambda: nc.vector.tensor_tensor(bias_row[:, :], bias_row[:, :], scale_row[:, :], ALU.mult),
                      lambda: nc.vector.tensor_tensor(bias_row[:, :], bias_row[:, :], rows[:, 3, :], ALU.add),
                      lambda: nc.vector.tensor_tensor(w2_sb[:, :, :], w2_sb[:, :, :], over(scale_row[:, :], 4),
                                                      ALU.mult))
                if last_layer:
                    return
                chain(lambda: nc.vector.reciprocal(vrows[:, 0, :], vrows[:, 0, :]),
                      lambda: nc.vector.tensor_tensor(scale_row[:, :], vrows[:, 0, :], vrows[:, 1, :], ALU.mult),
                      lambda: nc.vector.tensor_tensor(vrows[:, 2, :], vrows[:, 4, :], vrows[:, 2, :], ALU.subtract),
                      lambda: nc.vector.tensor_tensor(vrows[:, 2, :], vrows[:, 2, :], scale_row[:, :], ALU.mult),
                      lambda: nc.vector.tensor_tensor(vrows[:, 2, :], vrows[:, 2, :], vrows[:, 3, :], ALU.add))
                dve.wait_ge(vn_pe, VPE * l + 1)
                nc.vector.tensor_tensor(vtin, psV[:, 0:D], vn[:, :], ALU.add).then_inc(vn_dve, 1)
                dve.wait_ge(vn_pe, VPE * l + 2)
                nc.vector.tensor_scalar(vtT, psT[:, 0:D], 1.0, None, ALU.mult).then_inc(vn_dve, 1)
                dve.wait_ge(vn_pe, VPE * l + 3)
                chain(lambda: nc.vector.tensor_tensor(vtin, psO[:, 0:D], scale_row[:, :], ALU.mult),
                      lambda: nc.vector.tensor_tensor(vtin, vtin, vrows[:, 2, :], ALU.add))
                nc.vector.tensor_scalar(vtin, vtin, 0.0, None, ALU.max).then_inc(vn_dve, 1)
                dve.wait_ge(vn_pe, VPE * l + 4)
                nc.vector.tensor_scalar(vtT, psT[:, 0:D], 1.0, None, ALU.mult).then_inc(vn_dve, 1)
                dve.wait_ge(vn_pe, VPE * l + 5)
                chain(lambda: nc.vector.tensor_tensor(vn[:, :], psO[:, 0:D], vn[:, :], ALU.add),
                      lambda: nc.vector.tensor_tensor(vn[:, :], vn[:, :], vrows[:, 5, :], ALU.add))

            edge_pass(MESSAGE, l, l, loads, (first_pe, first_act, first_dve))

            def pre(dve, b, q):
                return nc.vector.tensor_tensor(tin[:, q, :], blk(H, b), blk(AGG, b, D, agg_pitch), ALU.add)

            def post(dve, b, q):
                h = blk(H, b)
                if last_layer:
                    a = blk(AGG, b, D, agg_pitch)
                    nc.vector.tensor_tensor(a, result_of(q), h, ALU.add)
                    dve.drain()
                    nc.vector.tensor_tensor(a, a, bias_row[:, :], ALU.add)
                    dve.wait_ge(residual_in, 16)
                    dve.drain()
                    nc.vector.tensor_tensor(a, a, blk(Y, b), ALU.add)
                    dve.drain()
                    return block_stats(b)
                nc.vector.tensor_tensor(tin2[:, q, :], result_of(q), bias_row[:, :], ALU.add)
                dve.drain()
                nc.vector.scalar_tensor_tensor(h, tin2[:, q, :], 0.0, h, ALU.max, ALU.add)
                dve.drain()
                return nc.vector.tensor_tensor(h, h, vn[:, :], ALU.add)

            def table_rows(pool, b, q):
                return nc.gpsimd.tensor_tensor(tab[:, q, 0:D], blk(H, b), be_row[:, :], ALU.add)

            def store(sp, b, q):
                return sp.dma_start(node_rows(b), tab[:, q, 0:D])

            if last_layer:
                node_phase(l, pre, post, hidden=True, loads=lambda sp: sp.dma_start(
                    whole(Y), x.rearrange("(b p) f -> p b f", p=P)).then_inc(residual_in, 16))
            else:
                node_phase(l, pre, post, hidden=True, store=store, st=l, pool_post=table_rows,
                           loads=lambda sp: load_we(sp, l + 1))

        def block_stats(b):
            return nc.vector.bn_stats(flat(stats[:, :, :])[:, bass.ds(b * 6, 6)] if not isinstance(b, int)
                                      else stats[:, b, :], blk(AGG, b, D, AW))

        agg_pitch = AW
        residual_in = sem("residual_in")

        def node_rows(b):
            return node_table[bass.ds(b * P, P), :] if not isinstance(b, int) else node_table[b * P:b * P + P, :]

        tin2 = sb("tin2", [P, 2, D])

        with nc.Fori(0, L - 1) as l:
            layer(l, False)
        layer(L - 1, True)

        root_ready, norm_ready, norm_done = sem("root_ready"), sem("norm_ready"), sem("norm_done")
        aggregated, norm_stored = sem("aggregated"), sem("norm_stored")
        shift = sb("shift", [P, NB])
        norms = [0]

        def layer_norm(store=None):
            n = norms[0]
            norms[0] += 1
            half = NB // 2
            with nc.Block() as block:
                @block.vector
                def _(dve):
                    for b in range(NB):
                        ins = nc.vector.bn_aggr(mv[:, b, :], stats[:, b, :])
                    dve.drain().then_inc(aggregated, 1)
                    dve.wait_ge(root_ready, n + 1)
                    nc.vector.reciprocal(rstd[:, :], rstd[:, :])
                    dve.drain()
                    nc.vector.scalar_tensor_tensor(shift[:, :], mv[:, :, 0:1].rearrange("p b o -> p (b o)"), -1.0,
                                                   rstd[:, :], ALU.mult, ALU.mult)
                    dve.drain().then_inc(norm_ready, 1)
                    for b in range(0, NB, 2):
                        nc.vector.tensor_scalar(H[:, D * b:D * b + D], AGG[:, AW * b:AW * b + D],
                                                mv[:, b, 0:1], rstd[:, b:b + 1], ALU.subtract, ALU.mult
                                                ).then_inc(norm_done, 1)

                @block.scalar
                def _(act):
                    act.wait_ge(aggregated, n + 1)
                    nc.scalar.activation(rstd[:, :], mv[:, :, 1:2].rearrange("p b o -> p (b o)"),
                                         ACT.Sqrt, bias=eps[:, 0:1]).then_inc(root_ready, 1)
                    act.wait_ge(norm_ready, n + 1)
                    for b in range(1, NB, 2):
                        nc.scalar.activation(H[:, D * b:D * b + D], AGG[:, AW * b:AW * b + D], ACT.Identity,
                                             bias=shift[:, b:b + 1], scale=rstd[:, b:b + 1]
                                             ).then_inc(norm_done_act, 1)

                @block.sync
                def _(sp):
                    if store:
                        for c in range(4):
                            sp.wait_ge(norm_done, half * n + half // 4 * (c + 1))
                            sp.wait_ge(norm_done_act, half * n + half // 4 * (c + 1))
                            b = NB // 4 * c
                            sp.dma_start(store[:, b:b + NB // 4, :], whole(H)[:, b:b + NB // 4, :]
                                         ).then_inc(norm_stored, 16)
                        norms_stored[0] += 4 * 16
                        sp.wait_ge(norm_stored, norms_stored[0])

        norm_done_act = sem("norm_done_act")
        norms_stored = [0]

        def on_both(*steps, stats_too=False):
            cut = 21
            with nc.Block() as block:
                @block.vector
                def _(dve):
                    for step in steps:
                        step(nc.vector, 0, cut)
                        dve.drain()
                    if stats_too:
                        for b in range(cut):
                            block_stats(b)
                        dve.wait_ge(pool_rows, both_count[0] + 1)
                        for b in range(cut, NB):
                            block_stats(b)

                @block.gpsimd
                def _(pool):
                    for step in steps:
                        step(nc.gpsimd, cut, NB)
                        pool.drain()
                    pool.sem_inc(pool_rows, 1)
            both_count[0] += 1

        pool_rows = sem("pool_rows")
        both_count = [0]

        layer_norm(node_view)

        def col_w(w):
            return w.rearrange("(f p) n -> p f n", p=P)

        def second_loads(sp):
            copy_in(sp, block_copied, block_count, (w1_sb[:, :, 0:D], col_w(W_rel)),
                    (w1_sb[:, :, D:2 * D], col_w(W_root)),
                    (bias_row[:, :], row_bcast(b_rel)), (rows[:, 0, :], row_bcast(gamma)),
                    (rows[:, 1, :], row_bcast(beta)))

        edge_pass(WEIGHTED, L, 0, second_loads)
        on_tensor([(lambda s=s, f=f, g=g: nc.tensor.transpose(
            psE[:, 1024 * s + 512 * f + P * g:1024 * s + 512 * f + P * g + P],
            w1_sb[:, g, D * s + P * f:D * s + P * f + P], ident[:, :]))
            for s in range(2) for f in range(2) for g in range(2)])
        on_vector([(lambda s=s, f=f: nc.vector.tensor_copy((wa_sb, wb_sb)[s][:, f, :],
                                                           psE[:, 1024 * s + 512 * f:1024 * s + 512 * f + D]))
                   for s in range(2) for f in range(2)])

        def pre_second(dve, b, q):
            copied(tin2[:, q, :], blk(H, b))
            dve.drain()
            return copied(tin[:, q, :], blk(AGG, b, D, AW))

        def to_agg(dve, b, q):
            return nc.vector.tensor_tensor(blk(AGG, b, D, AW), result_of(q), bias_row[:, :], ALU.add)

        def column_sums(t, pitch):
            cut = 21
            count = column_parts[0] = column_parts[0] + 1
            with nc.Block() as block:
                @block.vector
                def _(dve):
                    nc.vector.tensor_reduce(tin2[:, 0, :], whole(t, D, pitch)[:, 0:cut, :].rearrange("p b f -> p f b"),
                                            AX.X, ALU.add).then_inc(part_summed, 1)

                @block.tensor
                def _(pe):
                    for b in range(cut, NB):
                        nc.tensor.matmul(psV[:, 0:D], ones[:, :], t[:, pitch * b:pitch * b + D],
                                         start=(b == cut), stop=False)
                    pe.wait_ge(part_summed, count)
                    nc.tensor.matmul(psV[:, 0:D], ones[:, :], tin2[:, 0, :], start=False, stop=True)

        part_summed = sem("part_summed")
        column_parts = [0]
        node_phase(L, pre_second, to_agg, second=True)
        column_sums(AGG, AW)
        def rows_of(t, b0, b1, pitch=D):
            return whole(t, D, pitch)[:, b0:b1, :]

        def sums(b0, b1):
            return rows_of(AGG, b0, b1, AW)

        on_vector([lambda: nc.vector.tensor_scalar(scale_row[:, :], psV[:, 0:D], 1.0 / N, None, ALU.mult)])
        on_both(lambda e, b0, b1: e.tensor_tensor(sums(b0, b1), sums(b0, b1), over(scale_row[:, :], b1 - b0),
                                                  ALU.subtract),
                lambda e, b0, b1: e.tensor_tensor(rows_of(Y, b0, b1), sums(b0, b1), sums(b0, b1), ALU.mult))
        column_sums(Y, D)
        on_scalar([lambda: nc.scalar.activation(scale_row[:, :], psV[:, 0:D], ACT.Sqrt, bias=eps[:, 0:1],
                                                scale=1.0 / N)])
        on_vector([lambda: nc.vector.reciprocal(scale_row[:, :], scale_row[:, :]),
                   lambda: nc.vector.tensor_tensor(scale_row[:, :], scale_row[:, :], rows[:, 0, :], ALU.mult)])
        def relu(e, b0, b1):
            return e.tensor_scalar(sums(b0, b1), sums(b0, b1), 0.0, None, ALU.max)

        def add_h(e, b0, b1):
            return e.tensor_tensor(sums(b0, b1), sums(b0, b1), rows_of(H, b0, b1), ALU.add)

        def relu_add(e, b0, b1):
            if e is nc.vector:
                return e.scalar_tensor_tensor(sums(b0, b1), sums(b0, b1), 0.0, rows_of(H, b0, b1), ALU.max, ALU.add)
            relu(e, b0, b1)
            e.drain()
            return add_h(e, b0, b1)

        on_both(lambda e, b0, b1: e.tensor_tensor(sums(b0, b1), sums(b0, b1), over(scale_row[:, :], b1 - b0),
                                                  ALU.mult),
                lambda e, b0, b1: e.tensor_tensor(sums(b0, b1), sums(b0, b1), over(rows[:, 1, :], b1 - b0), ALU.add),
                relu_add, relu_add, stats_too=True)
        layer_norm()

        dma_block((wa_sb[:, :, :], col_w(gat_W)), (rows[:, 0, :], row_bcast(att_src.rearrange("h c -> (h c)"))),
                  (rows[:, 1, :], row_bcast(att_dst.rearrange("h c -> (h c)"))), (rows[:, 2, :], row_bcast(gat_bias)))

        def pre_h(dve, b, q):
            return copied(tin[:, q, :], blk(H, b))

        def post_att(dve, b, q):
            y = blk(Y, b)
            copied(y, result_of(q))
            dve.drain()
            nc.vector.tensor_tensor(tin2[:, :, :], y.unsqueeze(1).to_broadcast([P, 2, D]), rows[:, 0:2, :], ALU.mult)
            dve.drain()
            for r, scores in ((0, a_src), (1, a_dst)):
                s = flat(scores[:, :, :])
                ins = nc.vector.tensor_reduce(s[:, bass.ds(b * HEADS, HEADS)] if not isinstance(b, int) else
                                        s[:, b * HEADS:b * HEADS + HEADS],
                                        tin2[:, r, :].rearrange("p (h c) -> p h c", h=HEADS), AX.X, ALU.add)
            return ins

        def table_att(pool, b, q):
            nc.gpsimd.tensor_copy(tab[:, q, D:GW], blk(flat(a_src[:, :, :]), b, HEADS, HEADS))
            pool.drain()
            return nc.gpsimd.tensor_copy(tab[:, q, 0:D], blk(Y, b))

        def store_att(sp, b, q):
            t = att_table[bass.ds(b * P, P), :] if not isinstance(b, int) else att_table[b * P:b * P + P, :]
            return sp.dma_start(t, tab[:, q, :])

        node_phase(L + 1, pre_h, post_att, store=store_att, st=L - 1, pool_post=table_att)
        dma_block((score_table.rearrange("(b p) h -> p b h", p=P), a_src[:, :, :]))
        max_pass(L + 1)
        aS, aD, aM, eS = (flat(t[:, :, :]) for t in (a_src, a_dst, a_max, ex_self))
        both = stk_f[:, 8 * P:8 * P + NB * 2 * HEADS].rearrange("p (b h) -> p b h", b=NB)
        W2 = 2 * HEADS
        on_vector([
            lambda: nc.vector.tensor_tensor(aM, aM, aD, ALU.add),
            lambda: nc.vector.scalar_tensor_tensor(aM, aM, 0.2, aM, ALU.mult, ALU.max),
            lambda: nc.vector.tensor_copy(both[:, :, 0:HEADS], a_dst[:, :, :]),
            lambda: nc.vector.tensor_copy(both[:, :, HEADS:2 * HEADS], a_max[:, :, :]),
            lambda: nc.vector.tensor_copy(tgt[:, :, 0:W2], both),
            lambda: nc.vector.tensor_tensor(both, both, tgt[:, :, 0:W2], ALU.subtract),
            lambda: nc.vector.tensor_copy(tgt[:, :, W2:2 * W2], both),
            lambda: nc.vector.tensor_tensor(both, both, tgt[:, :, W2:2 * W2], ALU.subtract),
            lambda: nc.vector.tensor_copy(tgt[:, :, 2 * W2:3 * W2], both),
            lambda: nc.vector.tensor_tensor(eS, aS, aD, ALU.add),
            lambda: nc.vector.scalar_tensor_tensor(eS, eS, 0.2, eS, ALU.mult, ALU.max),
            lambda: nc.vector.tensor_tensor(eS, eS, aM, ALU.subtract),
        ])
        on_scalar([lambda: nc.scalar.activation(eS, eS, ACT.Exp)])
        conv_bias = [rows[:, r, :] for r in (3, 4, 0)]
        attend_pass(L + 2, lambda sp: copy_in(
            sp, block_copied, block_count, (wa_sb[:, :, :], col_w(gW1)), (wb_sb[:, :, :], col_w(gW2)),
            *((r, row_bcast(g)) for r, g in zip(conv_bias, (gb1, gb2, gb3)))))
        den = AGG[:, 0:NB * AW].rearrange("p (b f) -> p b f", f=AW)[:, :, D:GW]
        count = AGG[:, 0:NB * AW].rearrange("p (b f) -> p b f", f=AW)[:, :, AW - 1:AW]
        y4 = Y[:, :].rearrange("p (k c) -> p k c", c=C)
        def own_rows(e, b0, b1):
            y = y4[:, b0 * HEADS:b1 * HEADS, :]
            return e.tensor_tensor(y, y, eS[:, b0 * HEADS:b1 * HEADS].unsqueeze(2).to_broadcast(
                [P, (b1 - b0) * HEADS, C]), ALU.mult)

        def add_y(e, b0, b1):
            return e.tensor_tensor(rows_of(Y, b0, b1), rows_of(Y, b0, b1), sums(b0, b1), ALU.add)

        on_both(own_rows, add_y)
        on_vector([
            lambda: nc.vector.tensor_tensor(ex_self[:, :, :], ex_self[:, :, :], den, ALU.add),
            lambda: nc.vector.tensor_scalar_add(eS, eS, 1e-16),
            lambda: nc.vector.reciprocal(eS, eS),
            lambda: nc.vector.tensor_scalar_add(dinv[:, :], count.rearrange("p b o -> p (b o)"), 1.0),
        ])
        on_both(own_rows,
                lambda e, b0, b1: e.tensor_tensor(sums(b0, b1), rows_of(Y, b0, b1), over(rows[:, 2, :], b1 - b0),
                                                  ALU.add),
                add_h, stats_too=True)
        on_scalar([lambda: nc.scalar.activation(dinv[:, :], dinv[:, :], ACT.Sqrt)])
        on_vector([lambda: nc.vector.reciprocal(dinv[:, :], dinv[:, :])])
        layer_norm()

        def dv(b):
            return dinv[:, bass.ds(b, 1)] if not isinstance(b, int) else dinv[:, b:b + 1]

        def pre_conv(n):
            def pre(dve, b, q):
                nc.vector.tensor_tensor(tin2[:, q, :], blk(AGG, b, D, AW), blk(Y, b), ALU.add)
                dve.drain()
                nc.vector.scalar_tensor_tensor(tin2[:, q, :], tin2[:, q, :], dv(b), conv_bias[n - 1],
                                               ALU.mult, ALU.add)
                dve.drain()
                return nc.vector.tensor_scalar(tin[:, q, :], tin2[:, q, :], 0.0, None, ALU.max)
            return pre

        def post_conv(dve, b, q):
            return nc.vector.tensor_scalar(blk(Y, b), result_of(q), dv(b), None, ALU.mult)

        def table_conv(pool, b, q):
            return nc.gpsimd.tensor_copy(tab[:, q, 0:D], blk(Y, b))

        def store_conv(sp, b, q):
            return sp.dma_start(node_rows(b), tab[:, q, 0:D])

        def third_weights(sp):
            copy_in(sp, block_copied, block_count, (wa_sb[:, :, :], col_w(gW3)))

        def add_bias(dve):
            nc.vector.tensor_tensor(whole(H), whole(H), over(conv_bias[2]), ALU.add)

        for n in range(3):
            node_phase(L + 2 + n, pre_conv(n) if n else pre_h, post_conv, store=store_conv, st=L + n,
                       pool_post=table_conv, weights=(wa_sb, wb_sb, wa_sb)[n])
            edge_pass(PLAIN, L + 3 + n, first_dve=add_bias if n == 2 else None,
                      loads=third_weights if n == 0 else None)
        on_both(lambda e, b0, b1: e.tensor_tensor(sums(b0, b1), sums(b0, b1), rows_of(Y, b0, b1), ALU.add),
                lambda e, b0, b1: e.tensor_tensor(sums(b0, b1), sums(b0, b1),
                                                  dinv[:, b0:b1].unsqueeze(2).to_broadcast([P, b1 - b0, D]),
                                                  ALU.mult),
                add_h, stats_too=True)
        layer_norm(out.rearrange("(b p) f -> p b f", p=P))


_INS = ["x", "src", "dst", "edge_attr_16", "edge_weight", "L0_gnn_vn_emb0", "L0_gnn_We", "L0_gnn_be", "L0_gnn_W1",
        "L0_gnn_b1", "L0_gnn_W2", "L0_gnn_b2", "L0_gnn_bn_g", "L0_gnn_bn_b", "L0_gnn_bn_m", "L0_gnn_bn_v",
        "L0_gnn_Wv1", "L0_gnn_bv1", "L0_gnn_vn_g", "L0_gnn_vn_b", "L0_gnn_vn_m", "L0_gnn_vn_v", "L0_gnn_Wv2",
        "L0_gnn_bv2", "L1_gnn_W_rel", "L1_gnn_b_rel", "L1_gnn_W_root", "L1_gnn_gamma", "L1_gnn_beta", "L2_gnn_W",
        "L2_gnn_att_src", "L2_gnn_att_dst", "L2_gnn_bias", "L3_gnn_W1", "L3_gnn_b1", "L3_gnn_W2", "L3_gnn_b2",
        "L3_gnn_W3", "L3_gnn_b3"]


def kernel(**inputs):
    import concourse.bacc as bacc
    from concourse.bass_utils import run_bass_kernel_spmd

    nc = bacc.Bacc("TRN2", target_bir_lowering=False, num_devices=1)
    arrays, args = {}, []
    for name in _INS:
        a = np.ascontiguousarray(inputs[name])
        arrays[f"in_{name}"] = a
        args.append(nc.dram_tensor(f"in_{name}", a.shape, mybir.dt.from_np(a.dtype), kind="ExternalInput").ap())
    args.append(nc.dram_tensor("out_dram", [N, D], F32, kind="ExternalOutput").ap())
    build(nc, *args)
    r = run_bass_kernel_spmd(nc, [arrays], core_ids=[0])
    return r.results[0]["out_dram"]
```
